# Optimizing a Trainium2 kernel written in Bass

```python
import numpy as np
import jax
import jax.numpy as jnp

def _softmax(x, axis=-1):
    return jax.nn.softmax(x, axis=axis)

def _gelu(x):
    return jax.nn.gelu(x, approximate=True)

def _silu(x):
    return jax.nn.silu(x)

def _sigmoid(x):
    return jax.nn.sigmoid(x)

def _layernorm(x, axis=-1, eps=1e-05):
    m = jnp.mean(x, axis=axis, keepdims=True)
    v = jnp.var(x, axis=axis, keepdims=True)
    return (x - m) / jnp.sqrt(v + eps)

def _scatter_add(tgt, idx, src, axis=0):
    return tgt.at[idx].add(src)

def _segment_sum(src, seg, n):
    return jax.ops.segment_sum(src, seg, n)
kernel_name = 'mk_gps_d2_gnn_r8_f8d8bc'

def setup_inputs(seed: int=0):
    np.random.seed(seed)
    _w = jnp.asarray

    def _rec_inputs():
        import jax
        import jax.numpy as jnp
        _gk = jax.random.key(seed)
        x = -0.0003713 + 1 * jax.random.normal(jax.random.fold_in(_gk, 1), (6250, 256), jnp.float32)
        src = jax.random.randint(jax.random.fold_in(_gk, 2), (100000,), 0, 6250, jnp.int32)
        dst = jnp.minimum((6250 * jax.random.uniform(jax.random.fold_in(_gk, 3), (100000,)) ** 2.0).astype(jnp.int32), 49999)
        _o = jnp.argsort(dst, stable=True)
        src = src[_o]
        dst = dst[_o]
        edge_type_4 = jax.random.randint(jax.random.fold_in(_gk, 13), (100000,), 0, 4, jnp.int32)
        edge_type_8 = jax.random.randint(jax.random.fold_in(_gk, 14), (100000,), 0, 8, jnp.int32)
        return (x, src, dst, edge_type_4, edge_type_8)
    x, src, dst, edge_type_4, edge_type_8 = _rec_inputs()

    def _L0_gnn_setup():
        import jax, jax.numpy as jnp
        import numpy as np
        N_NODES = 6250
        N_EDGES = 100000
        DIM = 256
        DEPTH = 4
        N_REL = 4
        EPS = 1e-05

        def _rgcn_layer(X, W, root, bias, gamma, beta, src, dst, etype, inv_deg):
            h = jnp.einsum('ni,rio->rno', X, W)
            msg = h[etype, src] * inv_deg[:, None]
            agg = jax.ops.segment_sum(msg, dst, num_segments=X.shape[0])
            out = agg + X @ root + bias
            mu = jnp.mean(out, axis=-1, keepdims=True)
            var = jnp.mean(jnp.square(out - mu), axis=-1, keepdims=True)
            out = (out - mu) * jax.lax.rsqrt(var + EPS) * gamma + beta
            out = jax.nn.elu(out)
            return out + X
        key = jax.random.key(seed)
        ks = jax.random.split(key, 8)
        scale = 1.0 / np.sqrt(DIM)
        return {'node_embedding': jax.random.normal(ks[0], (N_NODES, DIM), jnp.float32), 'weights': jax.random.normal(ks[1], (DEPTH, N_REL, DIM, DIM), jnp.float32) * scale, 'roots': jax.random.normal(ks[2], (DEPTH, DIM, DIM), jnp.float32) * scale, 'biases': jax.random.normal(ks[3], (DEPTH, DIM), jnp.float32) * 0.01, 'ln_gamma': jnp.ones((DEPTH, DIM), jnp.float32), 'ln_beta': jnp.zeros((DEPTH, DIM), jnp.float32), 'edge_index': jax.random.randint(ks[4], (2, N_EDGES), 0, N_NODES, jnp.int32), 'edge_type': jax.random.randint(ks[5], (N_EDGES,), 0, N_REL, jnp.int32)}
    _L0_gnn_all = _L0_gnn_setup()
    _L0_gnn_in = {k: v for k, v in _L0_gnn_all.items() if k in ('weights', 'roots', 'biases', 'ln_gamma', 'ln_beta')}
    del _L0_gnn_all

    def _L0_mix_setup():
        import jax, jax.numpy as jnp
        import numpy as np
        N, F, C, H = (32, 512, 256, 8)
        D = C // H
        EPS_ATTN = 1e-06
        EPS_LN = 1e-05

        def layer_norm(x, g, b):
            mu = jnp.mean(x, axis=-1, keepdims=True)
            var = jnp.var(x, axis=-1, keepdims=True)
            return (x - mu) * jax.lax.rsqrt(var + EPS_LN) * g + b
        key = jax.random.key(seed)
        ks = jax.random.split(key, 8)
        s = 1.0 / np.sqrt(C)
        return {'x': jax.random.normal(ks[0], (N, F, C), jnp.float32), 'Wqkv': jax.random.uniform(ks[1], (3 * C, C), jnp.float32, -s, s), 'ln1_g': jnp.ones((C,), jnp.float32), 'ln1_b': jnp.zeros((C,), jnp.float32), 'W1': jax.random.uniform(ks[2], (C, C), jnp.float32, -s, s), 'b1': jax.random.uniform(ks[3], (C,), jnp.float32, -s, s), 'W2': jax.random.uniform(ks[4], (C, C), jnp.float32, -s, s), 'b2': jax.random.uniform(ks[5], (C,), jnp.float32, -s, s), 'ln2_g': jnp.ones((C,), jnp.float32), 'ln2_b': jnp.zeros((C,), jnp.float32)}
    _L0_mix_all = _L0_mix_setup()
    _L0_mix_in = {k: v for k, v in _L0_mix_all.items() if k in ('Wqkv', 'ln1_g', 'ln1_b', 'W1', 'b1', 'W2', 'b2', 'ln2_g', 'ln2_b')}
    del _L0_mix_all

    def _L0_ffn_setup():
        import jax, jax.numpy as jnp
        import numpy as np
        B, S, D = (8, 512, 256)
        H = 4 * D
        CAPACITY = 0.5
        key = jax.random.key(seed)
        ks = jax.random.split(key, 6)
        x = jax.random.normal(ks[0], (B, S, D), dtype=jnp.float32)
        attention_mask = jnp.zeros((B, 1, 1, S), dtype=jnp.float32)
        wr = jax.random.normal(ks[1], (D, 1), dtype=jnp.float32) * 0.02
        br = jnp.zeros((1,), dtype=jnp.float32)
        w1 = jax.random.normal(ks[2], (D, H), dtype=jnp.float32) * 0.02
        b1 = jnp.zeros((H,), dtype=jnp.float32)
        w2 = jax.random.normal(ks[3], (H, D), dtype=jnp.float32) * 0.02
        b2 = jnp.zeros((D,), dtype=jnp.float32)
        return {'x': x, 'attention_mask': attention_mask, 'wr': wr, 'br': br, 'w1': w1, 'b1': b1, 'w2': w2, 'b2': b2}
    _L0_ffn_all = _L0_ffn_setup()
    _L0_ffn_in = {k: v for k, v in _L0_ffn_all.items() if k in ('attention_mask', 'wr', 'br', 'w1', 'b1', 'w2', 'b2')}
    del _L0_ffn_all

    def _L1_gnn_setup():
        import jax, jax.numpy as jnp
        import numpy as np
        N_NODES = 2500
        N_EDGES = 40000
        NUM_RELS = 8
        DIM = 256
        BN_EPS = 1e-05
        key = jax.random.key(seed)
        k1, k2, k3, k4, k5 = jax.random.split(key, 5)
        h = jax.random.normal(k1, (N_NODES, DIM), dtype=jnp.float32)
        weight = jax.random.normal(k2, (NUM_RELS, DIM, DIM), dtype=jnp.float32) * 0.05
        gamma = jnp.ones((DIM,), dtype=jnp.float32)
        beta = jnp.zeros((DIM,), dtype=jnp.float32)
        src = jax.random.randint(k3, (N_EDGES,), 0, N_NODES, dtype=jnp.int32)
        dst = jax.random.randint(k4, (N_EDGES,), 0, N_NODES, dtype=jnp.int32)
        rel = jax.random.randint(k5, (N_EDGES,), 0, NUM_RELS, dtype=jnp.int32)
        return {'h': h, 'weight': weight, 'gamma': gamma, 'beta': beta, 'src': src, 'dst': dst, 'rel': rel}
    _L1_gnn_all = _L1_gnn_setup()
    _L1_gnn_in = {k: v for k, v in _L1_gnn_all.items() if k in ('weight', 'gamma', 'beta')}
    del _L1_gnn_all

    def _L1_mix_setup():
        import jax, jax.numpy as jnp
        import numpy as np
        import math
        EMBED = 256
        HEADS = 4
        HEAD_DIM = EMBED // HEADS
        OUT_DIM = 256
        LN_EPS = 1e-05

        def _qkv_init(key):
            spread = math.sqrt(3.0 / EMBED)
            gain, delta = (0.01, 0.01)
            w = jax.random.uniform(key, (EMBED, EMBED), minval=-spread, maxval=spread) * gain
            return w + delta * jnp.eye(EMBED, dtype=w.dtype)

        def _layer_norm(x, g, b):
            mu = jnp.mean(x, axis=-1, keepdims=True)
            var = jnp.mean(jnp.square(x - mu), axis=-1, keepdims=True)
            return (x - mu) * jax.lax.rsqrt(var + LN_EPS) * g + b

        def _split_heads(x, B, S):
            return x.reshape(B, S, HEADS, HEAD_DIM).transpose(0, 2, 1, 3)
        key = jax.random.key(seed)
        ks = jax.random.split(key, 6)
        seq = jax.random.normal(ks[0], (4, 1024, EMBED), dtype=jnp.float32)
        wq = _qkv_init(ks[1])
        wk = _qkv_init(ks[2])
        wv = _qkv_init(ks[3])
        bound = 1.0 / math.sqrt(EMBED)
        wo = jax.random.uniform(ks[4], (OUT_DIM, EMBED), minval=-bound, maxval=bound)
        bo = jax.random.uniform(ks[5], (OUT_DIM,), minval=-bound, maxval=bound)
        ln_k_g = jnp.ones((HEAD_DIM,), jnp.float32)
        ln_k_b = jnp.zeros((HEAD_DIM,), jnp.float32)
        ln_v_g = jnp.ones((HEAD_DIM,), jnp.float32)
        ln_v_b = jnp.zeros((HEAD_DIM,), jnp.float32)
        return {'seq': seq, 'wq': wq, 'wk': wk, 'wv': wv, 'wo': wo, 'bo': bo, 'ln_k_g': ln_k_g, 'ln_k_b': ln_k_b, 'ln_v_g': ln_v_g, 'ln_v_b': ln_v_b}
    _L1_mix_all = _L1_mix_setup()
    _L1_mix_in = {k: v for k, v in _L1_mix_all.items() if k in ('wq', 'wk', 'wv', 'wo', 'bo', 'ln_k_g', 'ln_k_b', 'ln_v_g', 'ln_v_b')}
    del _L1_mix_all

    def _L1_ffn_setup():
        import math
        import jax, jax.numpy as jnp
        import numpy as np
        CAPACITY_FACTOR = 1.25
        TOP_K = 2
        LN_EPS = 1e-05

        def _layer_norm(x, gamma, beta):
            mu = jnp.mean(x, axis=-1, keepdims=True)
            var = jnp.var(x, axis=-1, keepdims=True)
            return (x - mu) * jax.lax.rsqrt(var + LN_EPS) * gamma + beta
        key = jax.random.key(seed)
        ks = jax.random.split(key, 4)
        B, S, D, F, E = (8, 512, 256, 512, 8)
        x = jax.random.normal(ks[0], (B, S, D), dtype=jnp.float32)
        Wr = jax.random.normal(ks[1], (D, E), dtype=jnp.float32) / np.sqrt(D)
        br = jnp.zeros((E,), jnp.float32)
        W1 = jax.random.normal(ks[2], (E, D, F), dtype=jnp.float32) / np.sqrt(D)
        b1 = jnp.zeros((E, F), jnp.float32)
        W2 = jax.random.normal(ks[3], (E, F, D), dtype=jnp.float32) / np.sqrt(F)
        b2 = jnp.zeros((E, D), jnp.float32)
        gamma = jnp.ones((D,), jnp.float32)
        beta = jnp.zeros((D,), jnp.float32)
        return {'x': x, 'Wr': Wr, 'br': br, 'W1': W1, 'b1': b1, 'W2': W2, 'b2': b2, 'gamma': gamma, 'beta': beta}
    _L1_ffn_all = _L1_ffn_setup()
    _L1_ffn_in = {k: v for k, v in _L1_ffn_all.items() if k in ('Wr', 'br', 'W1', 'b1', 'W2', 'b2', 'gamma', 'beta')}
    del _L1_ffn_all
    return {'x': x, 'src': src, 'dst': dst, 'edge_type_4': edge_type_4, 'edge_type_8': edge_type_8, 'L0_gnn_weights': _L0_gnn_in['weights'], 'L0_gnn_roots': _L0_gnn_in['roots'], 'L0_gnn_biases': _L0_gnn_in['biases'], 'L0_gnn_ln_gamma': _L0_gnn_in['ln_gamma'], 'L0_gnn_ln_beta': _L0_gnn_in['ln_beta'], 'L0_mix_Wqkv': _L0_mix_in['Wqkv'], 'L0_mix_ln1_g': _L0_mix_in['ln1_g'], 'L0_mix_ln1_b': _L0_mix_in['ln1_b'], 'L0_mix_W1': _L0_mix_in['W1'], 'L0_mix_b1': _L0_mix_in['b1'], 'L0_mix_W2': _L0_mix_in['W2'], 'L0_mix_b2': _L0_mix_in['b2'], 'L0_mix_ln2_g': _L0_mix_in['ln2_g'], 'L0_mix_ln2_b': _L0_mix_in['ln2_b'], 'L0_ffn_attention_mask': _L0_ffn_in['attention_mask'], 'L0_ffn_wr': _L0_ffn_in['wr'], 'L0_ffn_br': _L0_ffn_in['br'], 'L0_ffn_w1': _L0_ffn_in['w1'], 'L0_ffn_b1': _L0_ffn_in['b1'], 'L0_ffn_w2': _L0_ffn_in['w2'], 'L0_ffn_b2': _L0_ffn_in['b2'], 'L1_gnn_weight': _L1_gnn_in['weight'], 'L1_gnn_gamma': _L1_gnn_in['gamma'], 'L1_gnn_beta': _L1_gnn_in['beta'], 'L1_mix_wq': _L1_mix_in['wq'], 'L1_mix_wk': _L1_mix_in['wk'], 'L1_mix_wv': _L1_mix_in['wv'], 'L1_mix_wo': _L1_mix_in['wo'], 'L1_mix_bo': _L1_mix_in['bo'], 'L1_mix_ln_k_g': _L1_mix_in['ln_k_g'], 'L1_mix_ln_k_b': _L1_mix_in['ln_k_b'], 'L1_mix_ln_v_g': _L1_mix_in['ln_v_g'], 'L1_mix_ln_v_b': _L1_mix_in['ln_v_b'], 'L1_ffn_Wr': _L1_ffn_in['Wr'], 'L1_ffn_br': _L1_ffn_in['br'], 'L1_ffn_W1': _L1_ffn_in['W1'], 'L1_ffn_b1': _L1_ffn_in['b1'], 'L1_ffn_W2': _L1_ffn_in['W2'], 'L1_ffn_b2': _L1_ffn_in['b2'], 'L1_ffn_gamma': _L1_ffn_in['gamma'], 'L1_ffn_beta': _L1_ffn_in['beta']}

def reference(x, src, dst, edge_type_4, edge_type_8, L0_gnn_weights, L0_gnn_roots, L0_gnn_biases, L0_gnn_ln_gamma, L0_gnn_ln_beta, L0_mix_Wqkv, L0_mix_ln1_g, L0_mix_ln1_b, L0_mix_W1, L0_mix_b1, L0_mix_W2, L0_mix_b2, L0_mix_ln2_g, L0_mix_ln2_b, L0_ffn_attention_mask, L0_ffn_wr, L0_ffn_br, L0_ffn_w1, L0_ffn_b1, L0_ffn_w2, L0_ffn_b2, L1_gnn_weight, L1_gnn_gamma, L1_gnn_beta, L1_mix_wq, L1_mix_wk, L1_mix_wv, L1_mix_wo, L1_mix_bo, L1_mix_ln_k_g, L1_mix_ln_k_b, L1_mix_ln_v_g, L1_mix_ln_v_b, L1_ffn_Wr, L1_ffn_br, L1_ffn_W1, L1_ffn_b1, L1_ffn_W2, L1_ffn_b2, L1_ffn_gamma, L1_ffn_beta):
    import jax
    import jax.numpy as jnp

    def _L0_gnn_ref(node_embedding, weights, roots, biases, ln_gamma, ln_beta, edge_index, edge_type):
        import jax, jax.numpy as jnp
        import numpy as np
        N_NODES = 6250
        N_EDGES = 100000
        DIM = 256
        DEPTH = 4
        N_REL = 4
        EPS = 1e-05

        def _rgcn_layer(X, W, root, bias, gamma, beta, src, dst, etype, inv_deg):
            h = jnp.einsum('ni,rio->rno', X, W)
            msg = h[etype, src] * inv_deg[:, None]
            agg = jax.ops.segment_sum(msg, dst, num_segments=X.shape[0])
            out = agg + X @ root + bias
            mu = jnp.mean(out, axis=-1, keepdims=True)
            var = jnp.mean(jnp.square(out - mu), axis=-1, keepdims=True)
            out = (out - mu) * jax.lax.rsqrt(var + EPS) * gamma + beta
            out = jax.nn.elu(out)
            return out + X
        src, dst = (edge_index[0], edge_index[1])
        cnt = jnp.zeros((node_embedding.shape[0], N_REL), node_embedding.dtype)
        cnt = cnt.at[dst, edge_type].add(1.0)
        inv_deg = 1.0 / jnp.maximum(cnt[dst, edge_type], 1.0)
        X = node_embedding
        for l in range(DEPTH):
            X = _rgcn_layer(X, weights[l], roots[l], biases[l], ln_gamma[l], ln_beta[l], src, dst, edge_type, inv_deg)
        return X

    def _L0_mix_ref(x, Wqkv, ln1_g, ln1_b, W1, b1, W2, b2, ln2_g, ln2_b):
        import jax, jax.numpy as jnp
        import numpy as np
        N, F, C, H = (32, 512, 256, 8)
        D = C // H
        EPS_ATTN = 1e-06
        EPS_LN = 1e-05

        def layer_norm(x, g, b):
            mu = jnp.mean(x, axis=-1, keepdims=True)
            var = jnp.var(x, axis=-1, keepdims=True)
            return (x - mu) * jax.lax.rsqrt(var + EPS_LN) * g + b
        n, f, c = x.shape
        qkv = jnp.einsum('nfc,oc->nfo', x, Wqkv)
        q, k, v = jnp.split(qkv, 3, axis=-1)
        q = q.reshape(n, f, H, D)
        k = k.reshape(n, f, H, D)
        v = v.reshape(n, f, H, D)
        q = jax.nn.elu(q) + 1.0
        k = jax.nn.elu(k) + 1.0
        kv = jnp.einsum('nshd,nshm->nhmd', k, v)
        ksum = jnp.sum(k, axis=1)
        z = 1.0 / (jnp.einsum('nlhd,nhd->nlh', q, ksum) + EPS_ATTN)
        t = jnp.einsum('nlhd,nhmd,nlh->nlhm', q, kv, z)
        t = t.reshape(n, f, c)
        x1 = layer_norm(t + x, ln1_g, ln1_b)
        h = jax.nn.gelu(jnp.einsum('nfc,oc->nfo', x1, W1) + b1, approximate=False)
        y = jnp.einsum('nfc,oc->nfo', h, W2) + b2
        return layer_norm(y + x1, ln2_g, ln2_b)

    def _L0_ffn_ref(x, attention_mask, wr, br, w1, b1, w2, b2):
        import jax, jax.numpy as jnp
        import numpy as np
        B, S, D = (8, 512, 256)
        H = 4 * D
        CAPACITY = 0.5
        b, s, d = x.shape
        weights = (jnp.einsum('bsd,do->bso', x, wr) + br)[..., 0]
        k = max(1, int(CAPACITY * s))
        kk = k - 1 if k > 1 else 1
        _, idx = jax.lax.top_k(weights, k)
        sel_idx = idx[:, :kk]
        sel = jnp.take_along_axis(x, sel_idx[:, :, None], axis=1)
        h = jax.nn.gelu(jnp.einsum('bkd,dh->bkh', sel, w1) + b1)
        y = jnp.einsum('bkh,hd->bkd', h, w2) + b2
        w_sel = jnp.take_along_axis(weights, sel_idx, axis=1)
        y = y * w_sel[..., None]
        batch_idx = jnp.arange(b)[:, None]
        processed = jnp.zeros_like(x).at[batch_idx, sel_idx].set(y)
        return processed + x

    def _L1_gnn_ref(h, weight, gamma, beta, src, dst, rel):
        import jax, jax.numpy as jnp
        import numpy as np
        N_NODES = 2500
        N_EDGES = 40000
        NUM_RELS = 8
        DIM = 256
        BN_EPS = 1e-05
        all_h = jnp.einsum('ni,rio->nro', h, weight)
        msg = all_h[src, rel]
        agg = jax.ops.segment_sum(msg, dst, num_segments=h.shape[0])
        mean = jnp.mean(agg, axis=0)
        var = jnp.mean(jnp.square(agg - mean), axis=0)
        out = (agg - mean) * jax.lax.rsqrt(var + BN_EPS) * gamma + beta
        return out

    def _L1_mix_ref(seq, wq, wk, wv, wo, bo, ln_k_g, ln_k_b, ln_v_g, ln_v_b):
        import jax, jax.numpy as jnp
        import numpy as np
        import math
        EMBED = 256
        HEADS = 4
        HEAD_DIM = EMBED // HEADS
        OUT_DIM = 256
        LN_EPS = 1e-05

        def _qkv_init(key):
            spread = math.sqrt(3.0 / EMBED)
            gain, delta = (0.01, 0.01)
            w = jax.random.uniform(key, (EMBED, EMBED), minval=-spread, maxval=spread) * gain
            return w + delta * jnp.eye(EMBED, dtype=w.dtype)

        def _layer_norm(x, g, b):
            mu = jnp.mean(x, axis=-1, keepdims=True)
            var = jnp.mean(jnp.square(x - mu), axis=-1, keepdims=True)
            return (x - mu) * jax.lax.rsqrt(var + LN_EPS) * g + b

        def _split_heads(x, B, S):
            return x.reshape(B, S, HEADS, HEAD_DIM).transpose(0, 2, 1, 3)
        B, S, _ = seq.shape
        q = _split_heads(seq @ wq.T, B, S)
        k = _split_heads(seq @ wk.T, B, S)
        v = _split_heads(seq @ wv.T, B, S)
        k = _layer_norm(k, ln_k_g, ln_k_b)
        v = _layer_norm(v, ln_v_g, ln_v_b)
        kv = jnp.einsum('bhsd,bhse->bhde', k, v) / S
        ga = jnp.einsum('bhsd,bhde->bhse', q, kv)
        ga = ga.transpose(0, 2, 1, 3).reshape(B, S, EMBED)
        return ga @ wo.T + bo

    def _L1_ffn_ref(x, Wr, br, W1, b1, W2, b2, gamma, beta):
        import math
        import jax, jax.numpy as jnp
        import numpy as np
        CAPACITY_FACTOR = 1.25
        TOP_K = 2
        LN_EPS = 1e-05

        def _layer_norm(x, gamma, beta):
            mu = jnp.mean(x, axis=-1, keepdims=True)
            var = jnp.var(x, axis=-1, keepdims=True)
            return (x - mu) * jax.lax.rsqrt(var + LN_EPS) * gamma + beta
        B, S, D = x.shape
        E = Wr.shape[1]
        N = B * S
        K = TOP_K
        logits = jnp.mean(x, axis=1) @ Wr + br
        routing_weights = jax.nn.softmax(logits, axis=-1)
        capacity = float(math.ceil(N * CAPACITY_FACTOR / E))
        expected_loads = routing_weights.sum(axis=0) * (N / B)
        scale = jnp.where(expected_loads > capacity, capacity / expected_loads, 1.0)
        routing_weights = jax.nn.softmax(routing_weights * scale, axis=-1)
        rw_tok = jnp.broadcast_to(routing_weights[:, None, :], (B, S, E)).reshape(N, E)
        top_w, top_i = jax.lax.top_k(rw_tok, K)
        top_w = jax.nn.softmax(top_w, axis=-1)
        xf = x.reshape(N, D)
        h = jax.nn.gelu(jnp.einsum('nd,edf->enf', xf, W1) + b1[:, None, :], approximate=False)
        y = jnp.einsum('enf,efd->end', h, W2) + b2[:, None, :]
        w_dense = jnp.zeros((N, E), x.dtype).at[jnp.arange(N)[:, None], top_i].add(top_w)
        out = jnp.einsum('ne,end->nd', w_dense, y).reshape(B, S, D)
        out = _layer_norm(out + x, gamma, beta)
        return out
    edge_index = jnp.stack([src, dst])
    xn = _layernorm(x, axis=-1)
    x = x + _L0_gnn_ref(xn, L0_gnn_weights, L0_gnn_roots, L0_gnn_biases, L0_gnn_ln_gamma, L0_gnn_ln_beta, edge_index, edge_type_4) + _L0_mix_ref(xn[None], L0_mix_Wqkv, L0_mix_ln1_g, L0_mix_ln1_b, L0_mix_W1, L0_mix_b1, L0_mix_W2, L0_mix_b2, L0_mix_ln2_g, L0_mix_ln2_b)[0]
    x = x + _L0_ffn_ref(_layernorm(x, axis=-1)[None], L0_ffn_attention_mask, L0_ffn_wr, L0_ffn_br, L0_ffn_w1, L0_ffn_b1, L0_ffn_w2, L0_ffn_b2)[0]
    xn = _layernorm(x, axis=-1)
    x = x + _L1_gnn_ref(xn, L1_gnn_weight, L1_gnn_gamma, L1_gnn_beta, src, dst, edge_type_8) + _L1_mix_ref(xn[None], L1_mix_wq, L1_mix_wk, L1_mix_wv, L1_mix_wo, L1_mix_bo, L1_mix_ln_k_g, L1_mix_ln_k_b, L1_mix_ln_v_g, L1_mix_ln_v_b)[0]
    x = x + _L1_ffn_ref(_layernorm(x, axis=-1)[None], L1_ffn_Wr, L1_ffn_br, L1_ffn_W1, L1_ffn_b1, L1_ffn_W2, L1_ffn_b2, L1_ffn_gamma, L1_ffn_beta)[0]
    return x

_drawn_inputs = setup_inputs


def setup_inputs(seed=0):
    import zlib

    import numpy as np

    out = dict(_drawn_inputs(seed))
    spreads = {'L0_gnn_ln_gamma': (1.0, 0.2),
     'L0_gnn_ln_beta': (0.0, 0.1),
     'L0_mix_ln1_g': (1.0, 0.2),
     'L0_mix_ln1_b': (0.0, 0.1),
     'L0_mix_ln2_g': (1.0, 0.2),
     'L0_mix_ln2_b': (0.0, 0.272),
     'L0_ffn_b1': (0.0, 0.8),
     'L0_ffn_b2': (0.0, 0.8),
     'L1_gnn_gamma': (1.0, 0.6),
     'L1_gnn_beta': (0.0, 1.011),
     'L1_mix_ln_k_g': (1.0, 0.6),
     'L1_mix_ln_k_b': (0.0, 0.8),
     'L1_mix_ln_v_g': (1.0, 0.6),
     'L1_mix_ln_v_b': (0.0, 0.8),
     'L1_ffn_br': (0.0, 0.8),
     'L1_ffn_b1': (0.0, 2.0),
     'L1_ffn_b2': (0.0, 2.0),
     'L1_ffn_gamma': (1.0, 0.6),
     'L1_ffn_beta': (0.0, 1.249)}
    factors = {'L0_gnn_biases': 8.0,
     'L0_mix_Wqkv': 8.0,
     'L0_mix_b1': 8.0,
     'L0_mix_b2': 5.126,
     'L0_ffn_wr': 8.0,
     'L0_ffn_w1': 8.0,
     'L0_ffn_w2': 8.0,
     'L1_mix_wq': 8.0,
     'L1_mix_wk': 8.0,
     'L1_mix_wv': 8.0,
     'L1_mix_wo': 8.0,
     'L1_mix_bo': 20.395}
    for name, (base, spread) in spreads.items():
        noise = np.random.default_rng([zlib.crc32(name.encode()), seed]).standard_normal(out[name].shape)
        drawn = base * np.exp(spread * noise) if base else spread * noise
        out[name] = jnp.asarray(drawn.astype(out[name].dtype))
    for name, factor in factors.items():
        out[name] = (out[name] * factor).astype(out[name].dtype)
    return out
```

```python
from contextlib import ExitStack

import concourse.bass as bass
from concourse import mybir

ALU = mybir.AluOpType
ACT = mybir.ActivationFunctionType
AX = mybir.AxisListType
F32 = mybir.dt.float32
BF16 = mybir.dt.bfloat16
I32 = mybir.dt.int32
ds = bass.ds

P = 128
N = 6250
D = 256
KH = D // P
E = 100000
NT = -(-N // P)
GT = 7
NG = NT // GT
NP = NT * P
LAST = N - (NT - 1) * P
GR = GT * P
CH = ((0, 4), (4, 3))
DEPTH, REL0, REL1 = 4, 4, 8
EPS = 1e-5
SLOTS = 16
HALF = SLOTS // 2
STEPS = -(-(E // P + 1 + NT) // SLOTS) * SLOTS
BODIES = STEPS // SLOTS
SB = -(-STEPS // P)
EP = 125
EC = E // EP
RECN = E + P
KK = N // 2 - 1
BIG = 1.0e30
assert NG * GT == NT and EP * EC == E


class Ledger:

    def __init__(self):
        self.used = [0] * 8

    def plan(self, banks, rounds):
        base = list(self.used)
        per = [banks.count(b) for b in range(8)]
        for b in range(8):
            self.used[b] += per[b] * rounds
        turns = []
        for j, b in enumerate(banks):
            turns.append((b, base[b] + banks[:j].count(b) + 1, per[b]))

        def turn(j, g):
            b, first, step = turns[j]
            return b, g * step + first

        return turn


class Core:
    pass


def rows_of(dram, first, tiles):
    return dram[ds(first, tiles * P), :].rearrange("(k p) c -> p k c", p=P)


def group(resident, g):
    return resident[:, ds(g * (GT * D), GT * D)].rearrange("p (k c) -> p k c", c=D)


def tile_of(resident, g, k, a=0, w=D):
    return resident[:, ds(g * (GT * D) + (k * D + a), w)]


def load_tiles(eng, c, first, n=HALF):
    regs = c.regs[str(eng.engine)][:n]
    eng.reg_load(regs, c.tile_row[0:1, ds(first, n)])
    return [eng.snap(r, min_val=0, max_val=NT - 1) for r in regs]


def gate(eng, c):
    eng.sem_inc(c.gates[str(eng.engine)], 1)


def transposed(pe, c, src, turn, j0, g, ready=None):
    for h in range(KH):
        for n, (k0, m) in enumerate(CH):
            b, t = turn(j0 + 2 * h + n, g)
            pe.wait_ge(c.bank_free[b], t)
            gate(pe, c)
            for k in range(k0, k0 + m):
                last = c.nc.tensor.transpose(c.bank[b][:, (k - k0) * P:(k - k0 + 1) * P], src(k, h), c.ident[:])
            last.then_inc(c.bank_full[b], 1)


def evacuate_transposed(act, c, dst, turn, j0, g, done):
    for h in range(KH):
        for n, (k0, m) in enumerate(CH):
            b, t = turn(j0 + 2 * h + n, g)
            act.wait_ge(c.bank_full[b], t)
            c.nc.scalar.copy(dst[:, h, k0 * P:(k0 + m) * P], c.bank[b][:, 0:m * P]).then_inc(c.bank_free[b], 1)
    act.wait_ge(c.bank_free[b], t + 1)
    act.sem_inc(done, 1)


def stats(dve, c, src, g, s_bn, s_mv):
    for k in range(GT):
        c.nc.vector.bn_stats(c.bn[:, k, :], src(k)).then_inc(s_bn, 1)
    dve.wait_ge(s_bn, (g + 1) * GT)
    gate(dve, c)
    for k in range(GT):
        c.nc.vector.bn_aggr(c.mv[:, k, :], c.bn[:, k, :]).then_inc(s_mv, 1)


def rstd(pool, c, g, s_mv, s_rs, s_tmp):
    pool.wait_ge(s_mv, (g + 1) * GT)
    c.nc.gpsimd.tensor_tensor(c.ve[:], c.mv[:, :, 1], c.eps7[:], ALU.add).then_inc(s_tmp, 1)
    pool.wait_ge(s_tmp, g + 1)
    c.nc.gpsimd.tensor_tensor(c.rs[:], c.ve[:], c.pow7[:], ALU.pow).then_inc(s_rs, 1)


def normalise(dve, c, dst, src, g, s_rs, done):
    dve.wait_ge(s_rs, g + 1)
    gate(dve, c)
    for k in range(GT):
        ins = c.nc.vector.tensor_scalar(dst(k), src(k), c.mv[:, k, 0:1], c.rs[:, k:k + 1], ALU.subtract, ALU.mult)
        ins.then_inc(done, 1)


def carver(resident):
    at = [0]

    def cut(*shape):
        n = 1
        for s in shape:
            n *= s
        view = resident[:, at[0]:at[0] + n]
        at[0] += n
        assert at[0] <= NT * D
        names = "abcd"[:len(shape)]
        if len(shape) == 1:
            return view
        return view.rearrange(f"p ({' '.join(names)}) -> p {' '.join(names)}", **dict(zip(names, shape)))

    return cut


class Phase:

    def __init__(self, nc, name):
        self.nc, self.name, self.held, self.stack = nc, name, [], ExitStack()

    def sem(self, name):
        self.held.append(self.nc.alloc_semaphore(f"{self.name}_{name}"))
        return self.held[-1]

    def sems(self, names):
        return [self.sem(n) for n in names.split()]

    def sb(self, name, shape, dtype=F32):
        return self.stack.enter_context(self.nc.sbuf_tensor(f"{self.name}_{name}", shape, dtype))

    def __enter__(self):
        return self

    def __exit__(self, *_):
        self.stack.close()
        self.nc.clear_and_free_semaphores(self.held)
        self.nc.all_engine_barrier()


def edge_tables(nc, c, src, dst, et4, et8):
    with Phase(nc, "edges") as ph:
        sb, sem = ph.sb, ph.sem
        e_src, e_dst, e_t4, e_t8 = (sb(n, [EP, EC], I32) for n in ("e_src", "e_dst", "e_t4", "e_t8"))
        e_rec = sb("e_rec", [EP, EC, 4], I32)
        e_tail = sb("e_tail", [P, 4], I32)
        hit = sb("hit", [EP, EC], F32)
        below = sb("below", [EP, NT + 1], F32)
        start = sb("start", [P, NT + 1], F32)
        cnt = sb("cnt", [P, NT], F32)
        cnt_i = sb("cnt_i", [P, NT], I32)
        nst = sb("nst", [P, NT], F32)
        cum = sb("cum", [P, 2, NT], F32)
        step_no = sb("step_no", [P, SB], F32)
        begun = sb("begun", [P, SB, NT], F32)
        over = sb("over", [P, SB, NT], F32)
        prod = sb("prod", [P, SB, NT], F32)
        tile_f = sb("tile_f", [P, SB], F32)
        base_f = sb("base_f", [P, SB], F32)
        s_f = sb("s_f", [P, SB], F32)
        end_f = sb("end_f", [P, SB], F32)
        e0 = sb("e0", [P, SB], F32)
        e0_i = sb("e0_i", [P, SB], I32)
        left = sb("left", [P, SB], F32)
        low = sb("low", [P, SB], F32)
        tile_i = sb("tile_i", [P, SB], I32)
        rows = c.xn[:, 0:SB * 4 * P].bitcast(I32).rearrange("p (b n) -> p b n", b=SB)
        slot_no = sb("slot_no", [P, P], F32)
        plane = c.agg[:, 0:SB * 4 * P].rearrange("p (b f s) -> p b f s", b=SB, f=4)
        valid = c.agg[:, SB * 4 * P:SB * 5 * P].rearrange("p (b s) -> p b s", b=SB)
        row8 = sb("row8", [P, SB * P], I32)
        rec_d = c.rec_d
        s_in, s_rec, s_recd, s_gat, s_tl, s_tr = (sem(n) for n in (
            "edges_in", "records_made", "records_stored", "records_gathered", "step_tiles_stored", "tile_row_loaded"))
        s_below, s_v, s_pl, s_iota, s_e0, s_ti, s_meta = (sem(n) for n in (
            "below_counted", "edge_vector_steps", "planes_made", "iotas_made", "step_starts_made",
            "step_tiles_made", "planes_copied"))
        turn = c.ledger.plan([b for b in range(7)] + [7], 1)
        with nc.Block() as block:

            @block.sync
            def _(sp):
                for to, of in ((e_src, src), (e_dst, dst), (e_t4, et4), (e_t8, et8)):
                    sp.dma_start(to[:], of.rearrange("(p n) -> p n", p=EP)).then_inc(s_in, 16)
                sp.wait_ge(s_rec, 4 + 1)
                sp.dma_start(rec_d[0:E, :].rearrange("(p n) f -> p n f", p=EP), e_rec[:]).then_inc(s_recd, 16)
                sp.dma_start(rec_d[E:RECN, :], e_tail[:]).then_inc(s_recd, 16)
                sp.wait_ge(s_ti, 1)
                sp.dma_start(c.tl_d.rearrange("(b p) -> p b", p=P), tile_i[:],
                             allow_slow_non_contiguous=True).then_inc(s_tl, 16)
                sp.wait_ge(s_tl, 16)
                sp.dma_start(c.tile_row[:], c.tl_d.rearrange("(a n) -> a n", a=1)).then_inc(s_tr, 16)
                sp.wait_ge(s_meta, 4 * SB)
                sp.dma_start(c.row8_d, row8[:]).then_inc(s_tr, 16)
                sp.wait_ge(s_tr, 32)

            @block.gpsimd
            def _(pool):
                nc.gpsimd.memset(e_tail[:], 0).then_inc(s_rec, 1)
                nc.gpsimd.iota(step_no[:], [[P, SB]], base=0, channel_multiplier=1,
                               allow_small_or_imprecise_dtypes=True).then_inc(s_iota, 1)
                nc.gpsimd.iota(slot_no[:], [[1, P]], base=0, channel_multiplier=0,
                               allow_small_or_imprecise_dtypes=True).then_inc(s_iota, 1)
                pool.wait_ge(s_recd, 32)
                pool.wait_ge(s_e0, 1)
                for b in range(SB):
                    nc.gpsimd.indirect_dma_start(
                        out=rows[:, b, :], out_offset=None, in_=rec_d,
                        in_offset=bass.IndirectOffsetOnAxis(ap=e0_i[:, b:b + 1], axis=0)).then_inc(s_gat, 16)

            @block.vector
            def _(dve):
                v = nc.vector
                done = [0]

                def then(ins):
                    done[0] += 1
                    ins.then_inc(s_v, 1)
                    dve.wait_ge(s_v, done[0])

                v.memset(below[:, 0:1], 0.0).then_inc(s_below, 1)
                dve.wait_ge(s_in, 64)
                v.scalar_tensor_tensor(e_rec[:, :, 0], e_t4[:], float(NP), e_src[:], ALU.mult, ALU.add).then_inc(s_rec, 1)
                v.scalar_tensor_tensor(e_rec[:, :, 1], e_t8[:], float(NP), e_src[:], ALU.mult, ALU.add).then_inc(s_rec, 1)
                v.tensor_copy(e_rec[:, :, 2], e_dst[:]).then_inc(s_rec, 1)
                v.tensor_copy(e_rec[:, :, 3], e_t4[:]).then_inc(s_rec, 1)
                for t in range(1, NT + 1):
                    if t > 1:
                        dve.wait_ge(s_below, t)
                    v.tensor_scalar(hit[:], e_dst[:], float(P * t), 0.0, ALU.is_lt, ALU.add,
                                    accum_out=below[:, t:t + 1]).then_inc(s_below, 1)
                dve.wait_ge(c.bank_full[0], 1)
                then(v.tensor_copy(start[:], c.bank[0][:, 0:NT + 1]))
                then(v.tensor_tensor(cnt[:], start[:, 1:NT + 1], start[:, 0:NT], ALU.subtract))
                then(v.tensor_scalar(cnt_i[:], cnt[:], float(P - 1), None, ALU.add))
                then(v.tensor_scalar(cnt_i[:], cnt_i[:], 7, None, ALU.arith_shift_right))
                then(v.tensor_copy(nst[:], cnt_i[:]))
                then(v.tensor_copy(cum[:, 0, :], nst[:]))
                s, at = 1, 0
                while s < NT:
                    then(v.tensor_copy(cum[:, 1 - at, 0:s], cum[:, at, 0:s]))
                    then(v.tensor_tensor(cum[:, 1 - at, s:NT], cum[:, at, s:NT], cum[:, at, 0:NT - s], ALU.add))
                    s, at = 2 * s, 1 - at
                incl, excl = cum[:, at, :], cum[:, 1 - at, :]
                then(v.tensor_tensor(excl, incl, nst[:], ALU.subtract))
                dve.wait_ge(s_iota, 2)
                wide = lambda a: a.unsqueeze(1).to_broadcast([P, SB, NT])
                num = step_no[:].unsqueeze(2).to_broadcast([P, SB, NT])
                then(v.tensor_tensor(over[:], wide(incl), num, ALU.is_le))
                then(v.tensor_tensor(begun[:], wide(excl), num, ALU.is_le))
                then(v.tensor_reduce(tile_f[:], over[:], AX.X, ALU.add))
                then(v.tensor_tensor(prod[:], over[:], wide(nst[:]), ALU.mult))
                then(v.tensor_reduce(base_f[:], prod[:], AX.X, ALU.add))
                then(v.tensor_tensor(prod[:], over[:], wide(cnt[:]), ALU.mult))
                then(v.tensor_reduce(s_f[:], prod[:], AX.X, ALU.add))
                then(v.tensor_tensor(prod[:], begun[:], wide(cnt[:]), ALU.mult))
                then(v.tensor_reduce(end_f[:], prod[:], AX.X, ALU.add))
                then(v.tensor_scalar(tile_f[:], tile_f[:], float(NT - 1), None, ALU.min))
                v.tensor_copy(tile_i[:], tile_f[:]).then_inc(s_ti, 1)
                then(v.tensor_tensor(e0[:], step_no[:], base_f[:], ALU.subtract))
                then(v.scalar_tensor_tensor(e0[:], e0[:], float(P), s_f[:], ALU.mult, ALU.add))
                then(v.tensor_scalar(e0[:], e0[:], float(E), None, ALU.min))
                v.tensor_copy(e0_i[:], e0[:]).then_inc(s_e0, 1)
                then(v.tensor_tensor(left[:], end_f[:], e0[:], ALU.subtract))
                then(v.tensor_scalar(low[:], tile_f[:], float(P), -1.0, ALU.mult, ALU.add))
                for b in range(SB):
                    then(v.tensor_scalar(valid[:, b, :], slot_no[:], left[:, b:b + 1], None, ALU.is_lt))
                dve.wait_ge(s_gat, 16 * SB)
                recs = rows[:].rearrange("p b (s f) -> p b s f", f=4)
                for b in range(SB):
                    for f in (0, 1):
                        then(v.tensor_scalar(plane[:, b, f, :], recs[:, b, :, f], -float(1 << 20), None, ALU.add))
                        then(v.tensor_tensor(plane[:, b, f, :], plane[:, b, f, :], valid[:, b, :], ALU.mult))
                        then(v.tensor_scalar(plane[:, b, f, :], plane[:, b, f, :], float(1 << 20), None, ALU.add))
                    then(v.tensor_scalar(plane[:, b, 2, :], recs[:, b, :, 2], low[:, b:b + 1], None, ALU.subtract))
                    then(v.tensor_tensor(plane[:, b, 2, :], plane[:, b, 2, :], valid[:, b, :], ALU.mult))
                    then(v.tensor_scalar(plane[:, b, 2, :], plane[:, b, 2, :], -1.0, None, ALU.add))
                    v.tensor_copy(plane[:, b, 3, :], recs[:, b, :, 3]).then_inc(s_pl, 1)
                for b in range(SB):
                    bb, t = turn(1 + b if b < 6 else 7, 0)
                    dve.wait_ge(c.bank_full[bb], t)
                    for f, to in enumerate((c.row4, row8, c.local, c.rel4)):
                        ins = v.tensor_copy(to[:, b * P:(b + 1) * P], c.bank[bb][:, f * P:(f + 1) * P])
                        ins.then_inc(s_meta, 1)
                    dve.wait_ge(s_meta, 4 * (b + 1))
                    dve.sem_inc(c.bank_free[bb], 1)
                dve.sem_inc(c.bank_free[0], 1)

            @block.tensor
            def _(pe):
                pe.wait_ge(s_below, NT + 1)
                nc.tensor.matmul(c.bank[0][:, 0:NT + 1], c.ones[0:EP, :], below[:], start=True, stop=True)\
                    .then_inc(c.bank_full[0], 1)
                for b in range(SB):
                    bb, t = turn(1 + b if b < 6 else 7, 0)
                    pe.wait_ge(s_pl, b + 1)
                    for f in range(4):
                        ins = nc.tensor.transpose(c.bank[bb][:, f * P:(f + 1) * P], plane[:, b, f, :], c.ident[:])
                    ins.then_inc(c.bank_full[bb], 1)


def edge_weights(nc, c):
    PARTS = 3
    W = PARTS * REL0
    with Phase(nc, "degree") as ph:
        sb = ph.sb
        hot = sb("hot", [P, 2, SLOTS, P], BF16)
        hot_t = sb("hot_t", [P, 2, SLOTS, P], BF16)
        rel = sb("rel", [P, 2, SLOTS, REL0], BF16)
        wide_rel = sb("wide_rel", [P, SLOTS, W], F32)
        picked = sb("picked", [P, SLOTS, W], F32)
        rel_no = sb("rel_no", [P, W], F32)
        count = sb("count", [P, NT, REL0], F32)
        rest = sb("rest", [P, NT, REL0], F32)
        inv = sb("inv", [P, NT, W], BF16)
        ident16 = sb("ident16", [P, P], BF16)
        zero = sb("zero", [P, NT * REL0], BF16)
        (s_set, s_hot, s_hot2, s_cnt, s_tot, s_free, s_v, s_inv, s_turned, s_ht, s_rel, s_pick, s_w, s_out) = ph.sems(
            "constants_set hot_made hot_made_again counts_summed totals_made totals_read vector_steps inverse_made hot_turned hot_copied "
            "relation_made weights_picked weights_masked weights_made")
        iota = c.iota[:].unsqueeze(1).to_broadcast([P, SLOTS, P])
        b4 = c.iota[:, 0:REL0].unsqueeze(1).to_broadcast([P, SLOTS, REL0])
        loc = lambda i: c.local[:, ds(i * SLOTS, SLOTS)].unsqueeze(2).to_broadcast([P, SLOTS, P])
        ret = lambda i, w: c.rel4[:, ds(i * SLOTS, SLOTS)].unsqueeze(2).to_broadcast([P, SLOTS, w])
        PAIRS = BODIES // 2
        assert PAIRS * 2 == BODIES
        totals = c.bank[0][:, 0:NT * REL0]
        with nc.Block() as block:

            @block.vector
            def _(dve):
                v = nc.vector
                v.tensor_copy(ident16[:], c.ident[:]).then_inc(s_set, 1)
                v.memset(zero[:], 0.0).then_inc(s_set, 1)
                for k in range(PARTS):
                    v.tensor_copy(rel_no[:, k * REL0:(k + 1) * REL0], c.iota[:, 0:REL0]).then_inc(s_set, 1)

                with dve.Fori(0, PAIRS) as q:
                    for h in range(2):
                        n = q * 2 + h
                        dve.wait_ge(s_cnt, n + 1)
                        gate(dve, c)
                        v.tensor_tensor(hot[:, h], iota, loc(n), ALU.is_equal).then_inc(s_hot, 1)
                        v.tensor_tensor(rel[:, h], b4, ret(n, REL0), ALU.is_equal).then_inc(s_hot, 1)
                done = [0]

                def then(ins):
                    done[0] += 1
                    ins.then_inc(s_v, 1)
                    dve.wait_ge(s_v, done[0])

                dve.wait_ge(s_tot, 1)
                then(v.tensor_scalar(count[:].rearrange("p t r -> p (t r)"), totals, 1.0, None, ALU.max))
                then(v.reciprocal(count[:], count[:]))
                part = lambda k: inv[:, :, k * REL0:(k + 1) * REL0]
                then(v.tensor_copy(part(0), count[:]))
                then(v.tensor_tensor(rest[:], count[:], part(0), ALU.subtract))
                then(v.tensor_copy(part(1), rest[:]))
                then(v.tensor_tensor(rest[:], rest[:], part(1), ALU.subtract))
                then(v.tensor_copy(part(2), rest[:]))
                dve.sem_inc(s_inv, 1)

                def make(n, h):
                    dve.wait_ge(s_turned, n + 1)
                    gate(dve, c)
                    v.tensor_tensor(hot[:, h], iota, loc(n), ALU.is_equal).then_inc(s_hot2, 1)

                def weigh(n, h):
                    dve.wait_ge(s_w, n + 2)
                    dve.wait_ge(s_out, n + 1)
                    gate(dve, c)
                    v.tensor_tensor(wide_rel[:], rel_no[:].unsqueeze(1).to_broadcast([P, SLOTS, W]), ret(n, W),
                                    ALU.is_equal).then_inc(s_rel, 1)
                    dve.wait_ge(s_pick, n + 3)
                    dve.wait_ge(s_rel, n + 1)
                    v.tensor_tensor(picked[:], c.bank[6 + h][:, 0:SLOTS * W].rearrange("p (s r) -> p s r", r=W),
                                    wide_rel[:], ALU.mult).then_inc(s_w, 1)
                    dve.wait_ge(s_w, n + 3)
                    gate(dve, c)
                    v.tensor_reduce(c.meta[:, ds(n * SLOTS, SLOTS), 1], picked[:], AX.X, ALU.add).then_inc(s_out, 1)

                dve.sem_inc(s_w, 2)
                dve.sem_inc(s_out, 1)
                dve.wait_ge(s_set, 2 + PARTS)
                make(0, 0)
                with dve.Fori(0, PAIRS) as q:
                    make(q * 2 + 1, 1)
                    weigh(q * 2, 0)
                    make(q * 2 + 2, 0)
                    weigh(q * 2 + 1, 1)

            @block.tensor
            def _(pe):
                pe.wait_ge(s_set, 2 + PARTS)
                nc.tensor.matmul(totals, ident16[:], zero[:], start=True, stop=False)
                pe.sem_inc(s_cnt, 2)
                with pe.Fori(0, PAIRS) as q:
                    for h in range(2):
                        n = q * 2 + h
                        for u in range(SLOTS):
                            if u % HALF == 0:
                                tiles = load_tiles(pe, c, n * SLOTS + u)
                            if u == 0:
                                pe.wait_ge(s_hot, n * 2 + 2)
                            ins = nc.tensor.matmul(c.bank[0][:, ds(tiles[u % HALF] * REL0, REL0)], hot[:, h, u, :],
                                                   rel[:, h, u, :], start=False, stop=False)
                        ins.then_inc(s_cnt, 1)
                nc.tensor.matmul(totals, ident16[:], zero[:], start=False, stop=True).then_inc(s_tot, 1)

                def turn(n, h):
                    pe.wait_ge(s_hot2, n + 1)
                    pe.wait_ge(s_ht, n * 2 + 2)
                    gate(pe, c)
                    for u in range(SLOTS):
                        ins = nc.tensor.transpose(c.bank[2 + 2 * h + u // HALF][:].bitcast(BF16)[:, (u % HALF) * P:(u % HALF + 1) * P],
                                                  hot[:, h, u, :], ident16[:])
                    ins.then_inc(s_turned, 1)

                def pick(n, h):
                    for u in range(SLOTS):
                        if u % HALF == 0:
                            tiles = load_tiles(pe, c, n * SLOTS + u)
                        if u == 0:
                            pe.wait_ge(s_ht, n * 2 + 6)
                            pe.wait_ge(s_w, n + 1)
                        ins = nc.tensor.matmul(c.bank[6 + h][:, u * W:(u + 1) * W], hot_t[:, h, u, :],
                                               inv[:].rearrange("p t r -> p (t r)")[:, ds(tiles[u % HALF] * W, W)],
                                               start=True, stop=True)
                    ins.then_inc(s_pick, 1)

                pe.wait_ge(s_inv, 1)
                pe.sem_inc(s_turned, 2)
                pe.sem_inc(s_pick, 2)
                turn(0, 0)
                with pe.Fori(0, PAIRS) as q:
                    turn(q * 2 + 1, 1)
                    pick(q * 2, 0)
                    turn(q * 2 + 2, 0)
                    pick(q * 2 + 1, 1)

            @block.scalar
            def _(act):
                act.sem_inc(s_ht, 4)
                with act.Fori(0, PAIRS) as q:
                    for h in range(2):
                        n = q * 2 + h
                        act.wait_ge(s_turned, n + 3)
                        act.wait_ge(s_pick, n + 1)
                        for b in range(2):
                            nc.scalar.copy(hot_t[:, h, b * HALF:(b + 1) * HALF, :],
                                           c.bank[2 + 2 * h + b][:].bitcast(BF16).rearrange("p (u e) -> p u e", u=HALF)).then_inc(s_ht, 1)


class EdgeSum:

    def __init__(self, nc, c):
        self.nc, self.c = nc, c
        self.landed = [c.sem(f"message{s}_landed") for s in range(SLOTS)]
        self.ring_ready, self.hot_ready, self.summed, self.added = (
            c.sem(n) for n in ("slots_copied", "hot_made", "steps_summed", "steps_added"))

    def use(self, msg, hot, row_ring, meta_ring, rows, table, weighted):
        self.msg, self.hot = msg, hot
        self.row_ring, self.meta_ring, self.rows, self.table, self.weighted = row_ring, meta_ring, rows, table, weighted

    def scalar(self, act, i, n):
        for h in range(2):
            act.wait_ge(self.summed, n * SLOTS + (h + 1) * HALF)
            gate(act, self.c)
            at = ds(i * SLOTS + h * HALF, HALF)
            self.nc.scalar.copy(self.row_ring[:, h, :], self.rows[:, at]).then_inc(self.ring_ready, 1)
            self.nc.scalar.copy(self.meta_ring[:, h, :, :], self.c.meta[:, at, :]).then_inc(self.ring_ready, 1)

    def gpsimd(self, pool, n):
        for h in range(2):
            pool.wait_ge(self.ring_ready, n * 4 + (2 * h + 2))
            gate(pool, self.c)
            for u in range(HALF):
                s = h * HALF + u
                self.nc.gpsimd.indirect_dma_start(
                    out=self.msg[:, s, :], out_offset=None, in_=self.table,
                    in_offset=bass.IndirectOffsetOnAxis(ap=self.row_ring[:, h, u:u + 1], axis=0),
                    bounds_check=self.table.shape[0] - 1, oob_is_err=False).then_inc(self.landed[s], 16)

    def vector(self, dve, i, n):
        for h in range(2):
            dve.wait_ge(self.ring_ready, n * 4 + (2 * h + 2))
            for u in range(HALF):
                m = self.meta_ring[:, h, u, :]
                if self.weighted:
                    ins = self.nc.vector.tensor_scalar(self.hot[:, h * HALF + u, :], self.c.iota[:], m[:, 0:1], m[:, 1:2],
                                                       ALU.is_equal, ALU.mult)
                else:
                    ins = self.nc.vector.tensor_scalar(self.hot[:, h * HALF + u, :], self.c.iota[:], m[:, 0:1], None,
                                                       ALU.is_equal)
                ins.then_inc(self.hot_ready, 1)
            tiles = load_tiles(dve, self.c, i * SLOTS + h * HALF)
            for u, t in enumerate(tiles):
                s = h * HALF + u
                dve.wait_ge(self.summed, n * SLOTS + (SLOTS + s + 1))
                dve.wait_ge(self.added, n * SLOTS + (4 + s))
                at = self.c.agg[:, ds(t * D, D)]
                self.nc.vector.tensor_tensor(at, at, self.c.bank[4 + s % 4][:, 0:D], ALU.add).then_inc(self.added, 1)

    def tensor(self, pe, n):
        for s in range(SLOTS):
            pe.wait_ge(self.landed[s], n * 16 + 16)
            pe.wait_ge(self.hot_ready, n * SLOTS + s + 1)
            pe.wait_ge(self.added, n * SLOTS + (s + 1))
            self.nc.tensor.matmul(self.c.bank[4 + s % 4][:, 0:D], self.hot[:, s, :], self.msg[:, s, :],
                                  start=True, stop=True).then_inc(self.summed, 1)


def gnn0(nc, c, a):
    W, roots = a["L0_gnn_weights"], a["L0_gnn_roots"]
    with Phase(nc, "gnn0") as ph:
        sb = ph.sb
        msg = sb("msg", [P, SLOTS, D], F32)
        hot = sb("hot0", [P, SLOTS, P], F32)
        ex = sb("ex", [P, GT * D], F32)
        w = sb("w0", [P, KH, (REL0 + 1) * D], F32)
        vecs = sb("vecs", [P, 3, D], F32)
        row_ring = sb("row_ring", [P, 2, HALF], I32)
        meta_ring = sb("meta_ring", [P, 2, HALF, 2], F32)
        xt = hot[:].rearrange("p s e -> p (s e)")[:, 0:KH * GR].rearrange("p (h r) -> p h r", h=KH)
        flat_msg = msg[:].rearrange("p s d -> p (s d)")
        outs = flat_msg[:, 0:2 * REL0 * D].rearrange("p (o n) -> p o n", o=2)
        stage = flat_msg[:, 2 * REL0 * D:2 * REL0 * D + GT * D]
        edges = c.edges = EdgeSum(nc, c)
        edges.use(msg, hot, row_ring, meta_ring, c.row4, c.tab0_d, True)
        names = ("weights_in", "xt_ready", "xt_used", "tile_made", "roots_made", "bias_added", "partial", "variance",
                 "rstd", "sum", "normal", "gamma", "beta", "exp", "exp_cut", "elu", "state", "layer_tables", "staged", "vectors_in")
        (s_w, s_xt, s_xtu, s_out, s_root, s_bias, s_bn, s_mv, s_rs, s_tmp, s_nrm, s_gam, s_bet, s_exp, s_cut, s_elu,
         s_state, s_tabs, s_stage, s_vec) = (ph.sem(n) for n in names)
        s_store = [ph.sem(f"tile_stored{o}") for o in range(2)]
        NB = 3 * GT
        turn = c.ledger.plan([j % 4 for j in range(4 + NB)], DEPTH * NG)
        per = [(GT + 1) // 2, GT // 2]
        with nc.Block() as block:

            @block.sync
            def _(sp):
                with sp.Fori(0, DEPTH) as l:
                    sp.wait_ge(s_tabs, l + 1)
                    for h in range(KH):
                        sp.dma_start(w[:, h, 0:REL0 * D].rearrange("p (r o) -> p r o", r=REL0),
                                     W.rearrange("l r i o -> (l r) i o")[ds(l * REL0, REL0), h * P:(h + 1) * P, :]
                                     .rearrange("r p o -> p r o")).then_inc(s_w, 16)
                        sp.dma_start(w[:, h, REL0 * D:], roots[ds(l, 1), h * P:(h + 1) * P, :]
                                     .rearrange("l p o -> p (l o)")).then_inc(s_w, 16)
                    with sp.Fori(0, NG) as g:
                        q = l * NG + g
                        for k in range(GT):
                            sp.wait_ge(s_out, q * (2 * GT) + 2 * (k + 1))
                            at = g * GR + k * P
                            sp.dma_start(c.tab0_d.rearrange("(r n) d -> n r d", n=NP)[ds(at, P), 0:REL0, :],
                                         outs[:, k % 2, :].rearrange("p (r d) -> p r d", d=D)).then_inc(s_store[k % 2], 16)
                    sp.wait_ge(s_state, l * NG + NG)
                    for j, n in enumerate(("L0_gnn_biases", "L0_gnn_ln_gamma", "L0_gnn_ln_beta")):
                        sp.dma_start(vecs[:, j, :], a[n][ds(l, 1), :].to_broadcast([P, D])).then_inc(s_vec, 16)

            @block.tensor
            def _(pe):
                pe.sem_inc(s_tabs, 1)
                pe.sem_inc(s_xtu, 1)
                pe.sem_inc(edges.summed, SLOTS)
                with pe.Fori(0, DEPTH) as l:
                    pe.wait_ge(s_w, l * 64 + 64)
                    gate(pe, c)
                    with pe.Fori(0, NG) as g:
                        q = l * NG + g
                        pe.wait_ge(s_stage, q + 1)
                        transposed(pe, c, lambda k, h: stage[:, k * D + h * P:k * D + (h + 1) * P], turn, 0, q)
                        pe.wait_ge(s_xt, q + 1)
                        for k in range(GT):
                            for j in range(3):
                                b, t = turn(4 + 3 * k + j, q)
                                pe.wait_ge(c.bank_free[b], t)
                                width = 512 if j < 2 else D
                                for h in range(KH):
                                    ins = nc.tensor.matmul(c.bank[b][:, 0:width], xt[:, h, k * P:(k + 1) * P],
                                                           w[:, h, j * 512:j * 512 + width], start=(h == 0), stop=(h == KH - 1))
                                ins.then_inc(c.bank_full[b], 1)
                        pe.wait_ge(c.bank_full[b], t)
                        pe.sem_inc(s_xtu, 1)
                    pe.sem_inc(s_tabs, 1)
                    with pe.Fori(0, BODIES) as i:
                        edges.tensor(pe, l * BODIES + i)

            @block.scalar
            def _(act):
                for o in range(2):
                    act.sem_inc(s_store[o], 16)
                def tables(g, q):
                    act.wait_ge(s_state, q + 1)
                    act.wait_ge(s_xtu, q + 1)
                    gate(act, c)
                    nc.scalar.copy(stage, c.xn[:, ds(g * (GT * D), GT * D)]).then_inc(s_stage, 1)
                    evacuate_transposed(act, c, xt, turn, 0, q, s_xt)
                    for k in range(GT):
                        for j in range(2):
                            b, t = turn(4 + 3 * k + j, q)
                            if j == 0:
                                act.wait_ge(s_store[k % 2], (q * per[k % 2] + k // 2 + 1) * 16)
                            act.wait_ge(c.bank_full[b], t)
                            nc.scalar.copy(outs[:, k % 2, j * 512:(j + 1) * 512], c.bank[b][:]).then_inc(s_out, 1)
                            act.wait_ge(s_out, q * (2 * GT) + (2 * k + j + 1))
                            act.sem_inc(c.bank_free[b], 1)
                        b, t = turn(4 + 3 * k + 2, q)
                        act.wait_ge(c.bank_full[b], t)
                        gate(act, c)
                        nc.scalar.copy(tile_of(c.agg, g, k), c.bank[b][:, 0:D]).then_inc(s_root, 1)
                        act.wait_ge(s_root, q * GT + (k + 1))
                        act.sem_inc(c.bank_free[b], 1)

                def exponential(g, q):
                    act.wait_ge(s_bet, q + 1)
                    act.wait_ge(s_elu, q + 1)
                    gate(act, c)
                    nc.scalar.activation(ex[:], c.agg[:, ds(g * (GT * D), GT * D)], ACT.Exp).then_inc(s_exp, 1)

                with act.Fori(0, NG) as g:
                    tables(g, g)
                with act.Fori(0, DEPTH - 1) as l:
                    with act.Fori(0, BODIES) as i:
                        edges.scalar(act, i, l * BODIES + i)
                    exponential(0, l * NG)
                    with act.Fori(0, NG - 1) as g:
                        exponential(g + 1, l * NG + g + 1)
                        tables(g, l * NG + g + NG)
                    tables(NG - 1, l * NG + (2 * NG - 1))
                with act.Fori(0, BODIES) as i:
                    edges.scalar(act, i, (DEPTH - 1) * BODIES + i)
                with act.Fori(0, NG) as g:
                    exponential(g, (DEPTH - 1) * NG + g)

            @block.gpsimd
            def _(pool):
                with pool.Fori(0, DEPTH) as l:
                    for o in range(2):
                        pool.wait_ge(s_store[o], (l + 1) * (NG * per[o] * 16) + 16)
                    gate(pool, c)
                    with pool.Fori(0, BODIES) as i:
                        edges.gpsimd(pool, l * BODIES + i)
                    pool.wait_ge(edges.added, (l + 1) * STEPS + 4)
                    pool.wait_ge(s_vec, l * 48 + 48)
                    gate(pool, c)
                    with pool.Fori(0, NG) as g:
                        q = l * NG + g
                        gate(pool, c)
                        x = group(c.agg, g)
                        nc.gpsimd.tensor_tensor(x, x, vecs[:, 0:1, :].to_broadcast([P, GT, D]), ALU.add).then_inc(s_bias, 1)
                        rstd(pool, c, q, s_mv, s_rs, s_tmp)
                        pool.wait_ge(s_nrm, (q + 1) * GT)
                        gate(pool, c)
                        nc.gpsimd.tensor_tensor(x, x, vecs[:, 1:2, :].to_broadcast([P, GT, D]), ALU.mult).then_inc(s_gam, 1)

            @block.vector
            def _(dve):
                v = nc.vector
                dve.sem_inc(edges.added, 4)
                dve.sem_inc(s_state, NG)
                dve.sem_inc(s_elu, 1)
                with dve.Fori(0, DEPTH) as l:
                    dve.wait_ge(s_root, (l + 1) * NT)
                    gate(dve, c)
                    with dve.Fori(0, BODIES) as i:
                        edges.vector(dve, i, l * BODIES + i)
                    with dve.Fori(0, NG) as g:
                        q = l * NG + g
                        tile = lambda k: tile_of(c.agg, g, k)
                        dve.wait_ge(s_bias, q + 1)
                        gate(dve, c)
                        stats(dve, c, tile, q, s_bn, s_mv)
                        normalise(dve, c, tile, tile, q, s_rs, s_nrm)
                        dve.wait_ge(s_gam, q + 1)
                        x = group(c.agg, g)
                        v.tensor_tensor(x, x, vecs[:, 2:3, :].to_broadcast([P, GT, D]), ALU.add).then_inc(s_bet, 1)
                        dve.wait_ge(s_exp, q + 1)
                        v.tensor_scalar(ex[:], ex[:], 1.0, -1.0, ALU.min, ALU.add).then_inc(s_cut, 1)
                        dve.wait_ge(s_cut, q + 1)
                        flat = lambda r: r[:, ds(g * (GT * D), GT * D)]
                        v.scalar_tensor_tensor(flat(c.agg), flat(c.agg), 0.0, ex[:], ALU.max, ALU.add).then_inc(s_elu, 1)
                        dve.wait_ge(s_elu, q + 2)
                        v.tensor_tensor(flat(c.xn), flat(c.xn), flat(c.agg), ALU.add).then_inc(s_state, 1)


def spread(dram_vec, n=D):
    return dram_vec.rearrange("(a n) -> a n", a=1).to_broadcast([P, n])


def weights0(nc, c, a, wt):
    nat = c.agg[:, 0:10 * D].rearrange("p (b i) -> p b i", i=D)
    with Phase(nc, "weights0") as ph:
        s_in, = ph.sems("natural_in")
        turn = c.ledger.plan([0, 1, 2, 3, 4], 1)
        with nc.Block() as block:

            @block.sync
            def _(sp):
                for name, b, n in (("L0_mix_Wqkv", 0, 6), ("L0_mix_W1", 6, 2), ("L0_mix_W2", 8, 2)):
                    sp.dma_start(nat[:, b:b + n, :], a[name].rearrange("(b p) i -> p b i", p=P)).then_inc(s_in, 16)

            @block.tensor
            def _(pe):
                pe.wait_ge(s_in, 48)
                for j in range(5):
                    b, t = turn(j, 0)
                    pe.wait_ge(c.bank_free[b], t)
                    for h in range(KH):
                        for n in range(2):
                            ins = nc.tensor.transpose(c.bank[b][:, (2 * h + n) * P:(2 * h + n + 1) * P],
                                                      nat[:, 2 * j + n, h * P:(h + 1) * P], c.ident[:])
                    ins.then_inc(c.bank_full[b], 1)

            @block.scalar
            def _(act):
                for j in range(5):
                    b, t = turn(j, 0)
                    act.wait_ge(c.bank_full[b], t)
                    nc.scalar.copy(wt[:, :, j * D:(j + 1) * D],
                                   c.bank[b][:].rearrange("p (h o) -> p h o", h=KH)).then_inc(c.bank_free[b], 1)


def mix0_sums(nc, c, wt, kv):
    with Phase(nc, "keys0") as ph:
        cut = carver(c.agg)
        stage, er, rr = cut(GT, D), cut(GT, D), cut(GT, D)
        xt = cut(KH, GR)
        v1 = cut(GT, KH, P + 4)
        acc = ph.sb("acc", [P, KH, P + 1])
        (s_bn, s_mv, s_rs, s_tmp, s_nrm, s_xt, s_e, s_v, s_k, s_km, s_used, s_acc, s_copy, s_kvu, s_bd) = ph.sems(
            "partial variance rstd sum normal xt exp_relu values keys keys_masked stage_used accumulated copied kv_used diagonal")
        turn = c.ledger.plan([j % 6 for j in range(4 + GT + 1)], NG)
        with nc.Block() as block:

            @block.vector
            def _(dve):
                v = nc.vector
                v.memset(v1[:], 1.0).then_inc(s_v, 1)
                v.memset(acc[:], 0.0).then_inc(s_acc, 1)
                v.memset(kv[:], 0.0).then_inc(s_bd, 1)
                dve.sem_inc(s_used, 1)
                with dve.Fori(0, NG) as g:
                    stats(dve, c, lambda k: tile_of(c.res, g, k), g, s_bn, s_mv)
                    dve.wait_ge(s_used, g + 1)
                    dve.wait_ge(s_copy, g + 1)
                    normalise(dve, c, lambda k: stage[:, k, :], lambda k: tile_of(c.res, g, k), g, s_rs, s_nrm)
                    for k in range(GT):
                        dve.wait_ge(s_e, g * GT + (k + 1))
                        v.scalar_tensor_tensor(er[:, k, :], er[:, k, :], 1.0, rr[:, k, :], ALU.min, ALU.add).then_inc(s_k, 1)
                    dve.wait_ge(s_k, g * GT + GT)
                    v.tensor_scalar(er[:, GT - 1, :], er[:, GT - 1, :], c.real[:, ds(g * GT + (GT - 1), 1)], None,
                                    ALU.mult).then_inc(s_km, 1)
                    b, t = turn(4 + GT, g)
                    dve.wait_ge(c.bank_full[b], t)
                    dve.wait_ge(s_acc, g + 1)
                    v.tensor_tensor(acc[:], acc[:], c.bank[b][:, 0:KH * (P + 1)].rearrange("p (a m) -> p a m", a=KH),
                                    ALU.add).then_inc(s_acc, 1)
                    dve.wait_ge(s_acc, g + 2)
                    dve.sem_inc(c.bank_free[b], 1)
                dve.wait_ge(s_acc, NG + 1)
                dve.wait_ge(s_bd, 1)
                for j in range(4):
                    r = slice(32 * j, 32 * j + 32)
                    v.tensor_copy(kv[r, :, r], acc[r, :, r]).then_inc(s_bd, 1)
                    v.tensor_copy(kv[r, :, P + j:P + j + 1], acc[r, :, P:P + 1]).then_inc(s_bd, 1)

            @block.gpsimd
            def _(pool):
                with pool.Fori(0, NG) as g:
                    rstd(pool, c, g, s_mv, s_rs, s_tmp)

            @block.scalar
            def _(act):
                act.sem_inc(s_copy, 1)
                act.wait_ge(s_v, 1)
                with act.Fori(0, NG) as g:
                    act.wait_ge(s_nrm, (g + 1) * GT)
                    gate(act, c)
                    nc.scalar.copy(group(c.xn, g), stage[:]).then_inc(s_copy, 1)
                    evacuate_transposed(act, c, xt, turn, 0, g, s_xt)
                    for k in range(GT):
                        b, t = turn(4 + k, g)
                        act.wait_ge(c.bank_full[b], t)
                        act.wait_ge(s_kvu, g + 1)
                        nc.scalar.activation(er[:, k, :], c.bank[b][:, 0:D], ACT.Exp).then_inc(s_v, 1)
                        nc.scalar.activation(rr[:, k, :], c.bank[b][:, 0:D], ACT.Relu).then_inc(s_v, 1)
                        nc.scalar.copy(v1[:, k, :, 0:P], c.bank[b][:, D:2 * D].rearrange("p (a m) -> p a m", a=KH))\
                            .then_inc(s_v, 1)
                        act.wait_ge(s_v, g * (3 * GT) + (3 * k + 4))
                        act.sem_inc(c.bank_free[b], 1)
                        act.sem_inc(s_e, 1)

            @block.tensor
            def _(pe):
                pe.sem_inc(s_kvu, 1)
                with pe.Fori(0, NG) as g:
                    pe.wait_ge(s_nrm, (g + 1) * GT)
                    transposed(pe, c, lambda k, h: stage[:, k, h * P:(h + 1) * P], turn, 0, g)
                    pe.wait_ge(s_xt, g + 1)
                    pe.sem_inc(s_used, 1)
                    for k in range(GT):
                        b, t = turn(4 + k, g)
                        pe.wait_ge(c.bank_free[b], t)
                        for h in range(KH):
                            ins = nc.tensor.matmul(c.bank[b][:], xt[:, h, k * P:(k + 1) * P], wt[:, h, D:3 * D],
                                                   start=(h == 0), stop=(h == KH - 1))
                        ins.then_inc(c.bank_full[b], 1)
                    b, t = turn(4 + GT, g)
                    pe.wait_ge(c.bank_free[b], t)
                    pe.wait_ge(s_km, g + 1)
                    for s in range(KH):
                        for k in range(GT):
                            ins = nc.tensor.matmul(c.bank[b][:, s * (P + 1):(s + 1) * (P + 1)], er[:, k, s * P:(s + 1) * P],
                                                   v1[:, k, s, 0:P + 1], start=(k == 0), stop=(k == GT - 1))
                    ins.then_inc(c.bank_full[b], 1)
                    pe.wait_ge(c.bank_full[b], t)
                    pe.sem_inc(s_kvu, 1)


def mix0_main(nc, c, a, wt, kv):
    with Phase(nc, "mix0") as ph:
        cut = carver(c.agg)
        stage, u = cut(GT, D), cut(GT, D)
        xt, et, rt = cut(KH, GR), cut(KH, GR), cut(KH, GR)
        z = ph.sb("z", [P, GT, KH, 4])
        vec = ph.sb("vec", [P, 5, D])
        b1 = ph.sb("b1", [P, KH])
        (s_in, s_stage, s_xt, s_er, s_q, s_den, s_rec, s_t, s_u, s_bn, s_mv, s_rs, s_tmp, s_nrm, s_gam, s_x1, s_hid, s_b2,
         s_y, s_res, s_out) = ph.sems(
            "vectors_in staged xt exp_relu queries denominators reciprocals attended rows_made partial variance rstd sum "
            "normal gamma first_norm hidden bias_added second_rows beta_added group_done")
        NU = 4 + 4 + GT + 4 + 4 + 4
        turn = c.ledger.plan([j % 8 for j in range(NU)], NG)
        JQ, JT, JX, JH, JY = 4, 8, 8 + GT, 12 + GT, 16 + GT
        with nc.Block() as block:

            @block.sync
            def _(sp):
                for j, n in enumerate(("ln1_g", "ln1_b", "b2", "ln2_g", "ln2_b")):
                    sp.dma_start(vec[:, j, :], spread(a["L0_mix_" + n])).then_inc(s_in, 16)
                sp.dma_start(b1[:], a["L0_mix_b1"].rearrange("(h p) -> p h", p=P),
                             allow_slow_non_contiguous=True).then_inc(s_in, 16)

            @block.tensor
            def _(pe):
                with pe.Fori(0, NG) as g:
                    pe.wait_ge(s_stage, g + 1)
                    transposed(pe, c, lambda k, h: stage[:, k, h * P:(h + 1) * P], turn, 0, g)
                    pe.wait_ge(s_xt, g * 2 + 1)
                    for m in range(KH):
                        for n, (k0, w) in enumerate(CH):
                            b, t = turn(JQ + 2 * m + n, g)
                            pe.wait_ge(c.bank_free[b], t)
                            for h in range(KH):
                                ins = nc.tensor.matmul(c.bank[b][:, 0:w * P], wt[:, h, m * P:(m + 1) * P],
                                                       xt[:, h, k0 * P:(k0 + w) * P], start=(h == 0), stop=(h == KH - 1))
                            ins.then_inc(c.bank_full[b], 1)
                    pe.wait_ge(s_q, g * 4 + 4)
                    for k in range(GT):
                        b, t = turn(JT + k, g)
                        pe.wait_ge(c.bank_free[b], t)
                        for s in range(KH):
                            ins = nc.tensor.matmul(c.bank[b][:, s * (P + 4):(s + 1) * (P + 4)], et[:, s, k * P:(k + 1) * P],
                                                   kv[:, s, :], start=True, stop=True)
                        ins.then_inc(c.bank_full[b], 1)
                    pe.wait_ge(s_x1, g + 1)
                    transposed(pe, c, lambda k, h: u[:, k, h * P:(h + 1) * P], turn, JX, g)
                    pe.wait_ge(s_xt, g * 2 + 2)
                    for m in range(KH):
                        for n, (k0, w) in enumerate(CH):
                            b, t = turn(JH + 2 * m + n, g)
                            pe.wait_ge(c.bank_free[b], t)
                            for h in range(KH):
                                ins = nc.tensor.matmul(c.bank[b][:, 0:w * P], wt[:, h, 3 * D + m * P:3 * D + (m + 1) * P],
                                                       xt[:, h, k0 * P:(k0 + w) * P], start=(h == 0), stop=(h == KH - 1))
                            ins.then_inc(c.bank_full[b], 1)
                    pe.wait_ge(s_hid, g * 4 + 4)
                    for n in range(4):
                        b, t = turn(JY + n, g)
                        pe.wait_ge(c.bank_free[b], t)
                        for k in range(2 * n, min(2 * n + 2, GT)):
                            for h in range(KH):
                                ins = nc.tensor.matmul(c.bank[b][:, (k % 2) * D:(k % 2 + 1) * D], et[:, h, k * P:(k + 1) * P],
                                                       wt[:, h, 4 * D:5 * D], start=(h == 0), stop=(h == KH - 1))
                        ins.then_inc(c.bank_full[b], 1)

            @block.scalar
            def _(act):
                act.wait_ge(s_in, 96)
                with act.Fori(0, NG) as g:
                    act.wait_ge(s_out, g + 1)
                    gate(act, c)
                    nc.scalar.copy(stage[:], group(c.xn, g)).then_inc(s_stage, 1)
                    evacuate_transposed(act, c, xt, turn, 0, g, s_xt)
                    for m in range(KH):
                        for n, (k0, w) in enumerate(CH):
                            b, t = turn(JQ + 2 * m + n, g)
                            r = slice(k0 * P, (k0 + w) * P)
                            act.wait_ge(c.bank_full[b], t)
                            nc.scalar.activation(et[:, m, r], c.bank[b][:, 0:w * P], ACT.Exp).then_inc(s_er, 1)
                            nc.scalar.activation(rt[:, m, r], c.bank[b][:, 0:w * P], ACT.Relu).then_inc(s_er, 1)
                            act.wait_ge(s_er, g * 8 + (4 * m + 2 * n + 2))
                            act.sem_inc(c.bank_free[b], 1)
                    evacuate_transposed(act, c, xt, turn, JX, g, s_xt)
                    for m in range(KH):
                        for n, (k0, w) in enumerate(CH):
                            b, t = turn(JH + 2 * m + n, g)
                            r = slice(k0 * P, (k0 + w) * P)
                            act.wait_ge(c.bank_full[b], t)
                            nc.scalar.activation(et[:, m, r], c.bank[b][:, 0:w * P], ACT.Gelu, bias=b1[:, m:m + 1])\
                                .then_inc(s_hid, 1)
                            act.wait_ge(s_hid, g * 4 + (2 * m + n + 1))
                            act.sem_inc(c.bank_free[b], 1)

            @block.gpsimd
            def _(pool):
                pool.wait_ge(s_in, 96)
                p = nc.gpsimd
                wide = lambda j: vec[:, j:j + 1, :].to_broadcast([P, GT, D])
                with pool.Fori(0, NG) as g:
                    rstd(pool, c, g * 2, s_mv, s_rs, s_tmp)
                    pool.wait_ge(s_nrm, g * (2 * GT) + GT)
                    p.tensor_tensor(u[:], u[:], wide(0), ALU.mult).then_inc(s_gam, 1)
                    gate(pool, c)
                    p.tensor_tensor(group(c.res, g), group(c.res, g), wide(4), ALU.add).then_inc(s_res, 1)
                    pool.wait_ge(s_xt, g * 2 + 2)
                    p.tensor_tensor(u[:], u[:], wide(2), ALU.add).then_inc(s_b2, 1)
                    rstd(pool, c, g * 2 + 1, s_mv, s_rs, s_tmp)
                    pool.wait_ge(s_nrm, g * (2 * GT) + 2 * GT)
                    p.tensor_tensor(u[:], u[:], wide(3), ALU.mult).then_inc(s_gam, 1)

            @block.vector
            def _(dve):
                v = nc.vector
                dve.sem_inc(s_out, 1)
                dve.wait_ge(s_in, 96)
                with dve.Fori(0, NG) as g:
                    for m in range(KH):
                        for n, (k0, w) in enumerate(CH):
                            r = slice(k0 * P, (k0 + w) * P)
                            dve.wait_ge(s_er, g * 8 + (4 * m + 2 * n + 2))
                            v.scalar_tensor_tensor(et[:, m, r], et[:, m, r], 1.0, rt[:, m, r], ALU.min, ALU.add).then_inc(s_q, 1)
                    for k in range(GT):
                        b, t = turn(JT + k, g)
                        dve.wait_ge(c.bank_full[b], t)
                        v.tensor_scalar(z[:, k, :, :], c.bank[b][:, 0:KH * (P + 4)].rearrange("p (s m) -> p s m", s=KH)[:, :, P:],
                                        1e-6, None, ALU.add).then_inc(s_den, 1)
                    dve.wait_ge(s_den, g * GT + GT)
                    v.reciprocal(z[:], z[:]).then_inc(s_rec, 1)
                    dve.wait_ge(s_rec, g + 1)
                    for k in range(GT):
                        b, t = turn(JT + k, g)
                        v.tensor_tensor(u[:, k, :].rearrange("p (s j m) -> p s j m", s=KH, j=4),
                                        c.bank[b][:, 0:KH * (P + 4)].rearrange("p (s m) -> p s m", s=KH)[:, :, 0:P]
                                        .rearrange("p s (j m) -> p s j m", j=4),
                                        z[:, k, :, :].unsqueeze(3).to_broadcast([P, KH, 4, 32]), ALU.mult).then_inc(s_t, 1)
                        dve.wait_ge(s_t, g * GT + (k + 1))
                        dve.sem_inc(c.bank_free[b], 1)
                    v.tensor_tensor(u[:], u[:], stage[:], ALU.add).then_inc(s_u, 1)
                    dve.wait_ge(s_u, g + 1)
                    gate(dve, c)
                    tile = lambda k: u[:, k, :]
                    stats(dve, c, tile, g * 2, s_bn, s_mv)
                    normalise(dve, c, tile, tile, g * 2, s_rs, s_nrm)
                    dve.wait_ge(s_gam, g * 2 + 1)
                    v.tensor_tensor(u[:], u[:], vec[:, 1:2, :].to_broadcast([P, GT, D]), ALU.add).then_inc(s_x1, 1)
                    dve.wait_ge(s_b2, g + 1)
                    for n in range(4):
                        b, t = turn(JY + n, g)
                        w = min(2, GT - 2 * n)
                        dve.wait_ge(c.bank_full[b], t)
                        x = u[:, 2 * n:2 * n + w, :].rearrange("p k c -> p (k c)")
                        v.tensor_tensor(x, x, c.bank[b][:, 0:w * D], ALU.add).then_inc(s_y, 1)
                        dve.wait_ge(s_y, g * 4 + (n + 1))
                        dve.sem_inc(c.bank_free[b], 1)
                    stats(dve, c, tile, g * 2 + 1, s_bn, s_mv)
                    normalise(dve, c, tile, tile, g * 2 + 1, s_rs, s_nrm)
                    dve.wait_ge(s_gam, g * 2 + 2)
                    dve.wait_ge(s_res, g + 1)
                    gate(dve, c)
                    v.tensor_tensor(group(c.res, g), group(c.res, g), u[:], ALU.add).then_inc(s_out, 1)


class Mlp:
    NU = 4 + 16 + 4
    BANKS = [j % 8 for j in range(NU)]

    def __init__(self, nc, c, ph, turn, stage, cut, w1, w2, b1, act_fn):
        self.nc, self.c, self.turn, self.stage, self.w1, self.w2, self.b1, self.fn = nc, c, turn, stage, w1, w2, b1, act_fn
        self.xt = cut(KH, GR)
        self.ht = [cut(8, w * P) for _, w in CH]
        self.s_xt, self.s_hid, self.s_used = ph.sems("mlp_xt mlp_hidden mlp_hidden_used")

    def tensor(self, pe, g):
        nc, c, turn = self.nc, self.c, self.turn
        transposed(pe, c, lambda k, h: self.stage[:, k, h * P:(h + 1) * P], turn, 0, g)
        pe.wait_ge(self.s_xt, g + 1)
        for n, (k0, w) in enumerate(CH):
            for m in range(8):
                b, t = turn(4 + 8 * n + m, g)
                pe.wait_ge(c.bank_free[b], t)
                for h in range(KH):
                    ins = nc.tensor.matmul(c.bank[b][:, 0:w * P], self.w1[:, h, m * P:(m + 1) * P],
                                           self.xt[:, h, k0 * P:(k0 + w) * P], start=(h == 0), stop=(h == KH - 1))
                ins.then_inc(c.bank_full[b], 1)
        for n, (k0, w) in enumerate(CH):
            pe.wait_ge(self.s_hid, g * 16 + (8 * n + 8))
            for r in range(2):
                b, t = turn(20 + 2 * n + r, g)
                pe.wait_ge(c.bank_free[b], t)
                for k in range(2 * r, min(2 * r + 2, w)):
                    for m in range(8):
                        ins = nc.tensor.matmul(c.bank[b][:, (k % 2) * D:(k % 2 + 1) * D], self.ht[n][:, m, k * P:(k + 1) * P],
                                               self.w2[:, m, :], start=(m == 0), stop=(m == 7))
                ins.then_inc(c.bank_full[b], 1)
        pe.wait_ge(c.bank_full[b], t)
        pe.sem_inc(self.s_used, 1)

    def scalar(self, act, g):
        nc, c, turn = self.nc, self.c, self.turn
        act.wait_ge(self.s_used, g + 1)
        evacuate_transposed(act, c, self.xt, turn, 0, g, self.s_xt)
        for n, (k0, w) in enumerate(CH):
            for m in range(8):
                b, t = turn(4 + 8 * n + m, g)
                act.wait_ge(c.bank_full[b], t)
                nc.scalar.activation(self.ht[n][:, m, :], c.bank[b][:, 0:w * P], self.fn, bias=self.b1[:, m:m + 1])\
                    .then_inc(self.s_hid, 1)
                act.wait_ge(self.s_hid, g * 16 + (8 * n + m + 1))
                act.sem_inc(c.bank_free[b], 1)

    def pairs(self):
        return [(20 + 2 * n + r, k0 + 2 * r, min(2, w - 2 * r)) for n, (k0, w) in enumerate(CH) for r in range(2)]


def ffn0(nc, c, a, score):
    with Phase(nc, "ffn0") as ph:
        cut = carver(c.agg)
        stage, junk = cut(GT, D), cut(D)
        w1, w2, b1 = ph.sb("w1", [P, KH, 4 * D]), ph.sb("w2", [P, 8, D]), ph.sb("b1", [P, 8])
        vec, br, sc = ph.sb("vec", [P, 2, D]), ph.sb("br", [P, 1]), ph.sb("sc", [P, GT])
        turn = c.ledger.plan(Mlp.BANKS, NG)
        mlp = Mlp(nc, c, ph, turn, stage, cut, w1, w2, b1, ACT.Gelu_apprx_tanh)
        s_in, s_x1, s_bn, s_mv, s_rs, s_tmp, s_nrm, s_sc, s_scb, s_base, s_yb, s_y = ph.sems(
            "weights_in sum_made partial variance rstd sum normal score score_biased base_made y_biased y_scaled")
        with nc.Block() as block:

            @block.sync
            def _(sp):
                for h in range(KH):
                    sp.dma_start(w1[:, h, :], a["L0_ffn_w1"][h * P:(h + 1) * P, :]).then_inc(s_in, 16)
                sp.dma_start(w2[:], a["L0_ffn_w2"].rearrange("(m p) o -> p m o", p=P)).then_inc(s_in, 16)
                sp.dma_start(b1[:], a["L0_ffn_b1"].rearrange("(m p) -> p m", p=P), allow_slow_non_contiguous=True).then_inc(s_in, 16)
                sp.dma_start(vec[:, 0, :], a["L0_ffn_wr"].rearrange("d o -> o d").to_broadcast([P, D]),
                             allow_slow_non_contiguous=True).then_inc(s_in, 16)
                sp.dma_start(vec[:, 1, :], spread(a["L0_ffn_b2"])).then_inc(s_in, 16)
                sp.dma_start(br[:], spread(a["L0_ffn_br"], 1)).then_inc(s_in, 16)

            @block.tensor
            def _(pe):
                pe.sem_inc(mlp.s_used, 1)
                pe.wait_ge(s_in, 7 * 16)
                with pe.Fori(0, NG) as g:
                    pe.wait_ge(s_nrm, (g + 1) * GT)
                    mlp.tensor(pe, g)

            @block.scalar
            def _(act):
                act.wait_ge(s_in, 7 * 16)
                with act.Fori(0, NG) as g:
                    mlp.scalar(act, g)

            @block.gpsimd
            def _(pool):
                with pool.Fori(0, NG) as g:
                    rstd(pool, c, g, s_mv, s_rs, s_tmp)

            @block.vector
            def _(dve):
                v = nc.vector
                dve.wait_ge(s_in, 7 * 16)
                with dve.Fori(0, NG) as g:
                    v.tensor_tensor(group(c.res, g), group(c.res, g), group(c.xn, g), ALU.add).then_inc(s_x1, 1)
                    dve.wait_ge(s_x1, g + 1)
                    gate(dve, c)
                    stats(dve, c, lambda k: tile_of(c.res, g, k), g, s_bn, s_mv)
                    normalise(dve, c, lambda k: stage[:, k, :], lambda k: tile_of(c.res, g, k), g, s_rs, s_nrm)
                    dve.wait_ge(s_nrm, (g + 1) * GT)
                    for k in range(GT):
                        if k:
                            dve.wait_ge(s_sc, g * GT + k)
                        v.tensor_tensor_reduce(junk, stage[:, k, :], vec[:, 0, :], 1.0, 0.0, ALU.mult, ALU.add,
                                               sc[:, k:k + 1]).then_inc(s_sc, 1)
                    dve.wait_ge(s_sc, g * GT + GT)
                    v.tensor_scalar(sc[:], sc[:], br[:, 0:1], None, ALU.add).then_inc(s_scb, 1)
                    dve.wait_ge(s_scb, g * 2 + 1)
                    v.tensor_scalar(score[:, ds(g * GT, GT)], sc[:], 1.0, None, ALU.mult).then_inc(s_scb, 1)
                    v.tensor_tensor(group(c.res, g), group(c.res, g), stage[:], ALU.add).then_inc(s_base, 1)
                    dve.wait_ge(s_base, g + 1)
                    for n, (j, k, w) in enumerate(mlp.pairs()):
                        b, t = turn(j, g)
                        dve.wait_ge(c.bank_full[b], t)
                        v.tensor_tensor(stage[:, k:k + w, :], c.bank[b][:, 0:w * D].rearrange("p (k d) -> p k d", d=D),
                                        vec[:, 1:2, :].to_broadcast([P, w, D]), ALU.add).then_inc(s_yb, 1)
                        dve.wait_ge(s_yb, g * 4 + (n + 1))
                        dve.sem_inc(c.bank_free[b], 1)
                        for i in range(k, k + w):
                            v.tensor_scalar(tile_of(c.xn, g, i), stage[:, i, :], sc[:, i:i + 1], None, ALU.mult).then_inc(s_y, 1)
                    dve.wait_ge(s_y, (g + 1) * GT)
                    gate(dve, c)


def select(nc, c, score, take):
    ROUNDS = 64
    with Phase(nc, "select") as ph:
        lo, hi, mid, cnt, up, dn, top = (ph.sb(n, [P, 1]) for n in ("lo", "hi", "mid", "cnt", "up", "dn", "top"))
        junk, above, equal, off, off2, lim = (ph.sb(n, [P, NT]) for n in ("junk", "above", "equal", "off", "off2", "lim"))
        before = ph.sb("before", [P, P])
        s_v, s_max, s_cnt, s_tot = ph.sems("vector_steps maximum counted totalled")
        s_hi, s_lo, s_mid, s_ud = ph.sems("high low middle up_down")
        s_rank, = ph.sems("ranked")
        turn = c.ledger.plan([0, 1], 1)
        with nc.Block() as block:

            @block.gpsimd
            def _(pool):
                pool.wait_ge(s_v, 2)
                nc.gpsimd.partition_all_reduce(hi[:], top[:], P, bass.bass_isa.ReduceOp.max).then_inc(s_max, 1)

            @block.tensor
            def _(pe):
                with pe.Fori(0, ROUNDS) as i:
                    pe.wait_ge(s_cnt, i + 1)
                    nc.tensor.matmul(c.bank[2][:, 0:1], c.ones[:], cnt[:], start=True, stop=True).then_inc(s_tot, 1)
                pe.wait_ge(s_rank, 1)
                nc.tensor.matmul(c.bank[0][:, 0:NT], before[:], equal[:], start=True, stop=True)
                nc.tensor.matmul(c.bank[0][:, 64:64 + NT], c.ones[:], equal[:], start=True, stop=True)
                nc.tensor.matmul(c.bank[0][:, 128:129], c.ones[:], cnt[:], start=True, stop=True).then_inc(c.bank_full[0], 1)

            @block.vector
            def _(dve):
                v = nc.vector
                done = [0]

                def then(ins):
                    done[0] += 1
                    ins.then_inc(s_v, 1)
                    dve.wait_ge(s_v, done[0])

                then(v.tensor_tensor(junk[:], score[:], c.real[:], ALU.mult))
                then(v.tensor_reduce(top[:], junk[:], AX.X, ALU.max, apply_absolute_value=True))
                then(v.tensor_scalar(off[:], c.real[:], -1.0, BIG, ALU.add, ALU.mult))
                then(v.tensor_tensor(score[:], junk[:], off[:], ALU.add))
                then(v.tensor_scalar(before[:], c.iota[:], c.row_no[:, 0:1], None, ALU.is_gt))
                dve.wait_ge(s_max, 1)
                then(v.tensor_scalar(lo[:], hi[:], -1.0, None, ALU.mult))
                then(v.tensor_scalar(hi[:], hi[:], 1.0001, 1e-30, ALU.mult, ALU.add))
                dve.sem_inc(s_hi, 1)
                dve.sem_inc(s_lo, 1)
                with dve.Fori(0, ROUNDS) as i:
                    dve.wait_ge(s_hi, i + 1)
                    dve.wait_ge(s_lo, i + 1)
                    v.tensor_scalar(mid[:], lo[:], hi[:, 0:1], 0.5, ALU.add, ALU.mult).then_inc(s_mid, 1)
                    dve.wait_ge(s_mid, i + 1)
                    v.tensor_scalar(junk[:], score[:], mid[:, 0:1], 0.0, ALU.is_ge, ALU.add, accum_out=cnt[:]).then_inc(s_cnt, 1)
                    dve.wait_ge(s_tot, i + 1)
                    v.tensor_scalar(up[:], c.bank[2][:, 0:1], float(KK), BIG, ALU.is_ge, ALU.mult).then_inc(s_ud, 1)
                    v.tensor_scalar(dn[:], c.bank[2][:, 0:1], float(KK), -BIG, ALU.is_lt, ALU.mult).then_inc(s_ud, 1)
                    dve.wait_ge(s_ud, i * 2 + 2)
                    v.scalar_tensor_tensor(hi[:], up[:], mid[:, 0:1], hi[:], ALU.add, ALU.min).then_inc(s_hi, 1)
                    v.scalar_tensor_tensor(lo[:], dn[:], mid[:, 0:1], lo[:], ALU.add, ALU.max).then_inc(s_lo, 1)
                dve.wait_ge(s_hi, ROUNDS + 1)
                dve.wait_ge(s_lo, ROUNDS + 1)
                then(v.tensor_scalar(above[:], score[:], hi[:, 0:1], 0.0, ALU.is_ge, ALU.add, accum_out=cnt[:]))
                then(v.tensor_scalar(equal[:], score[:], lo[:, 0:1], None, ALU.is_ge))
                v.tensor_tensor(equal[:], equal[:], above[:], ALU.subtract).then_inc(s_rank, 1)
                dve.wait_ge(c.bank_full[0], turn(0, 0)[1])
                then(v.tensor_copy(off[:], c.bank[0][:, 64:64 + NT]))
                x, y, s = off, off2, 1
                while s < NT:
                    then(v.tensor_copy(y[:, 0:s], x[:, 0:s]))
                    then(v.tensor_tensor(y[:, s:NT], x[:, s:NT], x[:, 0:NT - s], ALU.add))
                    x, y, s = y, x, 2 * s
                then(v.tensor_tensor(x[:], x[:], c.bank[0][:, 64:64 + NT], ALU.subtract))
                then(v.tensor_tensor(x[:], x[:], c.bank[0][:, 0:NT], ALU.add))
                then(v.tensor_scalar(x[:], x[:], c.bank[0][:, 128:129], float(KK), ALU.add, ALU.is_lt))
                then(v.tensor_tensor(x[:], x[:], equal[:], ALU.mult))
                then(v.tensor_tensor(take[:], x[:], above[:], ALU.add))
                dve.sem_inc(c.bank_free[0], 1)
                dve.sem_inc(c.bank_free[1], 1)
                dve.sem_inc(c.bank_full[1], 1)


def weights1(nc, c, a, wt, wq):
    nat = c.agg[:, 0:6 * D].rearrange("p (b i) -> p b i", i=D)
    with Phase(nc, "weights1") as ph:
        s_in, = ph.sems("natural_in")
        turn = c.ledger.plan([0, 1, 2], 1)
        with nc.Block() as block:

            @block.sync
            def _(sp):
                for j, n in enumerate(("wk", "wv", "wo")):
                    sp.dma_start(nat[:, 2 * j:2 * j + 2, :], a["L1_mix_" + n].rearrange("(b p) i -> p b i", p=P)).then_inc(s_in, 16)
                sp.dma_start(wq[:], a["L1_mix_wq"].rearrange("(b p) i -> p b i", p=P)).then_inc(s_in, 16)

            @block.tensor
            def _(pe):
                pe.wait_ge(s_in, 64)
                for j in range(3):
                    b, t = turn(j, 0)
                    pe.wait_ge(c.bank_free[b], t)
                    for h in range(KH):
                        for n in range(2):
                            ins = nc.tensor.transpose(c.bank[b][:, (2 * h + n) * P:(2 * h + n + 1) * P],
                                                      nat[:, 2 * j + n, h * P:(h + 1) * P], c.ident[:])
                    ins.then_inc(c.bank_full[b], 1)

            @block.scalar
            def _(act):
                for j in range(3):
                    b, t = turn(j, 0)
                    act.wait_ge(c.bank_full[b], t)
                    nc.scalar.copy(wt[:, :, j * D:(j + 1) * D],
                                   c.bank[b][:].rearrange("p (h o) -> p h o", h=KH)).then_inc(c.bank_free[b], 1)


def mix1_matrix(nc, c, a, take, wt, wq, mx):
    HD, NH = 64, 8
    with Phase(nc, "keys1") as ph:
        cut = carver(c.agg)
        stage, kvb = cut(GT, D), cut(GT * NH, HD)
        xt = cut(KH, GR)
        bnk, mvk, vek, rsk = cut(GT * NH, 6), cut(GT * NH, 2), cut(GT * NH), cut(GT * NH)
        eps, power = cut(GT * NH), cut(GT * NH)
        acc, t1, bd = cut(4 * P + 2), cut(KH, D), cut(KH, P)
        gk, bk, gv = cut(P), cut(P), ph.sb("gv", [P, 2])
        s1, s2 = cut(P), cut(P)
        (s_in, s_x2, s_bn, s_mv, s_rs, s_tmp, s_nrm, s_copy, s_xt, s_kv, s_kst, s_kmv, s_krs, s_kmm, s_hat, s_acc, s_kvu,
         s_v, s_m, s_set) = ph.sems("vectors_in x_made partial variance rstd sum normal copied xt kv_out kv_partial kv_variance "
                             "kv_rstd kv_steps kv_normal accumulated kv_used vector_steps products set")
        turn = c.ledger.plan([j % 7 for j in range(4 + GT + 2)], NG)
        tail = c.ledger.plan([0, 1], 1)
        with nc.Block() as block:

            @block.sync
            def _(sp):
                for h in range(2):
                    r = slice(h * HD, (h + 1) * HD)
                    sp.dma_start(gk[:, r], spread(a["L1_mix_ln_k_g"], HD)).then_inc(s_in, 16)
                    sp.dma_start(bk[:, r], spread(a["L1_mix_ln_k_b"], HD)).then_inc(s_in, 16)
                    for j, n in enumerate(("g", "b")):
                        sp.dma_start(gv[r, j:j + 1], a["L1_mix_ln_v_" + n].rearrange("(p a) -> p a", a=1)).then_inc(s_in, 16)

            @block.vector
            def _(dve):
                v = nc.vector
                v.memset(acc, 0.0).then_inc(s_acc, 1)
                v.memset(eps, EPS).then_inc(s_set, 1)
                v.memset(power, -0.5).then_inc(s_set, 1)
                with dve.Fori(0, NG) as g:
                    for k in range(GT):
                        v.scalar_tensor_tensor(tile_of(c.res, g, k), tile_of(c.xn, g, k), take[:, ds(g * GT + k, 1)],
                                               tile_of(c.res, g, k), ALU.mult, ALU.add).then_inc(s_x2, 1)
                    dve.wait_ge(s_x2, (g + 1) * GT)
                    gate(dve, c)
                    stats(dve, c, lambda k: tile_of(c.res, g, k), g, s_bn, s_mv)
                    dve.wait_ge(s_copy, g + 1)
                    dve.wait_ge(s_xt, g + 1)
                    normalise(dve, c, lambda k: stage[:, k, :], lambda k: tile_of(c.res, g, k), g, s_rs, s_nrm)
                    for k in range(GT):
                        dve.wait_ge(s_kv, g * GT + (k + 1))
                        for i in range(NH):
                            v.bn_stats(bnk[:, k * NH + i, :], kvb[:, k * NH + i, :]).then_inc(s_kst, 1)
                    dve.wait_ge(s_kst, (g + 1) * (GT * NH))
                    gate(dve, c)
                    for i in range(GT * NH):
                        v.bn_aggr(mvk[:, i, :], bnk[:, i, :]).then_inc(s_kmv, 1)
                    dve.wait_ge(s_kmv, (g + 1) * (GT * NH))
                    v.tensor_tensor(kvb, kvb, mvk[:, :, 0].unsqueeze(2).to_broadcast([P, GT * NH, HD]), ALU.subtract)\
                        .then_inc(s_hat, 1)
                    dve.wait_ge(s_krs, g + 1)
                    dve.wait_ge(s_hat, g * 2 + 1)
                    v.tensor_tensor(kvb, kvb, rsk.unsqueeze(2).to_broadcast([P, GT * NH, HD]), ALU.mult).then_inc(s_hat, 1)
                    for n, (to, w) in enumerate(((0, D + 2), (D + 2, D))):
                        b, t = turn(4 + GT + n, g)
                        dve.wait_ge(c.bank_full[b], t)
                        dve.wait_ge(s_acc, g * 2 + (n + 1))
                        v.tensor_tensor(acc[:, to:to + w], acc[:, to:to + w], c.bank[b][:, 0:w], ALU.add).then_inc(s_acc, 1)
                        dve.wait_ge(s_acc, g * 2 + (n + 2))
                        dve.sem_inc(c.bank_free[b], 1)
                done = [0]

                def then(ins):
                    done[0] += 1
                    ins.then_inc(s_v, 1)
                    dve.wait_ge(s_v, done[0])

                dve.wait_ge(s_in, 8 * 16)
                then(v.memset(bd, 0.0))
                for s in range(KH):
                    then(v.tensor_tensor(s1, acc[:, s * P:(s + 1) * P], gk, ALU.mult))
                    then(v.scalar_tensor_tensor(s1, bk, acc[:, D + s:D + s + 1], s1, ALU.mult, ALU.add))
                    then(v.tensor_tensor(s2, acc[:, D + 2 + s * P:D + 2 + (s + 1) * P], gk, ALU.mult))
                    then(v.scalar_tensor_tensor(s2, bk, float(N), s2, ALU.mult, ALU.add))
                    then(v.tensor_scalar(s1, s1, gv[:, 0:1], 1.0 / N, ALU.mult, ALU.mult))
                    then(v.tensor_scalar(s2, s2, gv[:, 1:2], 1.0 / N, ALU.mult, ALU.mult))
                    then(v.tensor_tensor(s1, s1, s2, ALU.add))
                    for j in range(2):
                        r = slice(j * HD, (j + 1) * HD)
                        then(v.tensor_copy(bd[r, s, r], s1[r, r]))
                dve.sem_inc(s_m, 1)
                b, t = tail(0, 0)
                dve.wait_ge(c.bank_full[b], t)
                then(v.tensor_copy(t1.rearrange("p s o -> p (s o)"), c.bank[b][:]))
                dve.sem_inc(c.bank_free[b], 1)
                dve.sem_inc(s_m, 1)
                b, t = tail(1, 0)
                dve.wait_ge(c.bank_full[b], t)
                then(v.tensor_copy(mx[:].rearrange("p s o -> p (s o)"), c.bank[b][:]))
                dve.sem_inc(c.bank_free[b], 1)

            @block.gpsimd
            def _(pool):
                p = nc.gpsimd
                pool.wait_ge(s_set, 2)
                with pool.Fori(0, NG) as g:
                    rstd(pool, c, g, s_mv, s_rs, s_tmp)
                    pool.wait_ge(s_kmv, (g + 1) * (GT * NH))
                    p.tensor_tensor(vek, mvk[:, :, 1], eps, ALU.add).then_inc(s_kmm, 1)
                    pool.wait_ge(s_kmm, g * 2 + 1)
                    p.tensor_tensor(vek, vek, power, ALU.pow).then_inc(s_kmm, 1)
                    pool.wait_ge(s_kmm, g * 2 + 2)
                    gate(pool, c)
                    p.tensor_tensor(rsk.rearrange("p (k i) -> p k i", k=GT), vek.rearrange("p (k i) -> p k i", k=GT),
                                    c.real[:, ds(g * GT, GT)].unsqueeze(2).to_broadcast([P, GT, NH]), ALU.mult).then_inc(s_krs, 1)

            @block.scalar
            def _(act):
                act.sem_inc(s_copy, 1)
                act.sem_inc(s_xt, 1)
                with act.Fori(0, NG) as g:
                    act.wait_ge(s_nrm, (g + 1) * GT)
                    gate(act, c)
                    nc.scalar.copy(group(c.xn, g), stage).then_inc(s_copy, 1)
                    evacuate_transposed(act, c, xt, turn, 0, g, s_xt)
                    act.wait_ge(s_kvu, g + 1)
                    for k in range(GT):
                        b, t = turn(4 + k, g)
                        act.wait_ge(c.bank_full[b], t)
                        nc.scalar.copy(kvb[:, k * NH:(k + 1) * NH, :].rearrange("p i e -> p (i e)"), c.bank[b][:]).then_inc(s_kv, 1)
                        act.wait_ge(s_kv, g * GT + (k + 1))
                        act.sem_inc(c.bank_free[b], 1)

            @block.tensor
            def _(pe):
                pe.sem_inc(s_kvu, 1)
                flat = kvb.rearrange("p (k i) e -> p k (i e)", k=GT)
                with pe.Fori(0, NG) as g:
                    pe.wait_ge(s_nrm, (g + 1) * GT)
                    transposed(pe, c, lambda k, h: stage[:, k, h * P:(h + 1) * P], turn, 0, g)
                    pe.wait_ge(s_xt, g + 2)
                    for k in range(GT):
                        b, t = turn(4 + k, g)
                        pe.wait_ge(c.bank_free[b], t)
                        for h in range(KH):
                            ins = nc.tensor.matmul(c.bank[b][:], xt[:, h, k * P:(k + 1) * P], wt[:, h, 0:2 * D],
                                                   start=(h == 0), stop=(h == KH - 1))
                        ins.then_inc(c.bank_full[b], 1)
                    pe.wait_ge(s_hat, g * 2 + 2)
                    b, t = turn(4 + GT, g)
                    pe.wait_ge(c.bank_free[b], t)
                    for s in range(KH):
                        for k in range(GT):
                            nc.tensor.matmul(c.bank[b][:, s * P:(s + 1) * P], flat[:, k, D + s * P:D + (s + 1) * P],
                                             flat[:, k, s * P:(s + 1) * P], start=(k == 0), stop=(k == GT - 1))
                    for s in range(KH):
                        for k in range(GT):
                            ins = nc.tensor.matmul(c.bank[b][:, D + s:D + s + 1], flat[:, k, D + s * P:D + (s + 1) * P],
                                                   c.ones[:, 0:1], start=(k == 0), stop=(k == GT - 1))
                    ins.then_inc(c.bank_full[b], 1)
                    b, t = turn(5 + GT, g)
                    pe.wait_ge(c.bank_free[b], t)
                    for k in range(GT):
                        ins = nc.tensor.matmul(c.bank[b][:, 0:D], c.ones[:], flat[:, k, 0:D], start=(k == 0), stop=(k == GT - 1))
                    ins.then_inc(c.bank_full[b], 1)
                    pe.wait_ge(c.bank_full[b], t)
                    pe.sem_inc(s_kvu, 1)
                pe.wait_ge(s_m, 1)
                b, t = tail(0, 0)
                pe.wait_ge(c.bank_free[b], t)
                for s in range(KH):
                    ins = nc.tensor.matmul(c.bank[b][:, s * D:(s + 1) * D], bd[:, s, :], wt[:, s, 2 * D:3 * D], start=True, stop=True)
                ins.then_inc(c.bank_full[b], 1)
                pe.wait_ge(s_m, 2)
                b, t = tail(1, 0)
                pe.wait_ge(c.bank_free[b], t)
                for h in range(KH):
                    for s in range(KH):
                        ins = nc.tensor.matmul(c.bank[b][:, h * D:(h + 1) * D], wq[:, s, h * P:(h + 1) * P], t1[:, s, :],
                                               start=(s == 0), stop=(s == KH - 1))
                ins.then_inc(c.bank_full[b], 1)


def tables1(nc, c, a):
    W = a["L1_gnn_weight"]
    with Phase(nc, "tables1") as ph:
        cut = carver(c.agg)
        stage, xt, outs = cut(GT, D), cut(KH, GR), cut(4, 4 * D)
        w = ph.sb("w", [P, KH, REL1 * D])
        s_in, s_stage, s_xt, s_half = ph.sems("weights_in staged xt halves_made")
        s_half2, s_xtu = ph.sems("other_halves_made xt_used")
        s_store = [ph.sem(f"stored{o}") for o in range(4)]
        turn = c.ledger.plan([j % 8 for j in range(4 + 4 * GT)], NG)
        per = [4, 4, 3, 3]
        with nc.Block() as block:

            @block.sync
            def _(sp):
                for h in range(KH):
                    sp.dma_start(w[:, h, :].rearrange("p (r o) -> p r o", r=REL1),
                                 W[:, h * P:(h + 1) * P, :].rearrange("r p o -> p r o")).then_inc(s_in, 16)
                for o in range(4):
                    sp.sem_inc(s_store[o], 16)
                tab = c.tab1_d.rearrange("(r n) d -> n r d", n=NP)
                with sp.Fori(0, NG) as g:
                    for k in range(GT):
                        at = ds(g * GR + k * P, P)
                        for half, s in ((0, s_half), (1, s_half2)):
                            o = (k % 2) * 2 + half
                            sp.wait_ge(s, g * (2 * GT) + (2 * k + 2))
                            sp.dma_start(tab[at, 4 * half:4 * half + 4, :], outs[:, o, :].rearrange("p (r d) -> p r d", d=D))\
                                .then_inc(s_store[o], 16)
                for o in range(4):
                    sp.wait_ge(s_store[o], 16 + 16 * NG * per[o])

            @block.tensor
            def _(pe):
                pe.sem_inc(s_xtu, 1)
                pe.wait_ge(s_in, 32)
                with pe.Fori(0, NG) as g:
                    pe.wait_ge(s_stage, g + 1)
                    transposed(pe, c, lambda k, h: stage[:, k, h * P:(h + 1) * P], turn, 0, g)
                    pe.wait_ge(s_xt, g + 1)
                    for k in range(GT):
                        for j in range(4):
                            b, t = turn(4 + 4 * k + j, g)
                            pe.wait_ge(c.bank_free[b], t)
                            for h in range(KH):
                                ins = nc.tensor.matmul(c.bank[b][:], xt[:, h, k * P:(k + 1) * P], w[:, h, j * 512:(j + 1) * 512],
                                                       start=(h == 0), stop=(h == KH - 1))
                            ins.then_inc(c.bank_full[b], 1)
                    pe.wait_ge(c.bank_full[b], t)
                    pe.sem_inc(s_xtu, 1)

            def out(eng, copy, g, k, j, s):
                b, t = turn(4 + 4 * k + j, g)
                o = (k % 2) * 2 + j // 2
                if j % 2 == 0:
                    eng.wait_ge(s_store[o], (g * per[o] + k // 2 + 1) * 16)
                eng.wait_ge(c.bank_full[b], t)
                copy(outs[:, o, (j % 2) * 512:(j % 2 + 1) * 512], c.bank[b][:]).then_inc(s, 1)
                eng.wait_ge(s, g * (2 * GT) + (2 * k + j % 2 + 1))
                eng.sem_inc(c.bank_free[b], 1)

            @block.scalar
            def _(act):
                with act.Fori(0, NG) as g:
                    act.wait_ge(s_xtu, g + 1)
                    gate(act, c)
                    nc.scalar.copy(stage, group(c.xn, g)).then_inc(s_stage, 1)
                    evacuate_transposed(act, c, xt, turn, 0, g, s_xt)
                    for k in range(GT):
                        for j in range(2):
                            out(act, nc.scalar.copy, g, k, j, s_half)

            @block.vector
            def _(dve):
                with dve.Fori(0, NG) as g:
                    for k in range(GT):
                        for j in range(2, 4):
                            out(dve, nc.vector.tensor_copy, g, k, j, s_half2)


def gnn1(nc, c):
    with Phase(nc, "gnn1") as ph:
        msg, hot, row_ring, meta_ring, row8 = (ph.sb(n, s, d) for n, s, d in (
            ("msg", [P, SLOTS, D], F32), ("hot", [P, SLOTS, P], F32), ("row_ring", [P, 2, HALF], I32),
            ("meta_ring", [P, 2, HALF, 2], F32), ("row8", [P, SB * P], I32)))
        edges = c.edges
        edges.use(msg, hot, row_ring, meta_ring, row8, c.tab1_d, False)
        s_in, s_zero, s_agg = ph.sems("rows_in cleared sums_cleared")
        n0 = DEPTH * BODIES
        with nc.Block() as block:

            @block.sync
            def _(sp):
                sp.dma_start(row8[:], c.row8_d).then_inc(s_in, 16)

            @block.tensor
            def _(pe):
                with pe.Fori(0, BODIES) as i:
                    edges.tensor(pe, i + n0)

            @block.scalar
            def _(act):
                act.wait_ge(s_in, 16)
                gate(act, c)
                with act.Fori(0, BODIES) as i:
                    edges.scalar(act, i, i + n0)

            @block.gpsimd
            def _(pool):
                nc.gpsimd.memset(msg[:], 0.0).then_inc(s_zero, 1)
                pool.wait_ge(s_zero, 1)
                gate(pool, c)
                with pool.Fori(0, BODIES) as i:
                    edges.gpsimd(pool, i + n0)

            @block.vector
            def _(dve):
                nc.vector.memset(c.agg[:], 0.0).then_inc(s_agg, 1)
                dve.wait_ge(s_agg, 1)
                gate(dve, c)
                with dve.Fori(0, BODIES) as i:
                    edges.vector(dve, i, i + n0)


def batch_norm(nc, c, a, scale):
    with Phase(nc, "batch") as ph:
        sq = ph.sb("sq", [P, GT, D])
        acc, mean, gam, eps, power = (ph.sb(n, [P, D]) for n in ("acc", "mean", "gam", "eps", "power"))
        s_in, s_acc, s_v, s_cen, s_msk, s_sq, s_squ, s_p, s_mean = ph.sems(
            "gamma_in accumulated vector_steps centred masked squares squares_used pool_steps mean_made")
        turn = c.ledger.plan([0], NG)
        turn2 = c.ledger.plan([1], NG)
        with nc.Block() as block:

            @block.sync
            def _(sp):
                sp.dma_start(gam[:], spread(a["L1_gnn_gamma"])).then_inc(s_in, 16)

            @block.tensor
            def _(pe):
                pe.sem_inc(s_squ, 1)
                with pe.Fori(0, NG) as g:
                    b, t = turn(0, g)
                    pe.wait_ge(c.bank_free[b], t)
                    gate(pe, c)
                    for k in range(GT):
                        ins = nc.tensor.matmul(c.bank[b][:, 0:D], c.ones[:], tile_of(c.agg, g, k), start=(k == 0), stop=(k == GT - 1))
                    ins.then_inc(c.bank_full[b], 1)
                with pe.Fori(0, NG) as g:
                    b, t = turn2(0, g)
                    pe.wait_ge(c.bank_free[b], t)
                    pe.wait_ge(s_sq, g + 1)
                    for k in range(GT):
                        ins = nc.tensor.matmul(c.bank[b][:, 0:D], c.ones[:], sq[:, k, :], start=(k == 0), stop=(k == GT - 1))
                    ins.then_inc(c.bank_full[b], 1)
                    pe.wait_ge(c.bank_full[b], t)
                    pe.sem_inc(s_squ, 1)

            @block.scalar
            def _(act):
                with act.Fori(0, NG) as g:
                    act.wait_ge(s_msk, g + 1)
                    act.wait_ge(s_squ, g + 1)
                    gate(act, c)
                    nc.scalar.activation(sq[:], group(c.agg, g), ACT.Square).then_inc(s_sq, 1)

            @block.vector
            def _(dve):
                v = nc.vector
                v.memset(acc[:], 0.0).then_inc(s_acc, 1)
                v.memset(eps[:], EPS).then_inc(s_v, 1)
                v.memset(power[:], -0.5).then_inc(s_v, 1)

                def add_up(turn_, g, n):
                    b, t = turn_(0, g)
                    dve.wait_ge(c.bank_full[b], t)
                    dve.wait_ge(s_acc, g + n)
                    v.tensor_tensor(acc[:], acc[:], c.bank[b][:, 0:D], ALU.add).then_inc(s_acc, 1)
                    dve.wait_ge(s_acc, g + (n + 1))
                    dve.sem_inc(c.bank_free[b], 1)

                with dve.Fori(0, NG) as g:
                    add_up(turn, g, 1)
                v.tensor_scalar(mean[:], acc[:], 1.0 / N, None, ALU.mult).then_inc(s_mean, 1)
                dve.wait_ge(s_mean, 1)
                v.memset(acc[:], 0.0).then_inc(s_mean, 1)
                dve.wait_ge(s_mean, 2)
                gate(dve, c)
                with dve.Fori(0, NG) as g:
                    v.tensor_tensor(group(c.agg, g), group(c.agg, g), mean[:].unsqueeze(1).to_broadcast([P, GT, D]),
                                    ALU.subtract).then_inc(s_cen, 1)
                    dve.wait_ge(s_cen, g + 1)
                    last = tile_of(c.agg, g, GT - 1)
                    v.tensor_scalar(last, last, c.real[:, ds(g * GT + (GT - 1), 1)], None, ALU.mult).then_inc(s_msk, 1)
                    add_up(turn2, g, NG + 1)
                dve.wait_ge(s_v, 2)
                v.tensor_scalar(acc[:], acc[:], 1.0 / N, None, ALU.mult).then_inc(s_v, 1)
                dve.wait_ge(s_p, 2)
                dve.wait_ge(s_in, 16)
                v.tensor_tensor(scale[:], acc[:], gam[:], ALU.mult).then_inc(s_v, 1)

            @block.gpsimd
            def _(pool):
                pool.wait_ge(s_v, 3)
                nc.gpsimd.tensor_tensor(acc[:], acc[:], eps[:], ALU.add).then_inc(s_p, 1)
                pool.wait_ge(s_p, 1)
                nc.gpsimd.tensor_tensor(acc[:], acc[:], power[:], ALU.pow).then_inc(s_p, 1)


def mix1_main(nc, c, a, scale, mx, total):
    with Phase(nc, "mix1") as ph:
        stage, nrm = ph.sb("stage", [P, GT, D]), ph.sb("norm", [P, GT, D])
        xt = ph.sb("xt", [P, KH, GR])
        bias, bo = ph.sb("bias", [P, 1, D]), ph.sb("bo", [P, 1, D])
        (s_in, s_bias, s_stage, s_xt, s_xtu, s_sc, s_bb, s_r, s_y, s_bn, s_mv, s_rs, s_tmp, s_nrm, s_msk, s_copy, s_acc,
         s_nu) = ph.sems("vectors_in bias_made staged xt xt_used scaled biased sum_made products_added partial variance rstd "
                         "sum normal masked copied accumulated norm_used")
        turn = c.ledger.plan([j % 8 for j in range(4 + 4)] + [0], NG)
        with nc.Block() as block:

            @block.sync
            def _(sp):
                sp.dma_start(bias[:, 0, :], spread(a["L1_gnn_beta"])).then_inc(s_in, 16)
                sp.dma_start(bo[:, 0, :], spread(a["L1_mix_bo"])).then_inc(s_in, 16)

            @block.tensor
            def _(pe):
                pe.sem_inc(s_xtu, 1)
                pe.sem_inc(s_nu, 1)
                with pe.Fori(0, NG) as g:
                    pe.wait_ge(s_stage, g + 1)
                    transposed(pe, c, lambda k, h: stage[:, k, h * P:(h + 1) * P], turn, 0, g)
                    pe.wait_ge(s_xt, g + 1)
                    for n in range(4):
                        b, t = turn(4 + n, g)
                        pe.wait_ge(c.bank_free[b], t)
                        for k in range(2 * n, min(2 * n + 2, GT)):
                            for h in range(KH):
                                ins = nc.tensor.matmul(c.bank[b][:, (k % 2) * D:(k % 2 + 1) * D], xt[:, h, k * P:(k + 1) * P],
                                                       mx[:, h, :], start=(h == 0), stop=(h == KH - 1))
                        ins.then_inc(c.bank_full[b], 1)
                    pe.wait_ge(c.bank_full[b], t)
                    pe.sem_inc(s_xtu, 1)
                    b, t = turn(8, g)
                    pe.wait_ge(c.bank_free[b], t)
                    pe.wait_ge(s_nrm, (g + 1) * GT)
                    pe.wait_ge(s_msk, g + 1)
                    for k in range(GT):
                        ins = nc.tensor.matmul(c.bank[b][:, 0:D], c.ones[:], nrm[:, k, :], start=(k == 0), stop=(k == GT - 1))
                    ins.then_inc(c.bank_full[b], 1)
                    pe.wait_ge(c.bank_full[b], t)
                    pe.sem_inc(s_nu, 1)

            @block.scalar
            def _(act):
                with act.Fori(0, NG) as g:
                    act.wait_ge(s_xtu, g + 1)
                    gate(act, c)
                    nc.scalar.copy(stage[:], group(c.xn, g)).then_inc(s_stage, 1)
                    evacuate_transposed(act, c, xt, turn, 0, g, s_xt)
                    act.wait_ge(s_msk, g + 1)
                    gate(act, c)
                    nc.scalar.copy(group(c.xn, g), nrm[:]).then_inc(s_copy, 1)

            @block.gpsimd
            def _(pool):
                p = nc.gpsimd
                pool.wait_ge(s_in, 32)
                p.tensor_tensor(bias[:], bias[:], bo[:], ALU.add).then_inc(s_bias, 1)
                pool.wait_ge(s_bias, 1)
                gate(pool, c)
                with pool.Fori(0, NG) as g:
                    x = group(c.agg, g)
                    p.tensor_tensor(x, x, scale[:].unsqueeze(1).to_broadcast([P, GT, D]), ALU.mult).then_inc(s_sc, 1)
                    pool.wait_ge(s_sc, g + 1)
                    gate(pool, c)
                    p.tensor_tensor(x, x, bias[:].to_broadcast([P, GT, D]), ALU.add).then_inc(s_bb, 1)
                    rstd(pool, c, g, s_mv, s_rs, s_tmp)

            @block.vector
            def _(dve):
                v = nc.vector
                v.memset(total[:], 0.0).then_inc(s_acc, 1)
                with dve.Fori(0, NG) as g:
                    dve.wait_ge(s_bb, g + 1)
                    v.tensor_tensor(group(c.res, g), group(c.res, g), group(c.agg, g), ALU.add).then_inc(s_r, 1)
                    dve.wait_ge(s_r, g + 1)
                    for n in range(4):
                        b, t = turn(4 + n, g)
                        w = min(2, GT - 2 * n)
                        dve.wait_ge(c.bank_full[b], t)
                        x = tile_of(c.res, g, 2 * n, 0, w * D)
                        v.tensor_tensor(x, x, c.bank[b][:, 0:w * D], ALU.add).then_inc(s_y, 1)
                        dve.wait_ge(s_y, g * 4 + (n + 1))
                        dve.sem_inc(c.bank_free[b], 1)
                    stats(dve, c, lambda k: tile_of(c.res, g, k), g, s_bn, s_mv)
                    dve.wait_ge(s_nu, g + 1)
                    normalise(dve, c, lambda k: nrm[:, k, :], lambda k: tile_of(c.res, g, k), g, s_rs, s_nrm)
                    dve.wait_ge(s_nrm, (g + 1) * GT)
                    v.tensor_scalar(nrm[:, GT - 1, :], nrm[:, GT - 1, :], c.real[:, ds(g * GT + (GT - 1), 1)], None,
                                    ALU.mult).then_inc(s_msk, 1)
                    b, t = turn(8, g)
                    dve.wait_ge(c.bank_full[b], t)
                    dve.wait_ge(s_acc, g + 1)
                    v.tensor_tensor(total[:], total[:], c.bank[b][:, 0:D], ALU.add).then_inc(s_acc, 1)
                    dve.wait_ge(s_acc, g + 2)
                    dve.sem_inc(c.bank_free[b], 1)
                    dve.wait_ge(s_copy, g + 1)


def router(nc, c, a, total, chosen, share):
    NE = 8
    CAP = float(-(-N * 5 // (4 * NE)))
    with Phase(nc, "router") as ph:
        wr = ph.sb("wr", [1, NE, D])
        em, junk = ph.sb("em", [1, D]), ph.sb("junk", [1, D])
        lg, br, ex = (ph.sb(n, [1, NE]) for n in ("lg", "br", "ex"))
        m1, sm = ph.sb("m1", [1, 1]), ph.sb("sm", [1, 1])
        gt, tri, rank = ph.sb("gt", [1, NE, NE]), ph.sb("tri", [1, NE, NE]), ph.sb("rank", [1, NE])
        two, pick, val = ph.sb("two", [1, 2, NE]), ph.sb("pick", [1, 2]), ph.sb("val", [1, 2])
        s_in, s_v, s_e, s_w, s_bc = ph.sems("weights_in vector_steps differences_made shares_made exponentials")
        turn = c.ledger.plan([0, 1], 1)
        with nc.Block() as block:

            @block.sync
            def _(sp):
                sp.dma_start(wr[:],
                             a["L1_ffn_Wr"].rearrange("(a d) e -> a e d", a=1), allow_slow_non_contiguous=True).then_inc(s_in, 16)
                sp.dma_start(br[:], a["L1_ffn_br"].rearrange("(a e) -> a e", a=1)).then_inc(s_in, 16)

            @block.tensor
            def _(pe):
                pe.wait_ge(s_w, 1)
                nc.tensor.matmul(c.bank[0][:, 0:2], c.ones[0:1, :], val[:], start=True, stop=True).then_inc(c.bank_full[0], 1)
                pe.sem_inc(c.bank_full[1], 1)

            @block.scalar
            def _(act):
                act.wait_ge(s_e, 1)
                nc.scalar.activation(ex[:], lg[:], ACT.Exp).then_inc(s_bc, 1)
                act.wait_ge(s_e, 2)
                nc.scalar.activation(ex[:], lg[:], ACT.Exp).then_inc(s_bc, 1)
                act.wait_ge(s_e, 3)
                nc.scalar.activation(val[:], val[:], ACT.Exp).then_inc(s_bc, 1)

            @block.vector
            def _(dve):
                v = nc.vector
                done = [0]

                def then(ins):
                    done[0] += 1
                    ins.then_inc(s_v, 1)
                    dve.wait_ge(s_v, done[0])

                dve.wait_ge(s_in, 32)
                then(v.tensor_scalar(em[:], total[0:1, :], 1.0 / N, None, ALU.mult))
                for e in range(NE):
                    then(v.tensor_tensor_reduce(junk[:], em[:], wr[:, e, :], 1.0, 0.0, ALU.mult, ALU.add, lg[:, e:e + 1]))
                then(v.tensor_tensor(lg[:], lg[:], br[:], ALU.add))

                def softmax(n, x, y):
                    then(v.tensor_reduce(m1[:], x[:], AX.X, ALU.max))
                    then(v.tensor_scalar(x[:], x[:], m1[:, 0:1], None, ALU.subtract))
                    dve.sem_inc(s_e, 1)
                    dve.wait_ge(s_bc, n)
                    then(v.tensor_reduce(sm[:], y[:], AX.X, ALU.add))
                    then(v.reciprocal(sm[:], sm[:]))
                    then(v.tensor_scalar(x[:], y[:], sm[:, 0:1], None, ALU.mult))

                softmax(1, lg, ex)
                then(v.tensor_scalar(lg[:], lg[:], CAP / N, None, ALU.min))
                softmax(2, lg, ex)
                me = lg[:].unsqueeze(2).to_broadcast([1, NE, NE])
                other = lg[:].unsqueeze(1).to_broadcast([1, NE, NE])
                no = c.iota[0:1, 0:NE]
                then(v.tensor_tensor(gt[:], other, me, ALU.is_equal))
                then(v.tensor_tensor(tri[:], no.unsqueeze(1).to_broadcast([1, NE, NE]), no.unsqueeze(2).to_broadcast([1, NE, NE]),
                                     ALU.is_lt))
                then(v.tensor_tensor(tri[:], tri[:], gt[:], ALU.mult))
                then(v.tensor_tensor(gt[:], other, me, ALU.is_gt))
                then(v.tensor_tensor(gt[:], gt[:], tri[:], ALU.add))
                then(v.tensor_reduce(rank[:], gt[:], AX.X, ALU.add))
                then(v.tensor_tensor(two[:], rank[:].unsqueeze(1).to_broadcast([1, 2, NE]),
                                     c.iota[0:1, 0:2].unsqueeze(2).to_broadcast([1, 2, NE]), ALU.is_equal))
                then(v.tensor_tensor(gt[:, 0:2, :], two[:], no.unsqueeze(1).to_broadcast([1, 2, NE]), ALU.mult))
                then(v.tensor_reduce(pick[:], gt[:, 0:2, :], AX.X, ALU.add))
                then(v.tensor_copy(chosen[:], pick[:]))
                then(v.tensor_tensor(gt[:, 0:2, :], two[:], lg[:].unsqueeze(1).to_broadcast([1, 2, NE]), ALU.mult))
                then(v.tensor_reduce(val[:], gt[:, 0:2, :], AX.X, ALU.add))
                softmax(3, val, val)
                dve.sem_inc(s_w, 1)
                dve.wait_ge(c.bank_full[0], turn(0, 0)[1])
                then(v.tensor_copy(share[:], c.bank[0][:, 0:2]))
                dve.sem_inc(c.bank_free[0], 1)
                dve.sem_inc(c.bank_free[1], 1)


def experts(nc, c, a, chosen, share, out):
    with Phase(nc, "experts") as ph:
        cut = carver(c.agg)
        stage = cut(GT, D)
        w1, w2, b1 = ph.sb("w1", [P, KH, 4 * D]), ph.sb("w2", [P, 8, D]), ph.sb("b1", [P, 8])
        u = ph.sb("rows", [P, GT, D])
        done_rows = ph.sb("done", [P, GT, D])
        vec, b2 = ph.sb("vec", [P, 2, D]), ph.sb("b2", [P, 2, D])
        turn = c.ledger.plan(Mlp.BANKS, NG)
        mlp = Mlp(nc, c, ph, turn, stage, cut, w1, w2, b1, ACT.Gelu)
        (s_in, s_w, s_stage, s_u, s_y, s_bn, s_mv, s_rs, s_tmp, s_nrm, s_gam, s_bet, s_out, s_store) = ph.sems(
            "weights_in weighted staged rows_biased rows_summed partial variance rstd sum normal gamma beta rows_done stored")
        with nc.Block() as block:

            @block.sync
            def _(sp):
                for i in range(2):
                    e = sp.value_load(chosen[0:1, i:i + 1], min_val=0, max_val=7)
                    one = ds(e, 1)
                    for h in range(KH):
                        sp.dma_start(w1[:, h, i * 2 * D:(i + 1) * 2 * D],
                                     a["L1_ffn_W1"][one, h * P:(h + 1) * P, :].rearrange("e p f -> p (e f)")).then_inc(s_in, 16)
                    for m in range(4):
                        sp.dma_start(w2[:, 4 * i + m, :],
                                     a["L1_ffn_W2"][one, m * P:(m + 1) * P, :].rearrange("e p o -> p (e o)")).then_inc(s_in, 16)
                        sp.dma_start(b1[:, 4 * i + m:4 * i + m + 1],
                                     a["L1_ffn_b1"][one, m * P:(m + 1) * P].rearrange("e p -> p e"),
                                     allow_slow_non_contiguous=True).then_inc(s_in, 16)
                    sp.dma_start(b2[:, i, :], a["L1_ffn_b2"][one, :].to_broadcast([P, D])).then_inc(s_in, 16)
                for j, n in enumerate(("gamma", "beta")):
                    sp.dma_start(vec[:, j, :], spread(a["L1_ffn_" + n])).then_inc(s_in, 16)
                sp.sem_inc(s_store, 16)
                with sp.Fori(0, NG - 1) as g:
                    sp.wait_ge(s_out, g + 1)
                    sp.dma_start(out[ds(g * GR, GR), :].rearrange("(k p) d -> p k d", p=P), done_rows[:]).then_inc(s_store, 16)
                sp.wait_ge(s_out, NG)
                at = (NG - 1) * GR
                sp.dma_start(out[at:at + (GT - 1) * P, :].rearrange("(k p) d -> p k d", p=P), done_rows[:, 0:GT - 1, :])\
                    .then_inc(s_store, 16)
                sp.dma_start(out[N - LAST:N, :], done_rows[0:LAST, GT - 1, :]).then_inc(s_store, 16)
                sp.wait_ge(s_store, 16 * (NG + 2))

            @block.tensor
            def _(pe):
                pe.sem_inc(mlp.s_used, 1)
                pe.wait_ge(s_w, 4)
                with pe.Fori(0, NG) as g:
                    pe.wait_ge(s_stage, g + 1)
                    mlp.tensor(pe, g)

            @block.scalar
            def _(act):
                act.wait_ge(s_in, 24 * 16)
                with act.Fori(0, NG) as g:
                    act.wait_ge(mlp.s_used, g + 1)
                    act.wait_ge(s_u, g + 1)
                    gate(act, c)
                    nc.scalar.copy(stage, group(c.xn, g)).then_inc(s_stage, 1)
                    mlp.scalar(act, g)

            @block.gpsimd
            def _(pool):
                p = nc.gpsimd
                pool.wait_ge(s_w, 4)
                pool.sem_inc(s_u, 1)
                with pool.Fori(0, NG) as g:
                    pool.wait_ge(s_stage, g + 1)
                    pool.wait_ge(s_y, g * 5 + 1)
                    p.tensor_tensor(u[:], stage, b2[:, 0:1, :].to_broadcast([P, GT, D]), ALU.add).then_inc(s_u, 1)
                    rstd(pool, c, g, s_mv, s_rs, s_tmp)
                    pool.wait_ge(s_nrm, (g + 1) * GT)
                    p.tensor_tensor(u[:], u[:], vec[:, 0:1, :].to_broadcast([P, GT, D]), ALU.mult).then_inc(s_gam, 1)

            @block.vector
            def _(dve):
                v = nc.vector
                dve.wait_ge(s_in, 24 * 16)
                for i in range(2):
                    x = w2[:, 4 * i:4 * i + 4, :]
                    v.tensor_scalar(x, x, share[:, i:i + 1], None, ALU.mult).then_inc(s_w, 1)
                v.tensor_scalar(b2[:, 0, :], b2[:, 0, :], share[:, 0:1], None, ALU.mult).then_inc(s_w, 1)
                dve.wait_ge(s_w, 3)
                v.scalar_tensor_tensor(b2[:, 0, :], b2[:, 1, :], share[:, 1:2], b2[:, 0, :], ALU.mult, ALU.add).then_inc(s_w, 1)
                dve.sem_inc(s_y, 1)
                tile = lambda k: u[:, k, :]
                with dve.Fori(0, NG) as g:
                    dve.wait_ge(s_u, g + 2)
                    for n, (j, k, w) in enumerate(mlp.pairs()):
                        b, t = turn(j, g)
                        dve.wait_ge(c.bank_full[b], t)
                        x = u[:, k:k + w, :].rearrange("p k d -> p (k d)")
                        v.tensor_tensor(x, x, c.bank[b][:, 0:w * D], ALU.add).then_inc(s_y, 1)
                        dve.wait_ge(s_y, g * 5 + (n + 2))
                        dve.sem_inc(c.bank_free[b], 1)
                    stats(dve, c, tile, g, s_bn, s_mv)
                    normalise(dve, c, tile, tile, g, s_rs, s_nrm)
                    dve.wait_ge(s_gam, g + 1)
                    v.tensor_tensor(u[:], u[:], vec[:, 1:2, :].to_broadcast([P, GT, D]), ALU.add).then_inc(s_bet, 1)
                    dve.wait_ge(s_bet, g + 1)
                    dve.wait_ge(s_store, (g + 1) * 16)
                    gate(dve, c)
                    v.tensor_tensor(done_rows[:], u[:], group(c.res, g), ALU.add).then_inc(s_out, 1)
                    dve.wait_ge(s_out, g + 1)
                    dve.sem_inc(s_y, 1)


def program(nc, a, out):
    c = Core()
    c.nc = nc
    ctx = ExitStack()
    with ctx:
        sb = lambda n, s, d: ctx.enter_context(nc.sbuf_tensor(n, s, d))
        c.sem = lambda n: ctx.enter_context(nc.semaphore(n))
        c.phase_sems = []
        c.ledger = Ledger()
        c.bank = [ctx.enter_context(nc.psum_tensor(f"bank{b}", [P, 512], F32)) for b in range(8)]
        c.bank_full = [c.sem(f"bank_full{b}") for b in range(8)]
        c.bank_free = [c.sem(f"bank_free{b}") for b in range(8)]
        c.gates = {str(e.engine): c.sem(f"waits_passed_{n}") for n, e in
                   (("pe", nc.tensor), ("act", nc.scalar), ("dve", nc.vector), ("pool", nc.gpsimd), ("sp", nc.sync))}
        c.regs = {str(e.engine): [e.alloc_register(f"tile{u}") for u in range(HALF)] for e in (nc.vector, nc.tensor)}
        c.res = sb("residual", [P, NT * D], F32)
        c.xn = sb("state", [P, NT * D], F32)
        c.agg = sb("sums", [P, NT * D], F32)
        c.ident = sb("ident", [P, P], F32)
        c.ones = sb("ones", [P, P], F32)
        c.iota = sb("iota", [P, P], F32)
        c.eps7 = sb("eps7", [P, GT], F32)
        c.pow7 = sb("pow7", [P, GT], F32)
        c.bn = sb("bn", [P, GT, 6], F32)
        c.mv = sb("mv", [P, GT, 2], F32)
        c.ve = sb("ve", [P, GT], F32)
        c.rs = sb("rs", [P, GT], F32)
        c.row_no = sb("row_no", [P, 1], F32)
        c.real = sb("real", [P, NT], F32)
        c.meta = sb("meta", [P, SB * P, 2], F32)
        c.local = c.meta[:, :, 0]
        c.tile_row = sb("tile_row", [1, SB * P], I32)
        c.row4 = sb("row4", [P, SB * P], I32)
        c.rec_d = nc.dram_tensor("edge_records", (RECN, 4), I32, kind="Internal").ap()
        c.tl_d = nc.dram_tensor("step_tiles", (SB * P,), I32, kind="Internal").ap()
        c.row8_d = nc.dram_tensor("table_rows_1", (P, SB * P), I32, kind="Internal").ap()
        c.tab0_d = nc.dram_tensor("tables0", (REL0 * NP, D), F32, kind="Internal").ap()
        c.tab1_d = nc.dram_tensor("tables1", (REL1 * NP, D), F32, kind="Internal").ap()

        constants(nc, c, a["x"])
        with nc.sbuf_tensor("rel4", [P, SB * P], F32) as c.rel4:
            edge_tables(nc, c, a["src"], a["dst"], a["edge_type_4"], a["edge_type_8"])
            edge_weights(nc, c)
        with ExitStack() as mix:
            wt = mix.enter_context(nc.sbuf_tensor("wt", [P, KH, 5 * D], F32))
            kv = mix.enter_context(nc.sbuf_tensor("kv", [P, KH, P + 4], F32))
            weights0(nc, c, a, wt)
            mix0_sums(nc, c, wt, kv)
            mix0_main(nc, c, a, wt, kv)
        gnn0(nc, c, a)
        with ExitStack() as l1:
            small = lambda n, s, d=F32: l1.enter_context(nc.sbuf_tensor(n, s, d))
            score, take = small("score", [P, NT]), small("take", [P, NT])
            mx, scale, total = small("mx", [P, KH, D]), small("scale", [P, D]), small("total", [P, D])
            chosen, share = small("chosen", [1, 2], I32), small("share", [P, 2])
            ffn0(nc, c, a, score)
            select(nc, c, score, take)
            with nc.sbuf_tensor("wt1", [P, KH, 3 * D], F32) as wt, nc.sbuf_tensor("wq1", [P, KH, D], F32) as wq:
                weights1(nc, c, a, wt, wq)
                mix1_matrix(nc, c, a, take, wt, wq, mx)
            tables1(nc, c, a)
            gnn1(nc, c)
            batch_norm(nc, c, a, scale)
            mix1_main(nc, c, a, scale, mx, total)
            router(nc, c, a, total, chosen, share)
            experts(nc, c, a, chosen, share, out)


def constants(nc, c, x):
    s_x, s_pad, s_c, s_v, s_free = (c.sem(n) for n in ("x_in", "pad_cleared", "constants_made", "ident_cleared", "real_step"))
    with nc.Block() as block:

        @block.sync
        def _(sp):
            full = c.res[:, 0:(NT - 1) * D].rearrange("p (t c) -> p t c", c=D)
            sp.dma_start(full, x[0:(NT - 1) * P, :].rearrange("(t p) c -> p t c", p=P)).then_inc(s_x, 16)
            sp.wait_ge(s_pad, 1)
            sp.dma_start(c.res[0:LAST, (NT - 1) * D:NT * D], x[(NT - 1) * P:N, :]).then_inc(s_x, 16)
            sp.wait_ge(s_x, 32)

        @block.gpsimd
        def _(pool):
            g = nc.gpsimd
            g.memset(c.res[:, (NT - 1) * D:NT * D], 0.0).then_inc(s_pad, 1)
            g.memset(c.ident[:], 0.0).then_inc(s_v, 1)
            g.memset(c.ones[:], 1.0).then_inc(s_c, 1)
            g.iota(c.iota[:], [[1, P]], base=0, channel_multiplier=0,
                   allow_small_or_imprecise_dtypes=True).then_inc(s_c, 1)
            g.iota(c.real[:], [[P, NT]], base=0, channel_multiplier=1,
                   allow_small_or_imprecise_dtypes=True).then_inc(s_free, 1)
            g.iota(c.row_no[:], [[0, 1]], base=0, channel_multiplier=1,
                   allow_small_or_imprecise_dtypes=True).then_inc(s_c, 1)
            pool.wait_ge(s_v, 1)
            g.affine_select(out=c.ident[:], in_=c.ident[:], compare_op=ALU.not_equal, fill=1.0, base=0,
                            pattern=[[-1, P]], channel_multiplier=1).then_inc(s_c, 1)

        @block.vector
        def _(dve):
            v = nc.vector
            v.memset(c.eps7[:], EPS).then_inc(s_c, 1)
            v.memset(c.pow7[:], -0.5).then_inc(s_c, 1)
            dve.wait_ge(s_free, 1)
            v.tensor_scalar(c.real[:], c.real[:], float(N), None, ALU.is_lt).then_inc(s_c, 1)
            for b in range(8):
                dve.sem_inc(c.bank_free[b], 1)


def kernel(**inputs):
    import numpy as _np
    import concourse.bacc as _bacc
    from concourse import mybir as _mybir
    from concourse.bass_utils import run_bass_kernel_spmd as _run

    nc = _bacc.Bacc("TRN2", target_bir_lowering=False, num_devices=1)
    arrays, args = {}, {}
    for name, value in inputs.items():
        a = _np.ascontiguousarray(value)
        arrays[f"in_{name}_dram"] = a
        args[name] = nc.dram_tensor(f"in_{name}_dram", a.shape, _mybir.dt.from_np(a.dtype), kind="ExternalInput").ap()
    out = nc.dram_tensor("out_0_dram", (N, D), F32, kind="ExternalOutput").ap()
    program(nc, args, out)
    r = _run(nc, [arrays], core_ids=[0])
    return r.results[0]["out_0_dram"]
```

```python
from contextlib import ExitStack

import concourse.bass as bass
from concourse import mybir

ALU = mybir.AluOpType
ACT = mybir.ActivationFunctionType
AX = mybir.AxisListType
F32 = mybir.dt.float32
BF16 = mybir.dt.bfloat16
I32 = mybir.dt.int32
ds = bass.ds

P = 128
N = 6250
D = 256
KH = D // P
E = 100000
NT = -(-N // P)
GT = 7
NG = NT // GT
NP = NT * P
LAST = N - (NT - 1) * P
GR = GT * P
CH = ((0, 4), (4, 3))
DEPTH, REL0, REL1 = 4, 4, 8
EPS = 1e-5
SLOTS = 16
HALF = SLOTS // 2
STEPS = -(-(E // P + 1 + NT) // SLOTS) * SLOTS
BODIES = STEPS // SLOTS
SB = -(-STEPS // P)
EP = 125
EC = E // EP
RECN = E + P
KK = N // 2 - 1
BIG = 1.0e30
assert NG * GT == NT and EP * EC == E


class Ledger:

    def __init__(self):
        self.used = [0] * 8

    def plan(self, banks, rounds):
        base = list(self.used)
        per = [banks.count(b) for b in range(8)]
        for b in range(8):
            self.used[b] += per[b] * rounds
        turns = []
        for j, b in enumerate(banks):
            turns.append((b, base[b] + banks[:j].count(b) + 1, per[b]))

        def turn(j, g):
            b, first, step = turns[j]
            return b, g * step + first

        return turn


class Core:
    pass


def rows_of(dram, first, tiles):
    return dram[ds(first, tiles * P), :].rearrange("(k p) c -> p k c", p=P)


def group(resident, g):
    return resident[:, ds(g * (GT * D), GT * D)].rearrange("p (k c) -> p k c", c=D)


def tile_of(resident, g, k, a=0, w=D):
    return resident[:, ds(g * (GT * D) + (k * D + a), w)]


def load_tiles(eng, c, first, n=HALF):
    regs = c.regs[str(eng.engine)][:n]
    eng.reg_load(regs, c.tile_row[0:1, ds(first, n)])
    return [eng.snap(r, min_val=0, max_val=NT - 1) for r in regs]


def gate(eng, c):
    eng.sem_inc(c.gates[str(eng.engine)], 1)


def transposed(pe, c, src, turn, j0, g, ready=None):
    for h in range(KH):
        for n, (k0, m) in enumerate(CH):
            b, t = turn(j0 + 2 * h + n, g)
            pe.wait_ge(c.bank_free[b], t)
            gate(pe, c)
            for k in range(k0, k0 + m):
                last = c.nc.tensor.transpose(c.bank[b][:, (k - k0) * P:(k - k0 + 1) * P], src(k, h), c.ident[:])
            last.then_inc(c.bank_full[b], 1)


def evacuate_transposed(act, c, dst, turn, j0, g, done):
    for h in range(KH):
        for n, (k0, m) in enumerate(CH):
            b, t = turn(j0 + 2 * h + n, g)
            act.wait_ge(c.bank_full[b], t)
            c.nc.scalar.copy(dst[:, h, k0 * P:(k0 + m) * P], c.bank[b][:, 0:m * P]).then_inc(c.bank_free[b], 1)
    act.wait_ge(c.bank_free[b], t + 1)
    act.sem_inc(done, 1)


def stats(dve, c, src, g, s_bn, s_mv):
    for k in range(GT):
        c.nc.vector.bn_stats(c.bn[:, k, :], src(k)).then_inc(s_bn, 1)
    dve.wait_ge(s_bn, (g + 1) * GT)
    gate(dve, c)
    for k in range(GT):
        c.nc.vector.bn_aggr(c.mv[:, k, :], c.bn[:, k, :]).then_inc(s_mv, 1)


def rstd(pool, c, g, s_mv, s_rs, s_tmp):
    pool.wait_ge(s_mv, (g + 1) * GT)
    c.nc.gpsimd.tensor_tensor(c.ve[:], c.mv[:, :, 1], c.eps7[:], ALU.add).then_inc(s_tmp, 1)
    pool.wait_ge(s_tmp, g + 1)
    c.nc.gpsimd.tensor_tensor(c.rs[:], c.ve[:], c.pow7[:], ALU.pow).then_inc(s_rs, 1)


def normalise(dve, c, dst, src, g, s_rs, done):
    dve.wait_ge(s_rs, g + 1)
    gate(dve, c)
    for k in range(GT):
        ins = c.nc.vector.tensor_scalar(dst(k), src(k), c.mv[:, k, 0:1], c.rs[:, k:k + 1], ALU.subtract, ALU.mult)
        ins.then_inc(done, 1)


def carver(resident):
    at = [0]

    def cut(*shape):
        n = 1
        for s in shape:
            n *= s
        view = resident[:, at[0]:at[0] + n]
        at[0] += n
        assert at[0] <= NT * D
        names = "abcd"[:len(shape)]
        if len(shape) == 1:
            return view
        return view.rearrange(f"p ({' '.join(names)}) -> p {' '.join(names)}", **dict(zip(names, shape)))

    return cut


class Phase:

    def __init__(self, nc, name):
        self.nc, self.name, self.held, self.stack = nc, name, [], ExitStack()

    def sem(self, name):
        self.held.append(self.nc.alloc_semaphore(f"{self.name}_{name}"))
        return self.held[-1]

    def sems(self, names):
        return [self.sem(n) for n in names.split()]

    def sb(self, name, shape, dtype=F32):
        return self.stack.enter_context(self.nc.sbuf_tensor(f"{self.name}_{name}", shape, dtype))

    def __enter__(self):
        return self

    def __exit__(self, *_):
        self.stack.close()
        self.nc.clear_and_free_semaphores(self.held)
        self.nc.all_engine_barrier()


def edge_tables(nc, c, src, dst, et4, et8):
    with Phase(nc, "edges") as ph:
        sb, sem = ph.sb, ph.sem
        e_src, e_dst, e_t4, e_t8 = (sb(n, [EP, EC], I32) for n in ("e_src", "e_dst", "e_t4", "e_t8"))
        e_rec = sb("e_rec", [EP, EC, 4], I32)
        e_tail = sb("e_tail", [P, 4], I32)
        hit = sb("hit", [EP, EC], F32)
        below = sb("below", [EP, NT + 1], F32)
        start = sb("start", [P, NT + 1], F32)
        cnt = sb("cnt", [P, NT], F32)
        cnt_i = sb("cnt_i", [P, NT], I32)
        nst = sb("nst", [P, NT], F32)
        cum = sb("cum", [P, 2, NT], F32)
        step_no = sb("step_no", [P, SB], F32)
        begun = sb("begun", [P, SB, NT], F32)
        over = sb("over", [P, SB, NT], F32)
        prod = sb("prod", [P, SB, NT], F32)
        tile_f = sb("tile_f", [P, SB], F32)
        base_f = sb("base_f", [P, SB], F32)
        s_f = sb("s_f", [P, SB], F32)
        end_f = sb("end_f", [P, SB], F32)
        e0 = sb("e0", [P, SB], F32)
        e0_i = sb("e0_i", [P, SB], I32)
        left = sb("left", [P, SB], F32)
        low = sb("low", [P, SB], F32)
        tile_i = sb("tile_i", [P, SB], I32)
        rows = c.xn[:, 0:SB * 4 * P].bitcast(I32).rearrange("p (b n) -> p b n", b=SB)
        slot_no = sb("slot_no", [P, P], F32)
        plane = c.agg[:, 0:SB * 4 * P].rearrange("p (b f s) -> p b f s", b=SB, f=4)
        valid = c.agg[:, SB * 4 * P:SB * 5 * P].rearrange("p (b s) -> p b s", b=SB)
        row8 = sb("row8", [P, SB * P], I32)
        rec_d = c.rec_d
        s_in, s_rec, s_recd, s_gat, s_tl, s_tr = (sem(n) for n in (
            "edges_in", "records_made", "records_stored", "records_gathered", "step_tiles_stored", "tile_row_loaded"))
        s_below, s_v, s_pl, s_iota, s_e0, s_ti, s_meta = (sem(n) for n in (
            "below_counted", "edge_vector_steps", "planes_made", "iotas_made", "step_starts_made",
            "step_tiles_made", "planes_copied"))
        turn = c.ledger.plan([b for b in range(7)] + [7], 1)
        with nc.Block() as block:

            @block.sync
            def _(sp):
                for to, of in ((e_src, src), (e_dst, dst), (e_t4, et4), (e_t8, et8)):
                    sp.dma_start(to[:], of.rearrange("(p n) -> p n", p=EP)).then_inc(s_in, 16)
                sp.wait_ge(s_rec, 4 + 1)
                sp.dma_start(rec_d[0:E, :].rearrange("(p n) f -> p n f", p=EP), e_rec[:]).then_inc(s_recd, 16)
                sp.dma_start(rec_d[E:RECN, :], e_tail[:]).then_inc(s_recd, 16)
                sp.wait_ge(s_ti, 1)
                sp.dma_start(c.tl_d.rearrange("(b p) -> p b", p=P), tile_i[:],
                             allow_slow_non_contiguous=True).then_inc(s_tl, 16)
                sp.wait_ge(s_tl, 16)
                sp.dma_start(c.tile_row[:], c.tl_d.rearrange("(a n) -> a n", a=1)).then_inc(s_tr, 16)
                sp.wait_ge(s_meta, 4 * SB)
                sp.dma_start(c.row8_d, row8[:]).then_inc(s_tr, 16)
                sp.wait_ge(s_tr, 32)

            @block.gpsimd
            def _(pool):
                nc.gpsimd.memset(e_tail[:], 0).then_inc(s_rec, 1)
                nc.gpsimd.iota(step_no[:], [[P, SB]], base=0, channel_multiplier=1,
                               allow_small_or_imprecise_dtypes=True).then_inc(s_iota, 1)
                nc.gpsimd.iota(slot_no[:], [[1, P]], base=0, channel_multiplier=0,
                               allow_small_or_imprecise_dtypes=True).then_inc(s_iota, 1)
                pool.wait_ge(s_recd, 32)
                pool.wait_ge(s_e0, 1)
                for b in range(SB):
                    nc.gpsimd.indirect_dma_start(
                        out=rows[:, b, :], out_offset=None, in_=rec_d,
                        in_offset=bass.IndirectOffsetOnAxis(ap=e0_i[:, b:b + 1], axis=0)).then_inc(s_gat, 16)

            @block.vector
            def _(dve):
                v = nc.vector
                done = [0]

                def then(ins):
                    done[0] += 1
                    ins.then_inc(s_v, 1)
                    dve.wait_ge(s_v, done[0])

                v.memset(below[:, 0:1], 0.0).then_inc(s_below, 1)
                dve.wait_ge(s_in, 64)
                v.scalar_tensor_tensor(e_rec[:, :, 0], e_t4[:], float(NP), e_src[:], ALU.mult, ALU.add).then_inc(s_rec, 1)
                v.scalar_tensor_tensor(e_rec[:, :, 1], e_t8[:], float(NP), e_src[:], ALU.mult, ALU.add).then_inc(s_rec, 1)
                v.tensor_copy(e_rec[:, :, 2], e_dst[:]).then_inc(s_rec, 1)
                v.tensor_copy(e_rec[:, :, 3], e_t4[:]).then_inc(s_rec, 1)
                for t in range(1, NT + 1):
                    if t > 1:
                        dve.wait_ge(s_below, t)
                    v.tensor_scalar(hit[:], e_dst[:], float(P * t), 0.0, ALU.is_lt, ALU.add,
                                    accum_out=below[:, t:t + 1]).then_inc(s_below, 1)
                dve.wait_ge(c.bank_full[0], 1)
                then(v.tensor_copy(start[:], c.bank[0][:, 0:NT + 1]))
                then(v.tensor_tensor(cnt[:], start[:, 1:NT + 1], start[:, 0:NT], ALU.subtract))
                then(v.tensor_scalar(cnt_i[:], cnt[:], float(P - 1), None, ALU.add))
                then(v.tensor_scalar(cnt_i[:], cnt_i[:], 7, None, ALU.arith_shift_right))
                then(v.tensor_copy(nst[:], cnt_i[:]))
                then(v.tensor_copy(cum[:, 0, :], nst[:]))
                s, at = 1, 0
                while s < NT:
                    then(v.tensor_copy(cum[:, 1 - at, 0:s], cum[:, at, 0:s]))
                    then(v.tensor_tensor(cum[:, 1 - at, s:NT], cum[:, at, s:NT], cum[:, at, 0:NT - s], ALU.add))
                    s, at = 2 * s, 1 - at
                incl, excl = cum[:, at, :], cum[:, 1 - at, :]
                then(v.tensor_tensor(excl, incl, nst[:], ALU.subtract))
                dve.wait_ge(s_iota, 2)
                wide = lambda a: a.unsqueeze(1).to_broadcast([P, SB, NT])
                num = step_no[:].unsqueeze(2).to_broadcast([P, SB, NT])
                then(v.tensor_tensor(over[:], wide(incl), num, ALU.is_le))
                then(v.tensor_tensor(begun[:], wide(excl), num, ALU.is_le))
                then(v.tensor_reduce(tile_f[:], over[:], AX.X, ALU.add))
                then(v.tensor_tensor(prod[:], over[:], wide(nst[:]), ALU.mult))
                then(v.tensor_reduce(base_f[:], prod[:], AX.X, ALU.add))
                then(v.tensor_tensor(prod[:], over[:], wide(cnt[:]), ALU.mult))
                then(v.tensor_reduce(s_f[:], prod[:], AX.X, ALU.add))
                then(v.tensor_tensor(prod[:], begun[:], wide(cnt[:]), ALU.mult))
                then(v.tensor_reduce(end_f[:], prod[:], AX.X, ALU.add))
                then(v.tensor_scalar(tile_f[:], tile_f[:], float(NT - 1), None, ALU.min))
                v.tensor_copy(tile_i[:], tile_f[:]).then_inc(s_ti, 1)
                then(v.tensor_tensor(e0[:], step_no[:], base_f[:], ALU.subtract))
                then(v.scalar_tensor_tensor(e0[:], e0[:], float(P), s_f[:], ALU.mult, ALU.add))
                then(v.tensor_scalar(e0[:], e0[:], float(E), None, ALU.min))
                v.tensor_copy(e0_i[:], e0[:]).then_inc(s_e0, 1)
                then(v.tensor_tensor(left[:], end_f[:], e0[:], ALU.subtract))
                then(v.tensor_scalar(low[:], tile_f[:], float(P), -1.0, ALU.mult, ALU.add))
                for b in range(SB):
                    then(v.tensor_scalar(valid[:, b, :], slot_no[:], left[:, b:b + 1], None, ALU.is_lt))
                dve.wait_ge(s_gat, 16 * SB)
                recs = rows[:].rearrange("p b (s f) -> p b s f", f=4)
                for b in range(SB):
                    for f in (0, 1):
                        then(v.tensor_scalar(plane[:, b, f, :], recs[:, b, :, f], -float(1 << 20), None, ALU.add))
                        then(v.tensor_tensor(plane[:, b, f, :], plane[:, b, f, :], valid[:, b, :], ALU.mult))
                        then(v.tensor_scalar(plane[:, b, f, :], plane[:, b, f, :], float(1 << 20), None, ALU.add))
                    then(v.tensor_scalar(plane[:, b, 2, :], recs[:, b, :, 2], low[:, b:b + 1], None, ALU.subtract))
                    then(v.tensor_tensor(plane[:, b, 2, :], plane[:, b, 2, :], valid[:, b, :], ALU.mult))
                    then(v.tensor_scalar(plane[:, b, 2, :], plane[:, b, 2, :], -1.0, None, ALU.add))
                    v.tensor_copy(plane[:, b, 3, :], recs[:, b, :, 3]).then_inc(s_pl, 1)
                for b in range(SB):
                    bb, t = turn(1 + b if b < 6 else 7, 0)
                    dve.wait_ge(c.bank_full[bb], t)
                    for f, to in enumerate((c.row4, row8, c.local, c.rel4)):
                        ins = v.tensor_copy(to[:, b * P:(b + 1) * P], c.bank[bb][:, f * P:(f + 1) * P])
                        ins.then_inc(s_meta, 1)
                    dve.wait_ge(s_meta, 4 * (b + 1))
                    dve.sem_inc(c.bank_free[bb], 1)
                dve.sem_inc(c.bank_free[0], 1)

            @block.tensor
            def _(pe):
                pe.wait_ge(s_below, NT + 1)
                nc.tensor.matmul(c.bank[0][:, 0:NT + 1], c.ones[0:EP, :], below[:], start=True, stop=True)\
                    .then_inc(c.bank_full[0], 1)
                for b in range(SB):
                    bb, t = turn(1 + b if b < 6 else 7, 0)
                    pe.wait_ge(s_pl, b + 1)
                    for f in range(4):
                        ins = nc.tensor.transpose(c.bank[bb][:, f * P:(f + 1) * P], plane[:, b, f, :], c.ident[:])
                    ins.then_inc(c.bank_full[bb], 1)


def edge_weights(nc, c):
    PARTS = 3
    W = PARTS * REL0
    with Phase(nc, "degree") as ph:
        sb = ph.sb
        hot = sb("hot", [P, 2, SLOTS, P], BF16)
        hot_t = sb("hot_t", [P, 2, SLOTS, P], BF16)
        rel = sb("rel", [P, 2, SLOTS, REL0], BF16)
        wide_rel = sb("wide_rel", [P, SLOTS, W], F32)
        picked = sb("picked", [P, SLOTS, W], F32)
        rel_no = sb("rel_no", [P, W], F32)
        count = sb("count", [P, NT, REL0], F32)
        rest = sb("rest", [P, NT, REL0], F32)
        inv = sb("inv", [P, NT, W], BF16)
        ident16 = sb("ident16", [P, P], BF16)
        zero = sb("zero", [P, NT * REL0], BF16)
        (s_set, s_hot, s_hot2, s_cnt, s_tot, s_free, s_v, s_inv, s_turned, s_ht, s_rel, s_pick, s_w, s_out) = ph.sems(
            "constants_set hot_made hot_made_again counts_summed totals_made totals_read vector_steps inverse_made hot_turned hot_copied "
            "relation_made weights_picked weights_masked weights_made")
        iota = c.iota[:].unsqueeze(1).to_broadcast([P, SLOTS, P])
        b4 = c.iota[:, 0:REL0].unsqueeze(1).to_broadcast([P, SLOTS, REL0])
        loc = lambda i: c.local[:, ds(i * SLOTS, SLOTS)].unsqueeze(2).to_broadcast([P, SLOTS, P])
        ret = lambda i, w: c.rel4[:, ds(i * SLOTS, SLOTS)].unsqueeze(2).to_broadcast([P, SLOTS, w])
        PAIRS = BODIES // 2
        assert PAIRS * 2 == BODIES
        totals = c.bank[0][:, 0:NT * REL0]
        with nc.Block() as block:

            @block.vector
            def _(dve):
                v = nc.vector
                v.tensor_copy(ident16[:], c.ident[:]).then_inc(s_set, 1)
                v.memset(zero[:], 0.0).then_inc(s_set, 1)
                for k in range(PARTS):
                    v.tensor_copy(rel_no[:, k * REL0:(k + 1) * REL0], c.iota[:, 0:REL0]).then_inc(s_set, 1)

                with dve.Fori(0, PAIRS) as q:
                    for h in range(2):
                        n = q * 2 + h
                        dve.wait_ge(s_cnt, n + 1)
                        gate(dve, c)
                        v.tensor_tensor(hot[:, h], iota, loc(n), ALU.is_equal).then_inc(s_hot, 1)
                        v.tensor_tensor(rel[:, h], b4, ret(n, REL0), ALU.is_equal).then_inc(s_hot, 1)
                done = [0]

                def then(ins):
                    done[0] += 1
                    ins.then_inc(s_v, 1)
                    dve.wait_ge(s_v, done[0])

                dve.wait_ge(s_tot, 1)
                then(v.tensor_scalar(count[:].rearrange("p t r -> p (t r)"), totals, 1.0, None, ALU.max))
                then(v.reciprocal(count[:], count[:]))
                part = lambda k: inv[:, :, k * REL0:(k + 1) * REL0]
                then(v.tensor_copy(part(0), count[:]))
                then(v.tensor_tensor(rest[:], count[:], part(0), ALU.subtract))
                then(v.tensor_copy(part(1), rest[:]))
                then(v.tensor_tensor(rest[:], rest[:], part(1), ALU.subtract))
                then(v.tensor_copy(part(2), rest[:]))
                dve.sem_inc(s_inv, 1)

                def make(n, h):
                    dve.wait_ge(s_turned, n + 1)
                    gate(dve, c)
                    v.tensor_tensor(hot[:, h], iota, loc(n), ALU.is_equal).then_inc(s_hot2, 1)

                def weigh(n, h):
                    dve.wait_ge(s_w, n + 2)
                    dve.wait_ge(s_out, n + 1)
                    gate(dve, c)
                    v.tensor_tensor(wide_rel[:], rel_no[:].unsqueeze(1).to_broadcast([P, SLOTS, W]), ret(n, W),
                                    ALU.is_equal).then_inc(s_rel, 1)
                    dve.wait_ge(s_pick, n + 3)
                    dve.wait_ge(s_rel, n + 1)
                    v.tensor_tensor(picked[:], c.bank[6 + h][:, 0:SLOTS * W].rearrange("p (s r) -> p s r", r=W),
                                    wide_rel[:], ALU.mult).then_inc(s_w, 1)
                    dve.wait_ge(s_w, n + 3)
                    gate(dve, c)
                    v.tensor_reduce(c.meta[:, ds(n * SLOTS, SLOTS), 1], picked[:], AX.X, ALU.add).then_inc(s_out, 1)

                dve.sem_inc(s_w, 2)
                dve.sem_inc(s_out, 1)
                dve.wait_ge(s_set, 2 + PARTS)
                make(0, 0)
                with dve.Fori(0, PAIRS) as q:
                    make(q * 2 + 1, 1)
                    weigh(q * 2, 0)
                    make(q * 2 + 2, 0)
                    weigh(q * 2 + 1, 1)

            @block.tensor
            def _(pe):
                pe.wait_ge(s_set, 2 + PARTS)
                nc.tensor.matmul(totals, ident16[:], zero[:], start=True, stop=False)
                pe.sem_inc(s_cnt, 2)
                with pe.Fori(0, PAIRS) as q:
                    for h in range(2):
                        n = q * 2 + h
                        for u in range(SLOTS):
                            if u % HALF == 0:
                                tiles = load_tiles(pe, c, n * SLOTS + u)
                            if u == 0:
                                pe.wait_ge(s_hot, n * 2 + 2)
                            ins = nc.tensor.matmul(c.bank[0][:, ds(tiles[u % HALF] * REL0, REL0)], hot[:, h, u, :],
                                                   rel[:, h, u, :], start=False, stop=False)
                        ins.then_inc(s_cnt, 1)
                nc.tensor.matmul(totals, ident16[:], zero[:], start=False, stop=True).then_inc(s_tot, 1)

                def turn(n, h):
                    pe.wait_ge(s_hot2, n + 1)
                    pe.wait_ge(s_ht, n * 2 + 2)
                    gate(pe, c)
                    for u in range(SLOTS):
                        ins = nc.tensor.transpose(c.bank[2 + 2 * h + u // HALF][:].bitcast(BF16)[:, (u % HALF) * P:(u % HALF + 1) * P],
                                                  hot[:, h, u, :], ident16[:])
                    ins.then_inc(s_turned, 1)

                def pick(n, h):
                    for u in range(SLOTS):
                        if u % HALF == 0:
                            tiles = load_tiles(pe, c, n * SLOTS + u)
                        if u == 0:
                            pe.wait_ge(s_ht, n * 2 + 6)
                            pe.wait_ge(s_w, n + 1)
                        ins = nc.tensor.matmul(c.bank[6 + h][:, u * W:(u + 1) * W], hot_t[:, h, u, :],
                                               inv[:].rearrange("p t r -> p (t r)")[:, ds(tiles[u % HALF] * W, W)],
                                               start=True, stop=True)
                    ins.then_inc(s_pick, 1)

                pe.wait_ge(s_inv, 1)
                pe.sem_inc(s_turned, 2)
                pe.sem_inc(s_pick, 2)
                turn(0, 0)
                with pe.Fori(0, PAIRS) as q:
                    turn(q * 2 + 1, 1)
                    pick(q * 2, 0)
                    turn(q * 2 + 2, 0)
                    pick(q * 2 + 1, 1)

            @block.scalar
            def _(act):
                act.sem_inc(s_ht, 4)
                with act.Fori(0, PAIRS) as q:
                    for h in range(2):
                        n = q * 2 + h
                        act.wait_ge(s_turned, n + 3)
                        act.wait_ge(s_pick, n + 1)
                        for b in range(2):
                            nc.scalar.copy(hot_t[:, h, b * HALF:(b + 1) * HALF, :],
                                           c.bank[2 + 2 * h + b][:].bitcast(BF16).rearrange("p (u e) -> p u e", u=HALF)).then_inc(s_ht, 1)


class EdgeSum:

    def __init__(self, nc, c):
        self.nc, self.c = nc, c
        self.landed = [c.sem(f"message{s}_landed") for s in range(SLOTS)]
        self.ring_ready, self.hot_ready, self.summed, self.added = (
            c.sem(n) for n in ("slots_copied", "hot_made", "steps_summed", "steps_added"))

    def use(self, msg, hot, row_ring, meta_ring, rows, table, weighted):
        self.msg, self.hot = msg, hot
        self.row_ring, self.meta_ring, self.rows, self.table, self.weighted = row_ring, meta_ring, rows, table, weighted

    def scalar(self, act, i, n):
        for h in range(2):
            act.wait_ge(self.summed, n * SLOTS + (h + 1) * HALF)
            gate(act, self.c)
            at = ds(i * SLOTS + h * HALF, HALF)
            self.nc.scalar.copy(self.row_ring[:, h, :], self.rows[:, at]).then_inc(self.ring_ready, 1)
            self.nc.scalar.copy(self.meta_ring[:, h, :, :], self.c.meta[:, at, :]).then_inc(self.ring_ready, 1)

    def gpsimd(self, pool, n, after=None):
        for h in range(2):
            pool.wait_ge(self.ring_ready, n * 4 + (2 * h + 2))
            gate(pool, self.c)
            for u in range(HALF):
                s = h * HALF + u
                self.nc.gpsimd.indirect_dma_start(
                    out=self.msg[:, s, :], out_offset=None, in_=self.table,
                    in_offset=bass.IndirectOffsetOnAxis(ap=self.row_ring[:, h, u:u + 1], axis=0),
                    bounds_check=self.table.shape[0] - 1, oob_is_err=False).then_inc(self.landed[s], 16)
                if after:
                    after(s)

    def vector(self, dve, i, n, after=None):
        for h in range(2):
            dve.wait_ge(self.ring_ready, n * 4 + (2 * h + 2))
            for u in range(HALF):
                m = self.meta_ring[:, h, u, :]
                if self.weighted:
                    ins = self.nc.vector.tensor_scalar(self.hot[:, h * HALF + u, :], self.c.iota[:], m[:, 0:1], m[:, 1:2],
                                                       ALU.is_equal, ALU.mult)
                else:
                    ins = self.nc.vector.tensor_scalar(self.hot[:, h * HALF + u, :], self.c.iota[:], m[:, 0:1], None,
                                                       ALU.is_equal)
                ins.then_inc(self.hot_ready, 1)
            tiles = load_tiles(dve, self.c, i * SLOTS + h * HALF)
            for u, t in enumerate(tiles):
                s = h * HALF + u
                dve.wait_ge(self.summed, n * SLOTS + (SLOTS + s + 1))
                dve.wait_ge(self.added, n * SLOTS + (4 + s))
                at = self.c.agg[:, ds(t * D, D)]
                self.nc.vector.tensor_tensor(at, at, self.c.bank[4 + s % 4][:, 0:D], ALU.add).then_inc(self.added, 1)
                if after:
                    after(s)

    def tensor(self, pe, n, after=None):
        for s in range(SLOTS):
            pe.wait_ge(self.landed[s], n * 16 + 16)
            pe.wait_ge(self.hot_ready, n * SLOTS + s + 1)
            pe.wait_ge(self.added, n * SLOTS + (s + 1))
            self.nc.tensor.matmul(self.c.bank[4 + s % 4][:, 0:D], self.hot[:, s, :], self.msg[:, s, :],
                                  start=True, stop=True).then_inc(self.summed, 1)
            if after:
                after(s)


def gnn0(nc, c, a):
    W, roots = a["L0_gnn_weights"], a["L0_gnn_roots"]
    with Phase(nc, "gnn0") as ph:
        sb = ph.sb
        msg = sb("msg", [P, SLOTS, D], F32)
        hot = sb("hot0", [P, SLOTS, P], F32)
        ex = sb("ex", [P, GT * D], F32)
        w = sb("w0", [P, KH, (REL0 + 1) * D], F32)
        vecs = sb("vecs", [P, 3, D], F32)
        row_ring = sb("row_ring", [P, 2, HALF], I32)
        meta_ring = sb("meta_ring", [P, 2, HALF, 2], F32)
        xt = hot[:].rearrange("p s e -> p (s e)")[:, 0:KH * GR].rearrange("p (h r) -> p h r", h=KH)
        flat_msg = msg[:].rearrange("p s d -> p (s d)")
        outs = flat_msg[:, 0:6 * 2 * D].rearrange("p (o n) -> p o n", o=6)
        stage = flat_msg[:, 6 * 2 * D:]
        edges = c.edges = EdgeSum(nc, c)
        edges.use(msg, hot, row_ring, meta_ring, c.row4, c.tab0_d, True)
        names = ("weights_in", "xt_ready", "tile_made", "roots_made", "bias_added", "partial", "variance",
                 "rstd", "sum", "normal", "gamma", "beta", "exp", "exp_cut", "elu", "state", "layer_tables", "staged", "vectors_in")
        (s_w, s_xt, s_out, s_root, s_bias, s_bn, s_mv, s_rs, s_tmp, s_nrm, s_gam, s_bet, s_exp, s_cut, s_elu,
         s_state, s_tabs, s_stage, s_vec) = (ph.sem(n) for n in names)
        s_store = [ph.sem(f"tables_stored{o}") for o in range(6)]
        turned = c.ledger.plan([0, 1, 0, 1], DEPTH * NG)
        turn = c.ledger.plan([2 + j % 2 for j in range(3 * GT)], DEPTH * NG)
        ways = [0, 1, 2, 3, 4, 0, 1, 5, 2, 3, 0, 1, 4, 5]
        per = [ways.count(o) for o in range(6)]
        stored = lambda m, q: (q * per[ways[m]] + ways[:m].count(ways[m]) + 1) * 16
        with nc.Block() as block:

            @block.sync
            def _(sp):
                with sp.Fori(0, DEPTH) as l:
                    sp.wait_ge(s_tabs, l + 1)
                    for h in range(KH):
                        sp.dma_start(w[:, h, 0:REL0 * D].rearrange("p (r o) -> p r o", r=REL0),
                                     W.rearrange("l r i o -> (l r) i o")[ds(l * REL0, REL0), h * P:(h + 1) * P, :]
                                     .rearrange("r p o -> p r o")).then_inc(s_w, 16)
                        sp.dma_start(w[:, h, REL0 * D:], roots[ds(l, 1), h * P:(h + 1) * P, :]
                                     .rearrange("l p o -> p (l o)")).then_inc(s_w, 16)
                    with sp.Fori(0, NG) as g:
                        q = l * NG + g
                        for k in range(GT):
                            at = g * GR + k * P
                            for j in range(2):
                                o = ways[2 * k + j]
                                sp.wait_ge(s_out, q * (2 * GT) + (2 * k + j + 1))
                                sp.dma_start(c.tab0_d.rearrange("(r n) d -> n r d", n=NP)[ds(at, P), 2 * j:2 * j + 2, :],
                                             outs[:, o, :].rearrange("p (r d) -> p r d", d=D)).then_inc(s_store[o], 16)
                    sp.wait_ge(s_state, l * NG + NG)
                    for j, n in enumerate(("L0_gnn_biases", "L0_gnn_ln_gamma", "L0_gnn_ln_beta")):
                        sp.dma_start(vecs[:, j, :], a[n][ds(l, 1), :].to_broadcast([P, D])).then_inc(s_vec, 16)

            @block.tensor
            def _(pe):
                def turn_chunk(n, q):
                    k0, m = CH[n]
                    pe.wait_ge(s_stage, q * 2 + (n + 1))
                    for h in range(KH):
                        b, t = turned(2 * n + h, q)
                        pe.wait_ge(c.bank_free[b], t)
                        gate(pe, c)
                        for k in range(k0, k0 + m):
                            ins = nc.tensor.transpose(c.bank[b][:, (k - k0) * P:(k - k0 + 1) * P],
                                                      stage[:, (k - k0) * D + h * P:(k - k0) * D + (h + 1) * P], c.ident[:])
                        ins.then_inc(c.bank_full[b], 1)

                def multiply(n, q):
                    k0, m = CH[n]
                    pe.wait_ge(s_xt, q * 2 + (n + 1))
                    for k in range(k0, k0 + m):
                        for j in range(3):
                            b, t = turn(3 * k + j, q)
                            pe.wait_ge(c.bank_free[b], t)
                            width = 512 if j < 2 else D
                            for h in range(KH):
                                ins = nc.tensor.matmul(c.bank[b][:, 0:width], xt[:, h, k * P:(k + 1) * P],
                                                       w[:, h, j * 512:j * 512 + width], start=(h == 0), stop=(h == KH - 1))
                            ins.then_inc(c.bank_full[b], 1)
                    return b, t

                pe.sem_inc(s_tabs, 1)
                pe.sem_inc(edges.summed, SLOTS)
                with pe.Fori(0, DEPTH) as l:
                    pe.wait_ge(s_w, l * 64 + 64)
                    turn_chunk(0, l * NG)
                    with pe.Fori(0, NG - 1) as g:
                        turn_chunk(1, l * NG + g)
                        multiply(0, l * NG + g)
                        turn_chunk(0, l * NG + g + 1)
                        multiply(1, l * NG + g)
                    turn_chunk(1, l * NG + (NG - 1))
                    multiply(0, l * NG + (NG - 1))
                    b, t = multiply(1, l * NG + (NG - 1))
                    pe.wait_ge(c.bank_full[b], t)
                    pe.sem_inc(s_tabs, 1)
                    with pe.Fori(0, BODIES) as i:
                        edges.tensor(pe, l * BODIES + i)

            @block.scalar
            def _(act):
                for o in range(6):
                    act.sem_inc(s_store[o], 16)
                def prepare(n, g, q):
                    k0, m = CH[n]
                    act.wait_ge(s_state, q + 1)
                    gate(act, c)
                    nc.scalar.copy(stage[:, 0:m * D], c.xn[:, ds(g * (GT * D) + k0 * D, m * D)]).then_inc(s_stage, 1)
                    for h in range(KH):
                        b, t = turned(2 * n + h, q)
                        act.wait_ge(c.bank_full[b], t)
                        nc.scalar.copy(xt[:, h, k0 * P:(k0 + m) * P], c.bank[b][:, 0:m * P]).then_inc(c.bank_free[b], 1)
                    act.wait_ge(c.bank_free[b], t + 1)
                    act.sem_inc(s_xt, 1)

                def way_out(n, g, q):
                    k0, m = CH[n]
                    for k in range(k0, k0 + m):
                        for j in range(2):
                            b, t = turn(3 * k + j, q)
                            o = ways[2 * k + j]
                            act.wait_ge(s_store[o], stored(2 * k + j, q))
                            act.wait_ge(c.bank_full[b], t)
                            nc.scalar.copy(outs[:, o, :], c.bank[b][:]).then_inc(s_out, 1)
                            act.wait_ge(s_out, q * (2 * GT) + (2 * k + j + 1))
                            act.sem_inc(c.bank_free[b], 1)
                        b, t = turn(3 * k + 2, q)
                        act.wait_ge(c.bank_full[b], t)
                        gate(act, c)
                        nc.scalar.copy(tile_of(c.agg, g, k), c.bank[b][:, 0:D]).then_inc(s_root, 1)
                        act.wait_ge(s_root, q * GT + (k + 1))
                        act.sem_inc(c.bank_free[b], 1)

                def tables(g, q):
                    prepare(1, g, q)
                    way_out(0, g, q)
                    prepare(0, g + 1, q + 1)
                    way_out(1, g, q)

                def last_tables(q):
                    prepare(1, NG - 1, q)
                    way_out(0, NG - 1, q)
                    way_out(1, NG - 1, q)

                def exponential(g, q):
                    act.wait_ge(s_bet, q + 1)
                    act.wait_ge(s_elu, q + 1)
                    gate(act, c)
                    nc.scalar.activation(ex[:], c.agg[:, ds(g * (GT * D), GT * D)], ACT.Exp).then_inc(s_exp, 1)

                prepare(0, 0, 0)
                with act.Fori(0, NG - 1) as g:
                    tables(g, g)
                last_tables(NG - 1)
                with act.Fori(0, DEPTH - 1) as l:
                    with act.Fori(0, BODIES) as i:
                        edges.scalar(act, i, l * BODIES + i)
                    for g in range(2):
                        exponential(g, l * NG + g)
                    prepare(0, 0, l * NG + NG)
                    with act.Fori(0, NG - 2) as g:
                        exponential(g + 2, l * NG + g + 2)
                        tables(g, l * NG + g + NG)
                    tables(NG - 2, l * NG + (2 * NG - 2))
                    last_tables(l * NG + (2 * NG - 1))
                with act.Fori(0, BODIES) as i:
                    edges.scalar(act, i, (DEPTH - 1) * BODIES + i)
                with act.Fori(0, NG) as g:
                    exponential(g, (DEPTH - 1) * NG + g)

            @block.gpsimd
            def _(pool):
                with pool.Fori(0, DEPTH) as l:
                    for o in range(6):
                        pool.wait_ge(s_store[o], (l + 1) * (NG * per[o] * 16) + 16)
                    gate(pool, c)
                    with pool.Fori(0, BODIES) as i:
                        edges.gpsimd(pool, l * BODIES + i)
                    pool.wait_ge(edges.added, (l + 1) * STEPS + 4)
                    pool.wait_ge(s_vec, l * 48 + 48)
                    gate(pool, c)
                    with pool.Fori(0, NG) as g:
                        q = l * NG + g
                        gate(pool, c)
                        x = group(c.agg, g)
                        nc.gpsimd.tensor_tensor(x, x, vecs[:, 0:1, :].to_broadcast([P, GT, D]), ALU.add).then_inc(s_bias, 1)
                        rstd(pool, c, q, s_mv, s_rs, s_tmp)
                        pool.wait_ge(s_nrm, (q + 1) * GT)
                        gate(pool, c)
                        nc.gpsimd.tensor_tensor(x, x, vecs[:, 1:2, :].to_broadcast([P, GT, D]), ALU.mult).then_inc(s_gam, 1)

            @block.vector
            def _(dve):
                v = nc.vector
                dve.sem_inc(edges.added, 4)
                dve.sem_inc(s_state, NG)
                dve.sem_inc(s_elu, 1)
                with dve.Fori(0, DEPTH) as l:
                    dve.wait_ge(s_root, (l + 1) * NT)
                    gate(dve, c)
                    with dve.Fori(0, BODIES) as i:
                        edges.vector(dve, i, l * BODIES + i)
                    with dve.Fori(0, NG) as g:
                        q = l * NG + g
                        tile = lambda k: tile_of(c.agg, g, k)
                        dve.wait_ge(s_bias, q + 1)
                        gate(dve, c)
                        stats(dve, c, tile, q, s_bn, s_mv)
                        normalise(dve, c, tile, tile, q, s_rs, s_nrm)
                        dve.wait_ge(s_gam, q + 1)
                        x = group(c.agg, g)
                        v.tensor_tensor(x, x, vecs[:, 2:3, :].to_broadcast([P, GT, D]), ALU.add).then_inc(s_bet, 1)
                        dve.wait_ge(s_exp, q + 1)
                        v.tensor_scalar(ex[:], ex[:], 1.0, -1.0, ALU.min, ALU.add).then_inc(s_cut, 1)
                        dve.wait_ge(s_cut, q + 1)
                        flat = lambda r: r[:, ds(g * (GT * D), GT * D)]
                        v.scalar_tensor_tensor(flat(c.agg), flat(c.agg), 0.0, ex[:], ALU.max, ALU.add).then_inc(s_elu, 1)
                        dve.wait_ge(s_elu, q + 2)
                        v.tensor_tensor(flat(c.xn), flat(c.xn), flat(c.agg), ALU.add).then_inc(s_state, 1)


def spread(dram_vec, n=D):
    return dram_vec.rearrange("(a n) -> a n", a=1).to_broadcast([P, n])


def weights0(nc, c, a, wt):
    nat = c.agg[:, 0:10 * D].rearrange("p (b i) -> p b i", i=D)
    with Phase(nc, "weights0") as ph:
        s_in, = ph.sems("natural_in")
        turn = c.ledger.plan([0, 1, 2, 3, 4], 1)
        with nc.Block() as block:

            @block.sync
            def _(sp):
                for name, b, n in (("L0_mix_Wqkv", 0, 6), ("L0_mix_W1", 6, 2), ("L0_mix_W2", 8, 2)):
                    sp.dma_start(nat[:, b:b + n, :], a[name].rearrange("(b p) i -> p b i", p=P)).then_inc(s_in, 16)

            @block.tensor
            def _(pe):
                pe.wait_ge(s_in, 48)
                for j in range(5):
                    b, t = turn(j, 0)
                    pe.wait_ge(c.bank_free[b], t)
                    for h in range(KH):
                        for n in range(2):
                            ins = nc.tensor.transpose(c.bank[b][:, (2 * h + n) * P:(2 * h + n + 1) * P],
                                                      nat[:, 2 * j + n, h * P:(h + 1) * P], c.ident[:])
                    ins.then_inc(c.bank_full[b], 1)

            @block.scalar
            def _(act):
                for j in range(5):
                    b, t = turn(j, 0)
                    act.wait_ge(c.bank_full[b], t)
                    nc.scalar.copy(wt[:, :, j * D:(j + 1) * D],
                                   c.bank[b][:].rearrange("p (h o) -> p h o", h=KH)).then_inc(c.bank_free[b], 1)


def mix0_sums(nc, c, wt, kv):
    with Phase(nc, "keys0") as ph:
        cut = carver(c.agg)
        stage, er, rr = cut(GT, D), cut(GT, D), cut(GT, D)
        xt = cut(KH, GR)
        v1 = cut(GT, KH, P + 4)
        acc = ph.sb("acc", [P, KH, P + 1])
        (s_bn, s_mv, s_rs, s_tmp, s_nrm, s_xt, s_e, s_v, s_k, s_km, s_used, s_acc, s_copy, s_kvu, s_bd) = ph.sems(
            "partial variance rstd sum normal xt exp_relu values keys keys_masked stage_used accumulated copied kv_used diagonal")
        turn = c.ledger.plan([j % 6 for j in range(4 + GT + 1)], NG)
        with nc.Block() as block:

            @block.vector
            def _(dve):
                v = nc.vector
                v.memset(v1[:], 1.0).then_inc(s_v, 1)
                v.memset(acc[:], 0.0).then_inc(s_acc, 1)
                v.memset(kv[:], 0.0).then_inc(s_bd, 1)
                dve.sem_inc(s_used, 1)
                with dve.Fori(0, NG) as g:
                    stats(dve, c, lambda k: tile_of(c.res, g, k), g, s_bn, s_mv)
                    dve.wait_ge(s_used, g + 1)
                    dve.wait_ge(s_copy, g + 1)
                    normalise(dve, c, lambda k: stage[:, k, :], lambda k: tile_of(c.res, g, k), g, s_rs, s_nrm)
                    for k in range(GT):
                        dve.wait_ge(s_e, g * GT + (k + 1))
                        v.scalar_tensor_tensor(er[:, k, :], er[:, k, :], 1.0, rr[:, k, :], ALU.min, ALU.add).then_inc(s_k, 1)
                    dve.wait_ge(s_k, g * GT + GT)
                    v.tensor_scalar(er[:, GT - 1, :], er[:, GT - 1, :], c.real[:, ds(g * GT + (GT - 1), 1)], None,
                                    ALU.mult).then_inc(s_km, 1)
                    b, t = turn(4 + GT, g)
                    dve.wait_ge(c.bank_full[b], t)
                    dve.wait_ge(s_acc, g + 1)
                    v.tensor_tensor(acc[:], acc[:], c.bank[b][:, 0:KH * (P + 1)].rearrange("p (a m) -> p a m", a=KH),
                                    ALU.add).then_inc(s_acc, 1)
                    dve.wait_ge(s_acc, g + 2)
                    dve.sem_inc(c.bank_free[b], 1)
                dve.wait_ge(s_acc, NG + 1)
                dve.wait_ge(s_bd, 1)
                for j in range(4):
                    r = slice(32 * j, 32 * j + 32)
                    v.tensor_copy(kv[r, :, r], acc[r, :, r]).then_inc(s_bd, 1)
                    v.tensor_copy(kv[r, :, P + j:P + j + 1], acc[r, :, P:P + 1]).then_inc(s_bd, 1)

            @block.gpsimd
            def _(pool):
                with pool.Fori(0, NG) as g:
                    rstd(pool, c, g, s_mv, s_rs, s_tmp)

            @block.scalar
            def _(act):
                act.sem_inc(s_copy, 1)
                act.wait_ge(s_v, 1)
                with act.Fori(0, NG) as g:
                    act.wait_ge(s_nrm, (g + 1) * GT)
                    gate(act, c)
                    nc.scalar.copy(group(c.xn, g), stage[:]).then_inc(s_copy, 1)
                    evacuate_transposed(act, c, xt, turn, 0, g, s_xt)
                    for k in range(GT):
                        b, t = turn(4 + k, g)
                        act.wait_ge(c.bank_full[b], t)
                        act.wait_ge(s_kvu, g + 1)
                        nc.scalar.activation(er[:, k, :], c.bank[b][:, 0:D], ACT.Exp).then_inc(s_v, 1)
                        nc.scalar.activation(rr[:, k, :], c.bank[b][:, 0:D], ACT.Relu).then_inc(s_v, 1)
                        nc.scalar.copy(v1[:, k, :, 0:P], c.bank[b][:, D:2 * D].rearrange("p (a m) -> p a m", a=KH))\
                            .then_inc(s_v, 1)
                        act.wait_ge(s_v, g * (3 * GT) + (3 * k + 4))
                        act.sem_inc(c.bank_free[b], 1)
                        act.sem_inc(s_e, 1)

            @block.tensor
            def _(pe):
                pe.sem_inc(s_kvu, 1)
                with pe.Fori(0, NG) as g:
                    pe.wait_ge(s_nrm, (g + 1) * GT)
                    transposed(pe, c, lambda k, h: stage[:, k, h * P:(h + 1) * P], turn, 0, g)
                    pe.wait_ge(s_xt, g + 1)
                    pe.sem_inc(s_used, 1)
                    for k in range(GT):
                        b, t = turn(4 + k, g)
                        pe.wait_ge(c.bank_free[b], t)
                        for h in range(KH):
                            ins = nc.tensor.matmul(c.bank[b][:], xt[:, h, k * P:(k + 1) * P], wt[:, h, D:3 * D],
                                                   start=(h == 0), stop=(h == KH - 1))
                        ins.then_inc(c.bank_full[b], 1)
                    b, t = turn(4 + GT, g)
                    pe.wait_ge(c.bank_free[b], t)
                    pe.wait_ge(s_km, g + 1)
                    for s in range(KH):
                        for k in range(GT):
                            ins = nc.tensor.matmul(c.bank[b][:, s * (P + 1):(s + 1) * (P + 1)], er[:, k, s * P:(s + 1) * P],
                                                   v1[:, k, s, 0:P + 1], start=(k == 0), stop=(k == GT - 1))
                    ins.then_inc(c.bank_full[b], 1)
                    pe.wait_ge(c.bank_full[b], t)
                    pe.sem_inc(s_kvu, 1)


def mix0_main(nc, c, a, wt, kv):
    with Phase(nc, "mix0") as ph:
        cut = carver(c.agg)
        stage, u = cut(GT, D), cut(GT, D)
        xt, et, rt = cut(KH, GR), cut(KH, GR), cut(KH, GR)
        z = ph.sb("z", [P, GT, KH, 4])
        vec = ph.sb("vec", [P, 5, D])
        b1 = ph.sb("b1", [P, KH])
        (s_in, s_stage, s_xt, s_er, s_q, s_den, s_rec, s_t, s_u, s_bn, s_mv, s_rs, s_tmp, s_nrm, s_gam, s_x1, s_hid, s_b2,
         s_y, s_res, s_out) = ph.sems(
            "vectors_in staged xt exp_relu queries denominators reciprocals attended rows_made partial variance rstd sum "
            "normal gamma first_norm hidden bias_added second_rows beta_added group_done")
        NU = 4 + 4 + GT + 4 + 4 + 4
        turn = c.ledger.plan([j % 8 for j in range(NU)], NG)
        JQ, JT, JX, JH, JY = 4, 8, 8 + GT, 12 + GT, 16 + GT
        with nc.Block() as block:

            @block.sync
            def _(sp):
                for j, n in enumerate(("ln1_g", "ln1_b", "b2", "ln2_g", "ln2_b")):
                    sp.dma_start(vec[:, j, :], spread(a["L0_mix_" + n])).then_inc(s_in, 16)
                sp.dma_start(b1[:], a["L0_mix_b1"].rearrange("(h p) -> p h", p=P),
                             allow_slow_non_contiguous=True).then_inc(s_in, 16)

            @block.tensor
            def _(pe):
                with pe.Fori(0, NG) as g:
                    pe.wait_ge(s_stage, g + 1)
                    transposed(pe, c, lambda k, h: stage[:, k, h * P:(h + 1) * P], turn, 0, g)
                    pe.wait_ge(s_xt, g * 2 + 1)
                    for m in range(KH):
                        for n, (k0, w) in enumerate(CH):
                            b, t = turn(JQ + 2 * m + n, g)
                            pe.wait_ge(c.bank_free[b], t)
                            for h in range(KH):
                                ins = nc.tensor.matmul(c.bank[b][:, 0:w * P], wt[:, h, m * P:(m + 1) * P],
                                                       xt[:, h, k0 * P:(k0 + w) * P], start=(h == 0), stop=(h == KH - 1))
                            ins.then_inc(c.bank_full[b], 1)
                    pe.wait_ge(s_q, g * 4 + 4)
                    for k in range(GT):
                        b, t = turn(JT + k, g)
                        pe.wait_ge(c.bank_free[b], t)
                        for s in range(KH):
                            ins = nc.tensor.matmul(c.bank[b][:, s * (P + 4):(s + 1) * (P + 4)], et[:, s, k * P:(k + 1) * P],
                                                   kv[:, s, :], start=True, stop=True)
                        ins.then_inc(c.bank_full[b], 1)
                    pe.wait_ge(s_x1, g + 1)
                    transposed(pe, c, lambda k, h: u[:, k, h * P:(h + 1) * P], turn, JX, g)
                    pe.wait_ge(s_xt, g * 2 + 2)
                    for m in range(KH):
                        for n, (k0, w) in enumerate(CH):
                            b, t = turn(JH + 2 * m + n, g)
                            pe.wait_ge(c.bank_free[b], t)
                            for h in range(KH):
                                ins = nc.tensor.matmul(c.bank[b][:, 0:w * P], wt[:, h, 3 * D + m * P:3 * D + (m + 1) * P],
                                                       xt[:, h, k0 * P:(k0 + w) * P], start=(h == 0), stop=(h == KH - 1))
                            ins.then_inc(c.bank_full[b], 1)
                    pe.wait_ge(s_hid, g * 4 + 4)
                    for n in range(4):
                        b, t = turn(JY + n, g)
                        pe.wait_ge(c.bank_free[b], t)
                        for k in range(2 * n, min(2 * n + 2, GT)):
                            for h in range(KH):
                                ins = nc.tensor.matmul(c.bank[b][:, (k % 2) * D:(k % 2 + 1) * D], et[:, h, k * P:(k + 1) * P],
                                                       wt[:, h, 4 * D:5 * D], start=(h == 0), stop=(h == KH - 1))
                        ins.then_inc(c.bank_full[b], 1)

            @block.scalar
            def _(act):
                act.wait_ge(s_in, 96)
                with act.Fori(0, NG) as g:
                    act.wait_ge(s_out, g + 1)
                    gate(act, c)
                    nc.scalar.copy(stage[:], group(c.xn, g)).then_inc(s_stage, 1)
                    evacuate_transposed(act, c, xt, turn, 0, g, s_xt)
                    for m in range(KH):
                        for n, (k0, w) in enumerate(CH):
                            b, t = turn(JQ + 2 * m + n, g)
                            r = slice(k0 * P, (k0 + w) * P)
                            act.wait_ge(c.bank_full[b], t)
                            nc.scalar.activation(et[:, m, r], c.bank[b][:, 0:w * P], ACT.Exp).then_inc(s_er, 1)
                            nc.scalar.activation(rt[:, m, r], c.bank[b][:, 0:w * P], ACT.Relu).then_inc(s_er, 1)
                            act.wait_ge(s_er, g * 8 + (4 * m + 2 * n + 2))
                            act.sem_inc(c.bank_free[b], 1)
                    evacuate_transposed(act, c, xt, turn, JX, g, s_xt)
                    for m in range(KH):
                        for n, (k0, w) in enumerate(CH):
                            b, t = turn(JH + 2 * m + n, g)
                            r = slice(k0 * P, (k0 + w) * P)
                            act.wait_ge(c.bank_full[b], t)
                            nc.scalar.activation(et[:, m, r], c.bank[b][:, 0:w * P], ACT.Gelu, bias=b1[:, m:m + 1])\
                                .then_inc(s_hid, 1)
                            act.wait_ge(s_hid, g * 4 + (2 * m + n + 1))
                            act.sem_inc(c.bank_free[b], 1)

            @block.gpsimd
            def _(pool):
                pool.wait_ge(s_in, 96)
                p = nc.gpsimd
                wide = lambda j: vec[:, j:j + 1, :].to_broadcast([P, GT, D])
                with pool.Fori(0, NG) as g:
                    rstd(pool, c, g * 2, s_mv, s_rs, s_tmp)
                    pool.wait_ge(s_nrm, g * (2 * GT) + GT)
                    p.tensor_tensor(u[:], u[:], wide(0), ALU.mult).then_inc(s_gam, 1)
                    gate(pool, c)
                    p.tensor_tensor(group(c.res, g), group(c.res, g), wide(4), ALU.add).then_inc(s_res, 1)
                    pool.wait_ge(s_xt, g * 2 + 2)
                    p.tensor_tensor(u[:], u[:], wide(2), ALU.add).then_inc(s_b2, 1)
                    rstd(pool, c, g * 2 + 1, s_mv, s_rs, s_tmp)
                    pool.wait_ge(s_nrm, g * (2 * GT) + 2 * GT)
                    p.tensor_tensor(u[:], u[:], wide(3), ALU.mult).then_inc(s_gam, 1)

            @block.vector
            def _(dve):
                v = nc.vector
                dve.sem_inc(s_out, 1)
                dve.wait_ge(s_in, 96)
                with dve.Fori(0, NG) as g:
                    for m in range(KH):
                        for n, (k0, w) in enumerate(CH):
                            r = slice(k0 * P, (k0 + w) * P)
                            dve.wait_ge(s_er, g * 8 + (4 * m + 2 * n + 2))
                            v.scalar_tensor_tensor(et[:, m, r], et[:, m, r], 1.0, rt[:, m, r], ALU.min, ALU.add).then_inc(s_q, 1)
                    for k in range(GT):
                        b, t = turn(JT + k, g)
                        dve.wait_ge(c.bank_full[b], t)
                        v.tensor_scalar(z[:, k, :, :], c.bank[b][:, 0:KH * (P + 4)].rearrange("p (s m) -> p s m", s=KH)[:, :, P:],
                                        1e-6, None, ALU.add).then_inc(s_den, 1)
                    dve.wait_ge(s_den, g * GT + GT)
                    v.reciprocal(z[:], z[:]).then_inc(s_rec, 1)
                    dve.wait_ge(s_rec, g + 1)
                    for k in range(GT):
                        b, t = turn(JT + k, g)
                        v.tensor_tensor(u[:, k, :].rearrange("p (s j m) -> p s j m", s=KH, j=4),
                                        c.bank[b][:, 0:KH * (P + 4)].rearrange("p (s m) -> p s m", s=KH)[:, :, 0:P]
                                        .rearrange("p s (j m) -> p s j m", j=4),
                                        z[:, k, :, :].unsqueeze(3).to_broadcast([P, KH, 4, 32]), ALU.mult).then_inc(s_t, 1)
                        dve.wait_ge(s_t, g * GT + (k + 1))
                        dve.sem_inc(c.bank_free[b], 1)
                    v.tensor_tensor(u[:], u[:], stage[:], ALU.add).then_inc(s_u, 1)
                    dve.wait_ge(s_u, g + 1)
                    gate(dve, c)
                    tile = lambda k: u[:, k, :]
                    stats(dve, c, tile, g * 2, s_bn, s_mv)
                    normalise(dve, c, tile, tile, g * 2, s_rs, s_nrm)
                    dve.wait_ge(s_gam, g * 2 + 1)
                    v.tensor_tensor(u[:], u[:], vec[:, 1:2, :].to_broadcast([P, GT, D]), ALU.add).then_inc(s_x1, 1)
                    dve.wait_ge(s_b2, g + 1)
                    for n in range(4):
                        b, t = turn(JY + n, g)
                        w = min(2, GT - 2 * n)
                        dve.wait_ge(c.bank_full[b], t)
                        x = u[:, 2 * n:2 * n + w, :].rearrange("p k c -> p (k c)")
                        v.tensor_tensor(x, x, c.bank[b][:, 0:w * D], ALU.add).then_inc(s_y, 1)
                        dve.wait_ge(s_y, g * 4 + (n + 1))
                        dve.sem_inc(c.bank_free[b], 1)
                    stats(dve, c, tile, g * 2 + 1, s_bn, s_mv)
                    normalise(dve, c, tile, tile, g * 2 + 1, s_rs, s_nrm)
                    dve.wait_ge(s_gam, g * 2 + 2)
                    dve.wait_ge(s_res, g + 1)
                    gate(dve, c)
                    v.tensor_tensor(group(c.res, g), group(c.res, g), u[:], ALU.add).then_inc(s_out, 1)


class Mlp:
    NU = 4 + 16 + 4
    BANKS = [j % 8 for j in range(NU)]

    def __init__(self, nc, c, ph, turn, stage, cut, w1, w2, b1, act_fn):
        self.nc, self.c, self.turn, self.stage, self.w1, self.w2, self.b1, self.fn = nc, c, turn, stage, w1, w2, b1, act_fn
        self.xt = cut(KH, GR)
        self.ht = [cut(8, w * P) for _, w in CH]
        self.s_xt, self.s_hid, self.s_used = ph.sems("mlp_xt mlp_hidden mlp_hidden_used")

    def tensor(self, pe, g):
        nc, c, turn = self.nc, self.c, self.turn
        transposed(pe, c, lambda k, h: self.stage[:, k, h * P:(h + 1) * P], turn, 0, g)
        pe.wait_ge(self.s_xt, g + 1)
        for n, (k0, w) in enumerate(CH):
            for m in range(8):
                b, t = turn(4 + 8 * n + m, g)
                pe.wait_ge(c.bank_free[b], t)
                for h in range(KH):
                    ins = nc.tensor.matmul(c.bank[b][:, 0:w * P], self.w1[:, h, m * P:(m + 1) * P],
                                           self.xt[:, h, k0 * P:(k0 + w) * P], start=(h == 0), stop=(h == KH - 1))
                ins.then_inc(c.bank_full[b], 1)
        for n, (k0, w) in enumerate(CH):
            pe.wait_ge(self.s_hid, g * 16 + (8 * n + 8))
            for r in range(2):
                b, t = turn(20 + 2 * n + r, g)
                pe.wait_ge(c.bank_free[b], t)
                for k in range(2 * r, min(2 * r + 2, w)):
                    for m in range(8):
                        ins = nc.tensor.matmul(c.bank[b][:, (k % 2) * D:(k % 2 + 1) * D], self.ht[n][:, m, k * P:(k + 1) * P],
                                               self.w2[:, m, :], start=(m == 0), stop=(m == 7))
                ins.then_inc(c.bank_full[b], 1)
        pe.wait_ge(c.bank_full[b], t)
        pe.sem_inc(self.s_used, 1)

    def scalar(self, act, g):
        nc, c, turn = self.nc, self.c, self.turn
        act.wait_ge(self.s_used, g + 1)
        evacuate_transposed(act, c, self.xt, turn, 0, g, self.s_xt)
        for n, (k0, w) in enumerate(CH):
            for m in range(8):
                b, t = turn(4 + 8 * n + m, g)
                act.wait_ge(c.bank_full[b], t)
                nc.scalar.activation(self.ht[n][:, m, :], c.bank[b][:, 0:w * P], self.fn, bias=self.b1[:, m:m + 1])\
                    .then_inc(self.s_hid, 1)
                act.wait_ge(self.s_hid, g * 16 + (8 * n + m + 1))
                act.sem_inc(c.bank_free[b], 1)

    def pairs(self):
        return [(20 + 2 * n + r, k0 + 2 * r, min(2, w - 2 * r)) for n, (k0, w) in enumerate(CH) for r in range(2)]


def ffn0(nc, c, a, score):
    with Phase(nc, "ffn0") as ph:
        cut = carver(c.agg)
        stage, junk = cut(GT, D), cut(D)
        w1, w2, b1 = ph.sb("w1", [P, KH, 4 * D]), ph.sb("w2", [P, 8, D]), ph.sb("b1", [P, 8])
        vec, br, sc = ph.sb("vec", [P, 2, D]), ph.sb("br", [P, 1]), ph.sb("sc", [P, GT])
        turn = c.ledger.plan(Mlp.BANKS, NG)
        mlp = Mlp(nc, c, ph, turn, stage, cut, w1, w2, b1, ACT.Gelu_apprx_tanh)
        s_in, s_x1, s_bn, s_mv, s_rs, s_tmp, s_nrm, s_sc, s_scb, s_base, s_yb, s_y = ph.sems(
            "weights_in sum_made partial variance rstd sum normal score score_biased base_made y_biased y_scaled")
        with nc.Block() as block:

            @block.sync
            def _(sp):
                for h in range(KH):
                    sp.dma_start(w1[:, h, :], a["L0_ffn_w1"][h * P:(h + 1) * P, :]).then_inc(s_in, 16)
                sp.dma_start(w2[:], a["L0_ffn_w2"].rearrange("(m p) o -> p m o", p=P)).then_inc(s_in, 16)
                sp.dma_start(b1[:], a["L0_ffn_b1"].rearrange("(m p) -> p m", p=P), allow_slow_non_contiguous=True).then_inc(s_in, 16)
                sp.dma_start(vec[:, 0, :], a["L0_ffn_wr"].rearrange("d o -> o d").to_broadcast([P, D]),
                             allow_slow_non_contiguous=True).then_inc(s_in, 16)
                sp.dma_start(vec[:, 1, :], spread(a["L0_ffn_b2"])).then_inc(s_in, 16)
                sp.dma_start(br[:], spread(a["L0_ffn_br"], 1)).then_inc(s_in, 16)

            @block.tensor
            def _(pe):
                pe.sem_inc(mlp.s_used, 1)
                pe.wait_ge(s_in, 7 * 16)
                with pe.Fori(0, NG) as g:
                    pe.wait_ge(s_nrm, (g + 1) * GT)
                    mlp.tensor(pe, g)

            @block.scalar
            def _(act):
                act.wait_ge(s_in, 7 * 16)
                with act.Fori(0, NG) as g:
                    mlp.scalar(act, g)

            @block.gpsimd
            def _(pool):
                with pool.Fori(0, NG) as g:
                    rstd(pool, c, g, s_mv, s_rs, s_tmp)

            @block.vector
            def _(dve):
                v = nc.vector
                dve.wait_ge(s_in, 7 * 16)
                with dve.Fori(0, NG) as g:
                    v.tensor_tensor(group(c.res, g), group(c.res, g), group(c.xn, g), ALU.add).then_inc(s_x1, 1)
                    dve.wait_ge(s_x1, g + 1)
                    gate(dve, c)
                    stats(dve, c, lambda k: tile_of(c.res, g, k), g, s_bn, s_mv)
                    normalise(dve, c, lambda k: stage[:, k, :], lambda k: tile_of(c.res, g, k), g, s_rs, s_nrm)
                    dve.wait_ge(s_nrm, (g + 1) * GT)
                    for k in range(GT):
                        if k:
                            dve.wait_ge(s_sc, g * GT + k)
                        v.tensor_tensor_reduce(junk, stage[:, k, :], vec[:, 0, :], 1.0, 0.0, ALU.mult, ALU.add,
                                               sc[:, k:k + 1]).then_inc(s_sc, 1)
                    dve.wait_ge(s_sc, g * GT + GT)
                    v.tensor_scalar(sc[:], sc[:], br[:, 0:1], None, ALU.add).then_inc(s_scb, 1)
                    dve.wait_ge(s_scb, g * 2 + 1)
                    v.tensor_scalar(score[:, ds(g * GT, GT)], sc[:], 1.0, None, ALU.mult).then_inc(s_scb, 1)
                    v.tensor_tensor(group(c.res, g), group(c.res, g), stage[:], ALU.add).then_inc(s_base, 1)
                    dve.wait_ge(s_base, g + 1)
                    for n, (j, k, w) in enumerate(mlp.pairs()):
                        b, t = turn(j, g)
                        dve.wait_ge(c.bank_full[b], t)
                        v.tensor_tensor(stage[:, k:k + w, :], c.bank[b][:, 0:w * D].rearrange("p (k d) -> p k d", d=D),
                                        vec[:, 1:2, :].to_broadcast([P, w, D]), ALU.add).then_inc(s_yb, 1)
                        dve.wait_ge(s_yb, g * 4 + (n + 1))
                        dve.sem_inc(c.bank_free[b], 1)
                        for i in range(k, k + w):
                            v.tensor_scalar(tile_of(c.xn, g, i), stage[:, i, :], sc[:, i:i + 1], None, ALU.mult).then_inc(s_y, 1)
                    dve.wait_ge(s_y, (g + 1) * GT)
                    gate(dve, c)


def select(nc, c, score, take):
    ROUNDS = 64
    with Phase(nc, "select") as ph:
        lo, hi, mid, cnt, up, dn, top = (ph.sb(n, [P, 1]) for n in ("lo", "hi", "mid", "cnt", "up", "dn", "top"))
        junk, above, equal, off, off2, lim = (ph.sb(n, [P, NT]) for n in ("junk", "above", "equal", "off", "off2", "lim"))
        before = ph.sb("before", [P, P])
        s_v, s_max, s_cnt, s_tot = ph.sems("vector_steps maximum counted totalled")
        s_hi, s_lo, s_mid, s_ud = ph.sems("high low middle up_down")
        s_rank, = ph.sems("ranked")
        turn = c.ledger.plan([0, 1], 1)
        with nc.Block() as block:

            @block.gpsimd
            def _(pool):
                pool.wait_ge(s_v, 2)
                nc.gpsimd.partition_all_reduce(hi[:], top[:], P, bass.bass_isa.ReduceOp.max).then_inc(s_max, 1)

            @block.tensor
            def _(pe):
                with pe.Fori(0, ROUNDS) as i:
                    pe.wait_ge(s_cnt, i + 1)
                    nc.tensor.matmul(c.bank[2][:, 0:1], c.ones[:], cnt[:], start=True, stop=True).then_inc(s_tot, 1)
                pe.wait_ge(s_rank, 1)
                nc.tensor.matmul(c.bank[0][:, 0:NT], before[:], equal[:], start=True, stop=True)
                nc.tensor.matmul(c.bank[0][:, 64:64 + NT], c.ones[:], equal[:], start=True, stop=True)
                nc.tensor.matmul(c.bank[0][:, 128:129], c.ones[:], cnt[:], start=True, stop=True).then_inc(c.bank_full[0], 1)

            @block.vector
            def _(dve):
                v = nc.vector
                done = [0]

                def then(ins):
                    done[0] += 1
                    ins.then_inc(s_v, 1)
                    dve.wait_ge(s_v, done[0])

                then(v.tensor_tensor(junk[:], score[:], c.real[:], ALU.mult))
                then(v.tensor_reduce(top[:], junk[:], AX.X, ALU.max, apply_absolute_value=True))
                then(v.tensor_scalar(off[:], c.real[:], -1.0, BIG, ALU.add, ALU.mult))
                then(v.tensor_tensor(score[:], junk[:], off[:], ALU.add))
                then(v.tensor_scalar(before[:], c.iota[:], c.row_no[:, 0:1], None, ALU.is_gt))
                dve.wait_ge(s_max, 1)
                then(v.tensor_scalar(lo[:], hi[:], -1.0, None, ALU.mult))
                then(v.tensor_scalar(hi[:], hi[:], 1.0001, 1e-30, ALU.mult, ALU.add))
                dve.sem_inc(s_hi, 1)
                dve.sem_inc(s_lo, 1)
                with dve.Fori(0, ROUNDS) as i:
                    dve.wait_ge(s_hi, i + 1)
                    dve.wait_ge(s_lo, i + 1)
                    v.tensor_scalar(mid[:], lo[:], hi[:, 0:1], 0.5, ALU.add, ALU.mult).then_inc(s_mid, 1)
                    dve.wait_ge(s_mid, i + 1)
                    v.tensor_scalar(junk[:], score[:], mid[:, 0:1], 0.0, ALU.is_ge, ALU.add, accum_out=cnt[:]).then_inc(s_cnt, 1)
                    dve.wait_ge(s_tot, i + 1)
                    v.tensor_scalar(up[:], c.bank[2][:, 0:1], float(KK), BIG, ALU.is_ge, ALU.mult).then_inc(s_ud, 1)
                    v.tensor_scalar(dn[:], c.bank[2][:, 0:1], float(KK), -BIG, ALU.is_lt, ALU.mult).then_inc(s_ud, 1)
                    dve.wait_ge(s_ud, i * 2 + 2)
                    v.scalar_tensor_tensor(hi[:], up[:], mid[:, 0:1], hi[:], ALU.add, ALU.min).then_inc(s_hi, 1)
                    v.scalar_tensor_tensor(lo[:], dn[:], mid[:, 0:1], lo[:], ALU.add, ALU.max).then_inc(s_lo, 1)
                dve.wait_ge(s_hi, ROUNDS + 1)
                dve.wait_ge(s_lo, ROUNDS + 1)
                then(v.tensor_scalar(above[:], score[:], hi[:, 0:1], 0.0, ALU.is_ge, ALU.add, accum_out=cnt[:]))
                then(v.tensor_scalar(equal[:], score[:], lo[:, 0:1], None, ALU.is_ge))
                v.tensor_tensor(equal[:], equal[:], above[:], ALU.subtract).then_inc(s_rank, 1)
                dve.wait_ge(c.bank_full[0], turn(0, 0)[1])
                then(v.tensor_copy(off[:], c.bank[0][:, 64:64 + NT]))
                x, y, s = off, off2, 1
                while s < NT:
                    then(v.tensor_copy(y[:, 0:s], x[:, 0:s]))
                    then(v.tensor_tensor(y[:, s:NT], x[:, s:NT], x[:, 0:NT - s], ALU.add))
                    x, y, s = y, x, 2 * s
                then(v.tensor_tensor(x[:], x[:], c.bank[0][:, 64:64 + NT], ALU.subtract))
                then(v.tensor_tensor(x[:], x[:], c.bank[0][:, 0:NT], ALU.add))
                then(v.tensor_scalar(x[:], x[:], c.bank[0][:, 128:129], float(KK), ALU.add, ALU.is_lt))
                then(v.tensor_tensor(x[:], x[:], equal[:], ALU.mult))
                then(v.tensor_tensor(take[:], x[:], above[:], ALU.add))
                dve.sem_inc(c.bank_free[0], 1)
                dve.sem_inc(c.bank_free[1], 1)
                dve.sem_inc(c.bank_full[1], 1)


def weights1(nc, c, a, names, nat, wt):
    J = len(names)
    with Phase(nc, "weights1" + names[0]) as ph:
        s_in, = ph.sems("natural_in")
        turn = c.ledger.plan(list(range(J)), 1)
        with nc.Block() as block:

            @block.sync
            def _(sp):
                for j, n in enumerate(names):
                    sp.dma_start(nat[:, 2 * j:2 * j + 2, :], a["L1_mix_" + n].rearrange("(b p) i -> p b i", p=P)).then_inc(s_in, 16)

            @block.tensor
            def _(pe):
                pe.wait_ge(s_in, 16 * J)
                for j in range(J):
                    b, t = turn(j, 0)
                    pe.wait_ge(c.bank_free[b], t)
                    for h in range(KH):
                        for n in range(2):
                            ins = nc.tensor.transpose(c.bank[b][:, (2 * h + n) * P:(2 * h + n + 1) * P],
                                                      nat[:, 2 * j + n, h * P:(h + 1) * P], c.ident[:])
                    ins.then_inc(c.bank_full[b], 1)

            @block.scalar
            def _(act):
                for j in range(J):
                    b, t = turn(j, 0)
                    act.wait_ge(c.bank_full[b], t)
                    nc.scalar.copy(wt[:, :, j * D:(j + 1) * D],
                                   c.bank[b][:].rearrange("p (h o) -> p h o", h=KH)).then_inc(c.bank_free[b], 1)


def tables1(nc, c, a, take):
    W = a["L1_gnn_weight"]
    with Phase(nc, "tables1") as ph:
        cut = carver(c.agg)
        stage, xt, outs = cut(GT, D), cut(KH, GR), cut(4, 4 * D)
        w = ph.sb("w", [P, KH, REL1 * D])
        s_in, s_xt, s_half, s_half2, s_xtu, s_copy, s_x2, s_bn, s_mv, s_rs, s_tmp, s_nrm, s_msk = ph.sems(
            "weights_in xt halves_made other_halves_made xt_used copied x_made partial variance rstd sum normal masked")
        s_store = [ph.sem(f"stored{o}") for o in range(4)]
        turn = c.ledger.plan([j % 8 for j in range(4 + 4 * GT)], NG)
        per = [4, 4, 3, 3]
        with nc.Block() as block:

            @block.sync
            def _(sp):
                for h in range(KH):
                    sp.dma_start(w[:, h, :].rearrange("p (r o) -> p r o", r=REL1),
                                 W[:, h * P:(h + 1) * P, :].rearrange("r p o -> p r o")).then_inc(s_in, 16)
                for o in range(4):
                    sp.sem_inc(s_store[o], 16)
                tab = c.tab1_d.rearrange("(r n) d -> n r d", n=NP)
                with sp.Fori(0, NG) as g:
                    for k in range(GT):
                        at = ds(g * GR + k * P, P)
                        for half, s in ((0, s_half), (1, s_half2)):
                            o = (k % 2) * 2 + half
                            sp.wait_ge(s, g * (2 * GT) + (2 * k + 2))
                            sp.dma_start(tab[at, 4 * half:4 * half + 4, :], outs[:, o, :].rearrange("p (r d) -> p r d", d=D))\
                                .then_inc(s_store[o], 16)
                for o in range(4):
                    sp.wait_ge(s_store[o], 16 + 16 * NG * per[o])

            @block.tensor
            def _(pe):
                pe.sem_inc(s_xtu, 1)
                pe.wait_ge(s_in, 32)
                with pe.Fori(0, NG) as g:
                    pe.wait_ge(s_nrm, (g + 1) * GT)
                    pe.wait_ge(s_msk, g + 1)
                    transposed(pe, c, lambda k, h: stage[:, k, h * P:(h + 1) * P], turn, 0, g)
                    pe.wait_ge(s_xt, g + 2)
                    for k in range(GT):
                        for j in range(4):
                            b, t = turn(4 + 4 * k + j, g)
                            pe.wait_ge(c.bank_free[b], t)
                            for h in range(KH):
                                ins = nc.tensor.matmul(c.bank[b][:], xt[:, h, k * P:(k + 1) * P], w[:, h, j * 512:(j + 1) * 512],
                                                       start=(h == 0), stop=(h == KH - 1))
                            ins.then_inc(c.bank_full[b], 1)
                    pe.wait_ge(c.bank_full[b], t)
                    pe.sem_inc(s_xtu, 1)

            def out(eng, copy, g, k, j, s):
                b, t = turn(4 + 4 * k + j, g)
                o = (k % 2) * 2 + j // 2
                if j % 2 == 0:
                    eng.wait_ge(s_store[o], (g * per[o] + k // 2 + 1) * 16)
                eng.wait_ge(c.bank_full[b], t)
                copy(outs[:, o, (j % 2) * 512:(j % 2 + 1) * 512], c.bank[b][:]).then_inc(s, 1)
                eng.wait_ge(s, g * (2 * GT) + (2 * k + j % 2 + 1))
                eng.sem_inc(c.bank_free[b], 1)

            @block.scalar
            def _(act):
                act.sem_inc(s_xt, 1)
                act.sem_inc(s_copy, 1)
                with act.Fori(0, NG) as g:
                    act.wait_ge(s_xtu, g + 1)
                    evacuate_transposed(act, c, xt, turn, 0, g, s_xt)
                    act.wait_ge(s_nrm, (g + 1) * GT)
                    act.wait_ge(s_msk, g + 1)
                    gate(act, c)
                    nc.scalar.copy(group(c.xn, g), stage).then_inc(s_copy, 1)
                    for k in range(GT):
                        for j in range(2):
                            out(act, nc.scalar.copy, g, k, j, s_half)

            @block.gpsimd
            def _(pool):
                with pool.Fori(0, NG) as g:
                    rstd(pool, c, g, s_mv, s_rs, s_tmp)

            @block.vector
            def _(dve):
                v = nc.vector

                def norm(g):
                    for k in range(GT):
                        v.scalar_tensor_tensor(tile_of(c.res, g, k), tile_of(c.xn, g, k), take[:, ds(g * GT + k, 1)],
                                               tile_of(c.res, g, k), ALU.mult, ALU.add).then_inc(s_x2, 1)
                    dve.wait_ge(s_x2, (g + 1) * GT)
                    gate(dve, c)
                    stats(dve, c, lambda k: tile_of(c.res, g, k), g, s_bn, s_mv)
                    dve.wait_ge(s_copy, g + 1)
                    dve.wait_ge(s_xt, g + 1)
                    normalise(dve, c, lambda k: stage[:, k, :], lambda k: tile_of(c.res, g, k), g, s_rs, s_nrm)
                    dve.wait_ge(s_nrm, (g + 1) * GT)
                    last = stage[:, GT - 1, :]
                    gate(dve, c)
                    v.tensor_scalar(last, last, c.real[:, ds(g * GT + (GT - 1), 1)], None, ALU.mult).then_inc(s_msk, 1)

                def outs_of(g, k):
                    for j in range(2, 4):
                        out(dve, v.tensor_copy, g, k, j, s_half2)

                norm(0)
                with dve.Fori(0, NG - 1) as g:
                    for k in range(GT):
                        outs_of(g, k)
                        if k == 1:
                            norm(g + 1)
                for k in range(GT):
                    outs_of(NG - 1, k)


class Keys1:
    HD, NH = 64, 8

    def __init__(self, nc, c, ph, wt):
        self.nc, self.c, self.wt = nc, c, wt
        NH = self.NH
        self.x, self.xt = ph.sb("x", [P, D]), ph.sb("xt", [P, KH, P])
        self.hat = ph.sb("hat", [P, NH, self.HD])
        self.bn, self.mv = ph.sb("kv_bn", [P, NH, 6]), ph.sb("kv_mv", [P, NH, 2])
        self.ve, self.rs, self.eps, self.power, self.neg, self.shift = (
            ph.sb(n, [P, NH]) for n in ("kv_ve", "kv_rs", "kv_eps", "kv_pow", "kv_neg", "kv_shift"))
        self.zero = ph.sb("zero", [P, D + KH])
        (self.s_set, self.s_x, self.s_turned, self.s_xt, self.s_kv, self.s_bn, self.s_mv, self.s_ve, self.s_rs, self.s_hat,
         self.s_sum, self.s_neg, self.s_pow) = ph.sems("kv_set tile_staged tile_turned tile_xt keys_made keys_partial keys_variance keys_steps keys_rstd "
                               "keys_normal keys_summed means_negated powers")

    def scalar(self, act, i, first, second):
        if first:
            self.stage(act, i)
        if second:
            act.wait_ge(self.s_sum, i)
            act.wait_ge(self.s_rs, i)
            for n in range(self.NH):
                self.nc.scalar.activation(self.hat[:, n, :], self.c.bank[1][:, n * self.HD:(n + 1) * self.HD], ACT.Identity,
                                          bias=self.shift[:, n:n + 1], scale=self.rs[:, n:n + 1]).then_inc(self.s_hat, 1)

    def stage(self, act, i):
        act.wait_ge(self.s_turned, i + 1)
        gate(act, self.c)
        self.nc.scalar.copy(self.x[:], self.c.xn[:, ds(i * D, D)]).then_inc(self.s_x, 1)
        act.wait_ge(self.s_turned, i + 2)
        act.wait_ge(self.s_kv, i + 1)
        self.nc.scalar.copy(self.xt[:].rearrange("p h r -> p (h r)"), self.c.bank[0][:, 0:D]).then_inc(self.s_xt, 1)

    def begin_tensor(self, pe):
        t = self.nc.tensor
        pe.sem_inc(self.s_turned, 1)
        pe.sem_inc(self.s_kv, 1)
        pe.sem_inc(self.s_sum, 1)
        pe.wait_ge(self.s_set, 3)
        t.matmul(self.c.bank[2][:, 0:D + KH], self.c.ones[:], self.zero[:], start=True, stop=False)
        t.matmul(self.c.bank[3][:, 0:D], self.c.ones[:], self.zero[:, 0:D], start=True, stop=False)

    def end_tensor(self, pe):
        t = self.nc.tensor
        t.matmul(self.c.bank[2][:, 0:D + KH], self.c.ones[:], self.zero[:], start=False, stop=True)
        t.matmul(self.c.bank[3][:, 0:D], self.c.ones[:], self.zero[:, 0:D], start=False, stop=True).then_inc(self.s_sum, 1)

    def turn(self, pe, i):
        pe.wait_ge(self.s_x, i + 1)
        gate(pe, self.c)
        for h in range(KH):
            ins = self.nc.tensor.transpose(self.c.bank[0][:, h * P:(h + 1) * P], self.x[:, h * P:(h + 1) * P], self.c.ident[:])
        ins.then_inc(self.s_turned, 1)

    def keys(self, pe, i):
        pe.wait_ge(self.s_xt, i + 1)
        pe.wait_ge(self.s_hat, i * self.NH + 1)
        for h in range(KH):
            ins = self.nc.tensor.matmul(self.c.bank[1][:], self.xt[:, h, :], self.wt[:, h, :], start=(h == 0), stop=(h == KH - 1))
        ins.then_inc(self.s_kv, 1)

    def sums(self, pe, i):
        t, c = self.nc.tensor, self.c
        flat = self.hat[:].rearrange("p i e -> p (i e)")
        pe.wait_ge(self.s_hat, (i + 1) * self.NH + 1)
        for s in range(KH):
            vs = flat[:, D + s * P:D + (s + 1) * P]
            t.matmul(c.bank[2][:, s * P:(s + 1) * P], vs, flat[:, s * P:(s + 1) * P], start=False, stop=False)
            t.matmul(c.bank[2][:, D + s:D + s + 1], vs, c.ones[:, 0:1], start=False, stop=False)
        t.matmul(c.bank[3][:, 0:D], c.ones[:], flat[:, 0:D], start=False, stop=False).then_inc(self.s_sum, 1)

    def tensor(self, pe, i, first, second):
        def after(s):
            if s == 1 and first:
                self.turn(pe, i)
            if s == 8 and second:
                self.sums(pe, i - 1)
            if s == 10 and first:
                self.keys(pe, i)
        return after

    def gpsimd(self, pool, i, second):
        p, c = self.nc.gpsimd, self.c

        def after(s):
            if s == 4 and second:
                pool.wait_ge(self.s_mv, i * self.NH)
                p.tensor_tensor(self.ve[:], self.mv[:, :, 1], self.eps[:], ALU.add).then_inc(self.s_ve, 1)
                pool.wait_ge(self.s_ve, i)
                pool.wait_ge(self.s_hat, (i - 1) * self.NH + 1)
                p.tensor_tensor(self.rs[:], self.ve[:], self.power[:], ALU.pow).then_inc(self.s_pow, 1)
                pool.wait_ge(self.s_pow, i)
                pool.wait_ge(self.s_neg, i)
                p.tensor_tensor(self.shift[:], self.neg[:], self.rs[:], ALU.mult).then_inc(self.s_rs, 1)
        return after

    def begin_vector(self, dve):
        v = self.nc.vector
        dve.sem_inc(self.s_hat, 1)
        v.memset(self.eps[:], EPS).then_inc(self.s_set, 1)
        v.memset(self.power[:], -0.5).then_inc(self.s_set, 1)
        v.memset(self.zero[:], 0.0).then_inc(self.s_set, 1)

    def vector(self, dve, i, first):
        v, c, NH = self.nc.vector, self.c, self.NH
        kv = c.bank[1][:].rearrange("p (i e) -> p i e", i=NH)

        def after(s):
            if s == 13 and first:
                dve.wait_ge(self.s_kv, i + 2)
                for n in range(NH):
                    v.bn_stats(self.bn[:, n, :], kv[:, n, :]).then_inc(self.s_bn, 1)
                dve.wait_ge(self.s_bn, (i + 1) * NH)
                gate(dve, c)
                for n in range(NH):
                    v.bn_aggr(self.mv[:, n, :], self.bn[:, n, :]).then_inc(self.s_mv, 1)
                dve.wait_ge(self.s_mv, (i + 1) * NH)
                v.tensor_scalar(self.neg[:], self.mv[:, :, 0], -1.0, None, ALU.mult).then_inc(self.s_neg, 1)
        return after


def gnn1(nc, c, wt, acc):
    with Phase(nc, "gnn1") as ph:
        msg, hot, row_ring, meta_ring = (ph.sb(n, s, d) for n, s, d in (
            ("msg", [P, SLOTS, D], F32), ("hot", [P, SLOTS, P], F32), ("row_ring", [P, 2, HALF], I32),
            ("meta_ring", [P, 2, HALF, 2], F32)))
        edges = c.edges
        edges.use(msg, hot, row_ring, meta_ring, c.row4, c.tab1_d, False)
        keys = Keys1(nc, c, ph, wt)
        s_in, s_zero, s_agg, s_acc = ph.sems("rows_in cleared sums_cleared sums_read")
        n0 = DEPTH * BODIES
        assert BODIES > NT + 1

        def bodies(eng, body):
            body(0, True, False)
            with eng.Fori(1, NT) as i:
                body(i, True, True)
            body(NT, False, True)
            with eng.Fori(NT + 1, BODIES) as i:
                body(i, False, False)

        with nc.Block() as block:

            @block.sync
            def _(sp):
                sp.dma_start(c.row4[:], c.row8_d).then_inc(s_in, 16)

            @block.tensor
            def _(pe):
                keys.begin_tensor(pe)
                bodies(pe, lambda i, first, second: edges.tensor(pe, i + n0, keys.tensor(pe, i, first, second)))
                keys.end_tensor(pe)

            @block.scalar
            def _(act):
                act.wait_ge(s_in, 16)
                gate(act, c)

                def body(i, first, second):
                    edges.scalar(act, i, i + n0)
                    keys.scalar(act, i, first, second)

                bodies(act, body)

            @block.gpsimd
            def _(pool):
                nc.gpsimd.memset(msg[:], 0.0).then_inc(s_zero, 1)
                pool.wait_ge(s_zero, 1)
                pool.wait_ge(keys.s_set, 3)
                gate(pool, c)
                bodies(pool, lambda i, first, second: edges.gpsimd(pool, i + n0, keys.gpsimd(pool, i, second)))

            @block.vector
            def _(dve):
                keys.begin_vector(dve)
                nc.vector.memset(c.agg[:], 0.0).then_inc(s_agg, 1)
                dve.wait_ge(s_agg, 1)
                gate(dve, c)
                bodies(dve, lambda i, first, second: edges.vector(dve, i, i + n0, keys.vector(dve, i, first)))
                dve.wait_ge(keys.s_sum, NT + 2)
                nc.vector.tensor_copy(acc[:, 0:D + KH], c.bank[2][:, 0:D + KH]).then_inc(s_acc, 1)
                nc.vector.tensor_copy(acc[:, D + KH:], c.bank[3][:, 0:D]).then_inc(s_acc, 1)


def mix1_matrix(nc, c, a, acc, wo, mx):
    HD = Keys1.HD
    with Phase(nc, "matrix1") as ph:
        wq, t1, bd = ph.sb("wq", [P, KH, D]), ph.sb("t1", [P, KH, D]), ph.sb("bd", [P, KH, P])
        gk, bk, s1, s2 = (ph.sb(n, [P, P]) for n in ("gk", "bk", "s1", "s2"))
        gv = ph.sb("gv", [P, 2])
        s_in, s_v, s_m = ph.sems("weights_in vector_steps factors_made")
        tail = c.ledger.plan([0, 1], 1)
        with nc.Block() as block:

            @block.sync
            def _(sp):
                for h in range(2):
                    r = slice(h * HD, (h + 1) * HD)
                    sp.dma_start(gk[:, r], spread(a["L1_mix_ln_k_g"], HD)).then_inc(s_in, 16)
                    sp.dma_start(bk[:, r], spread(a["L1_mix_ln_k_b"], HD)).then_inc(s_in, 16)
                    for j, n in enumerate(("g", "b")):
                        sp.dma_start(gv[r, j:j + 1], a["L1_mix_ln_v_" + n].rearrange("(p a) -> p a", a=1)).then_inc(s_in, 16)
                sp.dma_start(wq[:], a["L1_mix_wq"].rearrange("(b p) i -> p b i", p=P)).then_inc(s_in, 16)

            @block.vector
            def _(dve):
                v = nc.vector
                done = [0]

                def then(ins):
                    done[0] += 1
                    ins.then_inc(s_v, 1)
                    dve.wait_ge(s_v, done[0])

                then(v.memset(bd[:], 0.0))
                dve.wait_ge(s_in, 9 * 16)
                for s in range(KH):
                    then(v.tensor_tensor(s1[:], acc[:, s * P:(s + 1) * P], gk[:], ALU.mult))
                    then(v.scalar_tensor_tensor(s1[:], bk[:], acc[:, D + s:D + s + 1], s1[:], ALU.mult, ALU.add))
                    then(v.tensor_tensor(s2[:], acc[:, D + 2 + s * P:D + 2 + (s + 1) * P], gk[:], ALU.mult))
                    then(v.scalar_tensor_tensor(s2[:], bk[:], float(N), s2[:], ALU.mult, ALU.add))
                    then(v.tensor_scalar(s1[:], s1[:], gv[:, 0:1], 1.0 / N, ALU.mult, ALU.mult))
                    then(v.tensor_scalar(s2[:], s2[:], gv[:, 1:2], 1.0 / N, ALU.mult, ALU.mult))
                    then(v.tensor_tensor(s1[:], s1[:], s2[:], ALU.add))
                    for j in range(2):
                        r = slice(j * HD, (j + 1) * HD)
                        then(v.tensor_copy(bd[r, s, r], s1[r, r]))
                dve.sem_inc(s_m, 1)
                for j, to in enumerate((t1, mx)):
                    b, t = tail(j, 0)
                    dve.wait_ge(c.bank_full[b], t)
                    then(v.tensor_copy(to[:].rearrange("p s o -> p (s o)"), c.bank[b][:]))
                    dve.sem_inc(c.bank_free[b], 1)
                    dve.sem_inc(s_m, 1)

            @block.tensor
            def _(pe):
                pe.wait_ge(s_m, 1)
                b, t = tail(0, 0)
                pe.wait_ge(c.bank_free[b], t)
                for s in range(KH):
                    ins = nc.tensor.matmul(c.bank[b][:, s * D:(s + 1) * D], bd[:, s, :], wo[:, s, :], start=True, stop=True)
                ins.then_inc(c.bank_full[b], 1)
                pe.wait_ge(s_m, 2)
                pe.wait_ge(s_in, 9 * 16)
                b, t = tail(1, 0)
                pe.wait_ge(c.bank_free[b], t)
                for h in range(KH):
                    for s in range(KH):
                        ins = nc.tensor.matmul(c.bank[b][:, h * D:(h + 1) * D], wq[:, s, h * P:(h + 1) * P], t1[:, s, :],
                                               start=(s == 0), stop=(s == KH - 1))
                ins.then_inc(c.bank_full[b], 1)


def batch_norm(nc, c, a, scale):
    with Phase(nc, "batch") as ph:
        sq = ph.sb("sq", [P, GT, D])
        acc, mean, gam, eps, power = (ph.sb(n, [P, D]) for n in ("acc", "mean", "gam", "eps", "power"))
        s_in, s_acc, s_v, s_cen, s_msk, s_sq, s_squ, s_p, s_mean = ph.sems(
            "gamma_in accumulated vector_steps centred masked squares squares_used pool_steps mean_made")
        turn = c.ledger.plan([0], NG)
        turn2 = c.ledger.plan([1], NG)
        with nc.Block() as block:

            @block.sync
            def _(sp):
                sp.dma_start(gam[:], spread(a["L1_gnn_gamma"])).then_inc(s_in, 16)

            @block.tensor
            def _(pe):
                pe.sem_inc(s_squ, 1)
                with pe.Fori(0, NG) as g:
                    b, t = turn(0, g)
                    pe.wait_ge(c.bank_free[b], t)
                    gate(pe, c)
                    for k in range(GT):
                        ins = nc.tensor.matmul(c.bank[b][:, 0:D], c.ones[:], tile_of(c.agg, g, k), start=(k == 0), stop=(k == GT - 1))
                    ins.then_inc(c.bank_full[b], 1)
                with pe.Fori(0, NG) as g:
                    b, t = turn2(0, g)
                    pe.wait_ge(c.bank_free[b], t)
                    pe.wait_ge(s_sq, g + 1)
                    for k in range(GT):
                        ins = nc.tensor.matmul(c.bank[b][:, 0:D], c.ones[:], sq[:, k, :], start=(k == 0), stop=(k == GT - 1))
                    ins.then_inc(c.bank_full[b], 1)
                    pe.wait_ge(c.bank_full[b], t)
                    pe.sem_inc(s_squ, 1)

            @block.scalar
            def _(act):
                with act.Fori(0, NG) as g:
                    act.wait_ge(s_msk, g + 1)
                    act.wait_ge(s_squ, g + 1)
                    gate(act, c)
                    nc.scalar.activation(sq[:], group(c.agg, g), ACT.Square).then_inc(s_sq, 1)

            @block.vector
            def _(dve):
                v = nc.vector
                v.memset(acc[:], 0.0).then_inc(s_acc, 1)
                v.memset(eps[:], EPS).then_inc(s_v, 1)
                v.memset(power[:], -0.5).then_inc(s_v, 1)

                def add_up(turn_, g, n):
                    b, t = turn_(0, g)
                    dve.wait_ge(c.bank_full[b], t)
                    dve.wait_ge(s_acc, g + n)
                    v.tensor_tensor(acc[:], acc[:], c.bank[b][:, 0:D], ALU.add).then_inc(s_acc, 1)
                    dve.wait_ge(s_acc, g + (n + 1))
                    dve.sem_inc(c.bank_free[b], 1)

                with dve.Fori(0, NG) as g:
                    add_up(turn, g, 1)
                v.tensor_scalar(mean[:], acc[:], 1.0 / N, None, ALU.mult).then_inc(s_mean, 1)
                dve.wait_ge(s_mean, 1)
                v.memset(acc[:], 0.0).then_inc(s_mean, 1)
                dve.wait_ge(s_mean, 2)
                gate(dve, c)
                with dve.Fori(0, NG) as g:
                    v.tensor_tensor(group(c.agg, g), group(c.agg, g), mean[:].unsqueeze(1).to_broadcast([P, GT, D]),
                                    ALU.subtract).then_inc(s_cen, 1)
                    dve.wait_ge(s_cen, g + 1)
                    last = tile_of(c.agg, g, GT - 1)
                    v.tensor_scalar(last, last, c.real[:, ds(g * GT + (GT - 1), 1)], None, ALU.mult).then_inc(s_msk, 1)
                    add_up(turn2, g, NG + 1)
                dve.wait_ge(s_v, 2)
                v.tensor_scalar(acc[:], acc[:], 1.0 / N, None, ALU.mult).then_inc(s_v, 1)
                dve.wait_ge(s_p, 2)
                dve.wait_ge(s_in, 16)
                v.tensor_tensor(scale[:], acc[:], gam[:], ALU.mult).then_inc(s_v, 1)

            @block.gpsimd
            def _(pool):
                pool.wait_ge(s_v, 3)
                nc.gpsimd.tensor_tensor(acc[:], acc[:], eps[:], ALU.add).then_inc(s_p, 1)
                pool.wait_ge(s_p, 1)
                nc.gpsimd.tensor_tensor(acc[:], acc[:], power[:], ALU.pow).then_inc(s_p, 1)


def mix1_main(nc, c, a, scale, mx, total):
    with Phase(nc, "mix1") as ph:
        stage, nrm = ph.sb("stage", [P, GT, D]), ph.sb("norm", [P, GT, D])
        xt = ph.sb("xt", [P, KH, GR])
        bias, bo = ph.sb("bias", [P, 1, D]), ph.sb("bo", [P, 1, D])
        (s_in, s_bias, s_stage, s_xt, s_xtu, s_sc, s_bb, s_r, s_y, s_bn, s_mv, s_rs, s_tmp, s_nrm, s_msk, s_copy, s_acc,
         s_nu) = ph.sems("vectors_in bias_made staged xt xt_used scaled biased sum_made products_added partial variance rstd "
                         "sum normal masked copied accumulated norm_used")
        turn = c.ledger.plan([j % 8 for j in range(4 + 4)] + [0], NG)
        with nc.Block() as block:

            @block.sync
            def _(sp):
                sp.dma_start(bias[:, 0, :], spread(a["L1_gnn_beta"])).then_inc(s_in, 16)
                sp.dma_start(bo[:, 0, :], spread(a["L1_mix_bo"])).then_inc(s_in, 16)

            @block.tensor
            def _(pe):
                pe.sem_inc(s_xtu, 1)
                pe.sem_inc(s_nu, 1)
                with pe.Fori(0, NG) as g:
                    pe.wait_ge(s_stage, g + 1)
                    transposed(pe, c, lambda k, h: stage[:, k, h * P:(h + 1) * P], turn, 0, g)
                    pe.wait_ge(s_xt, g + 1)
                    for n in range(4):
                        b, t = turn(4 + n, g)
                        pe.wait_ge(c.bank_free[b], t)
                        for k in range(2 * n, min(2 * n + 2, GT)):
                            for h in range(KH):
                                ins = nc.tensor.matmul(c.bank[b][:, (k % 2) * D:(k % 2 + 1) * D], xt[:, h, k * P:(k + 1) * P],
                                                       mx[:, h, :], start=(h == 0), stop=(h == KH - 1))
                        ins.then_inc(c.bank_full[b], 1)
                    pe.wait_ge(c.bank_full[b], t)
                    pe.sem_inc(s_xtu, 1)
                    b, t = turn(8, g)
                    pe.wait_ge(c.bank_free[b], t)
                    pe.wait_ge(s_nrm, (g + 1) * GT)
                    pe.wait_ge(s_msk, g + 1)
                    for k in range(GT):
                        ins = nc.tensor.matmul(c.bank[b][:, 0:D], c.ones[:], nrm[:, k, :], start=(k == 0), stop=(k == GT - 1))
                    ins.then_inc(c.bank_full[b], 1)
                    pe.wait_ge(c.bank_full[b], t)
                    pe.sem_inc(s_nu, 1)

            @block.scalar
            def _(act):
                with act.Fori(0, NG) as g:
                    act.wait_ge(s_xtu, g + 1)
                    gate(act, c)
                    nc.scalar.copy(stage[:], group(c.xn, g)).then_inc(s_stage, 1)
                    evacuate_transposed(act, c, xt, turn, 0, g, s_xt)
                    act.wait_ge(s_msk, g + 1)
                    gate(act, c)
                    nc.scalar.copy(group(c.xn, g), nrm[:]).then_inc(s_copy, 1)

            @block.gpsimd
            def _(pool):
                p = nc.gpsimd
                pool.wait_ge(s_in, 32)
                p.tensor_tensor(bias[:], bias[:], bo[:], ALU.add).then_inc(s_bias, 1)
                pool.wait_ge(s_bias, 1)
                gate(pool, c)
                with pool.Fori(0, NG) as g:
                    x = group(c.agg, g)
                    p.tensor_tensor(x, x, scale[:].unsqueeze(1).to_broadcast([P, GT, D]), ALU.mult).then_inc(s_sc, 1)
                    pool.wait_ge(s_sc, g + 1)
                    gate(pool, c)
                    p.tensor_tensor(x, x, bias[:].to_broadcast([P, GT, D]), ALU.add).then_inc(s_bb, 1)
                    rstd(pool, c, g, s_mv, s_rs, s_tmp)

            @block.vector
            def _(dve):
                v = nc.vector
                v.memset(total[:], 0.0).then_inc(s_acc, 1)
                with dve.Fori(0, NG) as g:
                    dve.wait_ge(s_bb, g + 1)
                    v.tensor_tensor(group(c.res, g), group(c.res, g), group(c.agg, g), ALU.add).then_inc(s_r, 1)
                    dve.wait_ge(s_r, g + 1)
                    for n in range(4):
                        b, t = turn(4 + n, g)
                        w = min(2, GT - 2 * n)
                        dve.wait_ge(c.bank_full[b], t)
                        x = tile_of(c.res, g, 2 * n, 0, w * D)
                        v.tensor_tensor(x, x, c.bank[b][:, 0:w * D], ALU.add).then_inc(s_y, 1)
                        dve.wait_ge(s_y, g * 4 + (n + 1))
                        dve.sem_inc(c.bank_free[b], 1)
                    stats(dve, c, lambda k: tile_of(c.res, g, k), g, s_bn, s_mv)
                    dve.wait_ge(s_nu, g + 1)
                    normalise(dve, c, lambda k: nrm[:, k, :], lambda k: tile_of(c.res, g, k), g, s_rs, s_nrm)
                    dve.wait_ge(s_nrm, (g + 1) * GT)
                    v.tensor_scalar(nrm[:, GT - 1, :], nrm[:, GT - 1, :], c.real[:, ds(g * GT + (GT - 1), 1)], None,
                                    ALU.mult).then_inc(s_msk, 1)
                    b, t = turn(8, g)
                    dve.wait_ge(c.bank_full[b], t)
                    dve.wait_ge(s_acc, g + 1)
                    v.tensor_tensor(total[:], total[:], c.bank[b][:, 0:D], ALU.add).then_inc(s_acc, 1)
                    dve.wait_ge(s_acc, g + 2)
                    dve.sem_inc(c.bank_free[b], 1)
                    dve.wait_ge(s_copy, g + 1)


def router(nc, c, a, total, chosen, share):
    NE = 8
    CAP = float(-(-N * 5 // (4 * NE)))
    with Phase(nc, "router") as ph:
        wr = ph.sb("wr", [1, NE, D])
        em, junk = ph.sb("em", [1, D]), ph.sb("junk", [1, D])
        lg, br, ex = (ph.sb(n, [1, NE]) for n in ("lg", "br", "ex"))
        m1, sm = ph.sb("m1", [1, 1]), ph.sb("sm", [1, 1])
        gt, tri, rank = ph.sb("gt", [1, NE, NE]), ph.sb("tri", [1, NE, NE]), ph.sb("rank", [1, NE])
        two, pick, val = ph.sb("two", [1, 2, NE]), ph.sb("pick", [1, 2]), ph.sb("val", [1, 2])
        s_in, s_v, s_e, s_w, s_bc = ph.sems("weights_in vector_steps differences_made shares_made exponentials")
        turn = c.ledger.plan([0, 1], 1)
        with nc.Block() as block:

            @block.sync
            def _(sp):
                sp.dma_start(wr[:],
                             a["L1_ffn_Wr"].rearrange("(a d) e -> a e d", a=1), allow_slow_non_contiguous=True).then_inc(s_in, 16)
                sp.dma_start(br[:], a["L1_ffn_br"].rearrange("(a e) -> a e", a=1)).then_inc(s_in, 16)

            @block.tensor
            def _(pe):
                pe.wait_ge(s_w, 1)
                nc.tensor.matmul(c.bank[0][:, 0:2], c.ones[0:1, :], val[:], start=True, stop=True).then_inc(c.bank_full[0], 1)
                pe.sem_inc(c.bank_full[1], 1)

            @block.scalar
            def _(act):
                act.wait_ge(s_e, 1)
                nc.scalar.activation(ex[:], lg[:], ACT.Exp).then_inc(s_bc, 1)
                act.wait_ge(s_e, 2)
                nc.scalar.activation(ex[:], lg[:], ACT.Exp).then_inc(s_bc, 1)
                act.wait_ge(s_e, 3)
                nc.scalar.activation(val[:], val[:], ACT.Exp).then_inc(s_bc, 1)

            @block.vector
            def _(dve):
                v = nc.vector
                done = [0]

                def then(ins):
                    done[0] += 1
                    ins.then_inc(s_v, 1)
                    dve.wait_ge(s_v, done[0])

                dve.wait_ge(s_in, 32)
                then(v.tensor_scalar(em[:], total[0:1, :], 1.0 / N, None, ALU.mult))
                for e in range(NE):
                    then(v.tensor_tensor_reduce(junk[:], em[:], wr[:, e, :], 1.0, 0.0, ALU.mult, ALU.add, lg[:, e:e + 1]))
                then(v.tensor_tensor(lg[:], lg[:], br[:], ALU.add))

                def softmax(n, x, y):
                    then(v.tensor_reduce(m1[:], x[:], AX.X, ALU.max))
                    then(v.tensor_scalar(x[:], x[:], m1[:, 0:1], None, ALU.subtract))
                    dve.sem_inc(s_e, 1)
                    dve.wait_ge(s_bc, n)
                    then(v.tensor_reduce(sm[:], y[:], AX.X, ALU.add))
                    then(v.reciprocal(sm[:], sm[:]))
                    then(v.tensor_scalar(x[:], y[:], sm[:, 0:1], None, ALU.mult))

                softmax(1, lg, ex)
                then(v.tensor_scalar(lg[:], lg[:], CAP / N, None, ALU.min))
                softmax(2, lg, ex)
                me = lg[:].unsqueeze(2).to_broadcast([1, NE, NE])
                other = lg[:].unsqueeze(1).to_broadcast([1, NE, NE])
                no = c.iota[0:1, 0:NE]
                then(v.tensor_tensor(gt[:], other, me, ALU.is_equal))
                then(v.tensor_tensor(tri[:], no.unsqueeze(1).to_broadcast([1, NE, NE]), no.unsqueeze(2).to_broadcast([1, NE, NE]),
                                     ALU.is_lt))
                then(v.tensor_tensor(tri[:], tri[:], gt[:], ALU.mult))
                then(v.tensor_tensor(gt[:], other, me, ALU.is_gt))
                then(v.tensor_tensor(gt[:], gt[:], tri[:], ALU.add))
                then(v.tensor_reduce(rank[:], gt[:], AX.X, ALU.add))
                then(v.tensor_tensor(two[:], rank[:].unsqueeze(1).to_broadcast([1, 2, NE]),
                                     c.iota[0:1, 0:2].unsqueeze(2).to_broadcast([1, 2, NE]), ALU.is_equal))
                then(v.tensor_tensor(gt[:, 0:2, :], two[:], no.unsqueeze(1).to_broadcast([1, 2, NE]), ALU.mult))
                then(v.tensor_reduce(pick[:], gt[:, 0:2, :], AX.X, ALU.add))
                then(v.tensor_copy(chosen[:], pick[:]))
                then(v.tensor_tensor(gt[:, 0:2, :], two[:], lg[:].unsqueeze(1).to_broadcast([1, 2, NE]), ALU.mult))
                then(v.tensor_reduce(val[:], gt[:, 0:2, :], AX.X, ALU.add))
                softmax(3, val, val)
                dve.sem_inc(s_w, 1)
                dve.wait_ge(c.bank_full[0], turn(0, 0)[1])
                then(v.tensor_copy(share[:], c.bank[0][:, 0:2]))
                dve.sem_inc(c.bank_free[0], 1)
                dve.sem_inc(c.bank_free[1], 1)


def experts(nc, c, a, chosen, share, out):
    with Phase(nc, "experts") as ph:
        cut = carver(c.agg)
        stage = cut(GT, D)
        w1, w2, b1 = ph.sb("w1", [P, KH, 4 * D]), ph.sb("w2", [P, 8, D]), ph.sb("b1", [P, 8])
        u = ph.sb("rows", [P, GT, D])
        done_rows = ph.sb("done", [P, GT, D])
        vec, b2 = ph.sb("vec", [P, 2, D]), ph.sb("b2", [P, 2, D])
        turn = c.ledger.plan(Mlp.BANKS, NG)
        mlp = Mlp(nc, c, ph, turn, stage, cut, w1, w2, b1, ACT.Gelu)
        (s_in, s_w, s_stage, s_u, s_y, s_bn, s_mv, s_rs, s_tmp, s_nrm, s_gam, s_bet, s_out, s_store) = ph.sems(
            "weights_in weighted staged rows_biased rows_summed partial variance rstd sum normal gamma beta rows_done stored")
        with nc.Block() as block:

            @block.sync
            def _(sp):
                for i in range(2):
                    e = sp.value_load(chosen[0:1, i:i + 1], min_val=0, max_val=7)
                    one = ds(e, 1)
                    for h in range(KH):
                        sp.dma_start(w1[:, h, i * 2 * D:(i + 1) * 2 * D],
                                     a["L1_ffn_W1"][one, h * P:(h + 1) * P, :].rearrange("e p f -> p (e f)")).then_inc(s_in, 16)
                    for m in range(4):
                        sp.dma_start(w2[:, 4 * i + m, :],
                                     a["L1_ffn_W2"][one, m * P:(m + 1) * P, :].rearrange("e p o -> p (e o)")).then_inc(s_in, 16)
                        sp.dma_start(b1[:, 4 * i + m:4 * i + m + 1],
                                     a["L1_ffn_b1"][one, m * P:(m + 1) * P].rearrange("e p -> p e"),
                                     allow_slow_non_contiguous=True).then_inc(s_in, 16)
                    sp.dma_start(b2[:, i, :], a["L1_ffn_b2"][one, :].to_broadcast([P, D])).then_inc(s_in, 16)
                for j, n in enumerate(("gamma", "beta")):
                    sp.dma_start(vec[:, j, :], spread(a["L1_ffn_" + n])).then_inc(s_in, 16)
                sp.sem_inc(s_store, 16)
                with sp.Fori(0, NG - 1) as g:
                    sp.wait_ge(s_out, g + 1)
                    sp.dma_start(out[ds(g * GR, GR), :].rearrange("(k p) d -> p k d", p=P), done_rows[:]).then_inc(s_store, 16)
                sp.wait_ge(s_out, NG)
                at = (NG - 1) * GR
                sp.dma_start(out[at:at + (GT - 1) * P, :].rearrange("(k p) d -> p k d", p=P), done_rows[:, 0:GT - 1, :])\
                    .then_inc(s_store, 16)
                sp.dma_start(out[N - LAST:N, :], done_rows[0:LAST, GT - 1, :]).then_inc(s_store, 16)
                sp.wait_ge(s_store, 16 * (NG + 2))

            @block.tensor
            def _(pe):
                pe.sem_inc(mlp.s_used, 1)
                pe.wait_ge(s_w, 4)
                with pe.Fori(0, NG) as g:
                    pe.wait_ge(s_stage, g + 1)
                    mlp.tensor(pe, g)

            @block.scalar
            def _(act):
                act.wait_ge(s_in, 24 * 16)
                with act.Fori(0, NG) as g:
                    act.wait_ge(mlp.s_used, g + 1)
                    act.wait_ge(s_u, g + 1)
                    gate(act, c)
                    nc.scalar.copy(stage, group(c.xn, g)).then_inc(s_stage, 1)
                    mlp.scalar(act, g)

            @block.gpsimd
            def _(pool):
                p = nc.gpsimd
                pool.wait_ge(s_w, 4)
                pool.sem_inc(s_u, 1)
                with pool.Fori(0, NG) as g:
                    pool.wait_ge(s_stage, g + 1)
                    pool.wait_ge(s_y, g * 5 + 1)
                    p.tensor_tensor(u[:], stage, b2[:, 0:1, :].to_broadcast([P, GT, D]), ALU.add).then_inc(s_u, 1)
                    rstd(pool, c, g, s_mv, s_rs, s_tmp)
                    pool.wait_ge(s_nrm, (g + 1) * GT)
                    p.tensor_tensor(u[:], u[:], vec[:, 0:1, :].to_broadcast([P, GT, D]), ALU.mult).then_inc(s_gam, 1)

            @block.vector
            def _(dve):
                v = nc.vector
                dve.wait_ge(s_in, 24 * 16)
                for i in range(2):
                    x = w2[:, 4 * i:4 * i + 4, :]
                    v.tensor_scalar(x, x, share[:, i:i + 1], None, ALU.mult).then_inc(s_w, 1)
                v.tensor_scalar(b2[:, 0, :], b2[:, 0, :], share[:, 0:1], None, ALU.mult).then_inc(s_w, 1)
                dve.wait_ge(s_w, 3)
                v.scalar_tensor_tensor(b2[:, 0, :], b2[:, 1, :], share[:, 1:2], b2[:, 0, :], ALU.mult, ALU.add).then_inc(s_w, 1)
                dve.sem_inc(s_y, 1)
                tile = lambda k: u[:, k, :]
                with dve.Fori(0, NG) as g:
                    dve.wait_ge(s_u, g + 2)
                    for n, (j, k, w) in enumerate(mlp.pairs()):
                        b, t = turn(j, g)
                        dve.wait_ge(c.bank_full[b], t)
                        x = u[:, k:k + w, :].rearrange("p k d -> p (k d)")
                        v.tensor_tensor(x, x, c.bank[b][:, 0:w * D], ALU.add).then_inc(s_y, 1)
                        dve.wait_ge(s_y, g * 5 + (n + 2))
                        dve.sem_inc(c.bank_free[b], 1)
                    stats(dve, c, tile, g, s_bn, s_mv)
                    normalise(dve, c, tile, tile, g, s_rs, s_nrm)
                    dve.wait_ge(s_gam, g + 1)
                    v.tensor_tensor(u[:], u[:], vec[:, 1:2, :].to_broadcast([P, GT, D]), ALU.add).then_inc(s_bet, 1)
                    dve.wait_ge(s_bet, g + 1)
                    dve.wait_ge(s_store, (g + 1) * 16)
                    gate(dve, c)
                    v.tensor_tensor(done_rows[:], u[:], group(c.res, g), ALU.add).then_inc(s_out, 1)
                    dve.wait_ge(s_out, g + 1)
                    dve.sem_inc(s_y, 1)


def program(nc, a, out):
    c = Core()
    c.nc = nc
    ctx = ExitStack()
    with ctx:
        sb = lambda n, s, d: ctx.enter_context(nc.sbuf_tensor(n, s, d))
        c.sem = lambda n: ctx.enter_context(nc.semaphore(n))
        c.phase_sems = []
        c.ledger = Ledger()
        c.bank = [ctx.enter_context(nc.psum_tensor(f"bank{b}", [P, 512], F32)) for b in range(8)]
        c.bank_full = [c.sem(f"bank_full{b}") for b in range(8)]
        c.bank_free = [c.sem(f"bank_free{b}") for b in range(8)]
        c.gates = {str(e.engine): c.sem(f"waits_passed_{n}") for n, e in
                   (("pe", nc.tensor), ("act", nc.scalar), ("dve", nc.vector), ("pool", nc.gpsimd), ("sp", nc.sync))}
        c.regs = {str(e.engine): [e.alloc_register(f"tile{u}") for u in range(HALF)] for e in (nc.vector, nc.tensor)}
        c.res = sb("residual", [P, NT * D], F32)
        c.xn = sb("state", [P, NT * D], F32)
        c.agg = sb("sums", [P, NT * D], F32)
        c.ident = sb("ident", [P, P], F32)
        c.ones = sb("ones", [P, P], F32)
        c.iota = sb("iota", [P, P], F32)
        c.eps7 = sb("eps7", [P, GT], F32)
        c.pow7 = sb("pow7", [P, GT], F32)
        c.bn = sb("bn", [P, GT, 6], F32)
        c.mv = sb("mv", [P, GT, 2], F32)
        c.ve = sb("ve", [P, GT], F32)
        c.rs = sb("rs", [P, GT], F32)
        c.row_no = sb("row_no", [P, 1], F32)
        c.real = sb("real", [P, NT], F32)
        c.meta = sb("meta", [P, SB * P, 2], F32)
        c.local = c.meta[:, :, 0]
        c.tile_row = sb("tile_row", [1, SB * P], I32)
        c.row4 = sb("row4", [P, SB * P], I32)
        c.rec_d = nc.dram_tensor("edge_records", (RECN, 4), I32, kind="Internal").ap()
        c.tl_d = nc.dram_tensor("step_tiles", (SB * P,), I32, kind="Internal").ap()
        c.row8_d = nc.dram_tensor("table_rows_1", (P, SB * P), I32, kind="Internal").ap()
        c.tab0_d = nc.dram_tensor("tables0", (REL0 * NP, D), F32, kind="Internal").ap()
        c.tab1_d = nc.dram_tensor("tables1", (REL1 * NP, D), F32, kind="Internal").ap()

        constants(nc, c, a["x"])
        with nc.sbuf_tensor("rel4", [P, SB * P], F32) as c.rel4:
            edge_tables(nc, c, a["src"], a["dst"], a["edge_type_4"], a["edge_type_8"])
            edge_weights(nc, c)
        with ExitStack() as mix:
            wt = mix.enter_context(nc.sbuf_tensor("wt", [P, KH, 5 * D], F32))
            kv = mix.enter_context(nc.sbuf_tensor("kv", [P, KH, P + 4], F32))
            weights0(nc, c, a, wt)
            mix0_sums(nc, c, wt, kv)
            mix0_main(nc, c, a, wt, kv)
        gnn0(nc, c, a)
        with ExitStack() as l1:
            small = lambda n, s, d=F32: l1.enter_context(nc.sbuf_tensor(n, s, d))
            score, take = small("score", [P, NT]), small("take", [P, NT])
            mx, scale, total = small("mx", [P, KH, D]), small("scale", [P, D]), small("total", [P, D])
            chosen, share = small("chosen", [1, 2], I32), small("share", [P, 2])
            ffn0(nc, c, a, score)
            select(nc, c, score, take)
            with nc.sbuf_tensor("acc1", [P, 4 * P + KH], F32) as acc:
                with nc.sbuf_tensor("wt1", [P, KH, 2 * D], F32) as wt:
                    weights1(nc, c, a, ("wk", "wv"), c.agg[:, 0:4 * D].rearrange("p (b i) -> p b i", i=D), wt)
                    tables1(nc, c, a, take)
                    gnn1(nc, c, wt, acc)
                with nc.sbuf_tensor("nat1", [P, 2, D], F32) as nat, nc.sbuf_tensor("wo1", [P, KH, D], F32) as wo:
                    weights1(nc, c, a, ("wo",), nat, wo)
                    mix1_matrix(nc, c, a, acc, wo, mx)
            batch_norm(nc, c, a, scale)
            mix1_main(nc, c, a, scale, mx, total)
            router(nc, c, a, total, chosen, share)
            experts(nc, c, a, chosen, share, out)


def constants(nc, c, x):
    s_x, s_pad, s_c, s_v, s_free = (c.sem(n) for n in ("x_in", "pad_cleared", "constants_made", "ident_cleared", "real_step"))
    with nc.Block() as block:

        @block.sync
        def _(sp):
            full = c.res[:, 0:(NT - 1) * D].rearrange("p (t c) -> p t c", c=D)
            sp.dma_start(full, x[0:(NT - 1) * P, :].rearrange("(t p) c -> p t c", p=P)).then_inc(s_x, 16)
            sp.wait_ge(s_pad, 1)
            sp.dma_start(c.res[0:LAST, (NT - 1) * D:NT * D], x[(NT - 1) * P:N, :]).then_inc(s_x, 16)
            sp.wait_ge(s_x, 32)

        @block.gpsimd
        def _(pool):
            g = nc.gpsimd
            g.memset(c.res[:, (NT - 1) * D:NT * D], 0.0).then_inc(s_pad, 1)
            g.memset(c.ident[:], 0.0).then_inc(s_v, 1)
            g.memset(c.ones[:], 1.0).then_inc(s_c, 1)
            g.iota(c.iota[:], [[1, P]], base=0, channel_multiplier=0,
                   allow_small_or_imprecise_dtypes=True).then_inc(s_c, 1)
            g.iota(c.real[:], [[P, NT]], base=0, channel_multiplier=1,
                   allow_small_or_imprecise_dtypes=True).then_inc(s_free, 1)
            g.iota(c.row_no[:], [[0, 1]], base=0, channel_multiplier=1,
                   allow_small_or_imprecise_dtypes=True).then_inc(s_c, 1)
            pool.wait_ge(s_v, 1)
            g.affine_select(out=c.ident[:], in_=c.ident[:], compare_op=ALU.not_equal, fill=1.0, base=0,
                            pattern=[[-1, P]], channel_multiplier=1).then_inc(s_c, 1)

        @block.vector
        def _(dve):
            v = nc.vector
            v.memset(c.eps7[:], EPS).then_inc(s_c, 1)
            v.memset(c.pow7[:], -0.5).then_inc(s_c, 1)
            dve.wait_ge(s_free, 1)
            v.tensor_scalar(c.real[:], c.real[:], float(N), None, ALU.is_lt).then_inc(s_c, 1)
            for b in range(8):
                dve.sem_inc(c.bank_free[b], 1)


def kernel(**inputs):
    import numpy as _np
    import concourse.bacc as _bacc
    from concourse import mybir as _mybir
    from concourse.bass_utils import run_bass_kernel_spmd as _run

    nc = _bacc.Bacc("TRN2", target_bir_lowering=False, num_devices=1)
    arrays, args = {}, {}
    for name, value in inputs.items():
        a = _np.ascontiguousarray(value)
        arrays[f"in_{name}_dram"] = a
        args[name] = nc.dram_tensor(f"in_{name}_dram", a.shape, _mybir.dt.from_np(a.dtype), kind="ExternalInput").ap()
    out = nc.dram_tensor("out_0_dram", (N, D), F32, kind="ExternalOutput").ap()
    program(nc, args, out)
    r = _run(nc, [arrays], core_ids=[0])
    return r.results[0]["out_0_dram"]
```

```python
from contextlib import ExitStack

import concourse.bass as bass
from concourse import mybir

ALU = mybir.AluOpType
ACT = mybir.ActivationFunctionType
AX = mybir.AxisListType
F32 = mybir.dt.float32
BF16 = mybir.dt.bfloat16
I32 = mybir.dt.int32
ds = bass.ds

P = 128
N = 6250
D = 256
KH = D // P
E = 100000
NT = -(-N // P)
GT = 7
NG = NT // GT
NP = NT * P
LAST = N - (NT - 1) * P
GR = GT * P
CH = ((0, 4), (4, 3))
DEPTH, REL0, REL1 = 4, 4, 8
EPS = 1e-5
SLOTS = 16
HALF = SLOTS // 2
STEPS = -(-(E // P + 1 + NT) // SLOTS) * SLOTS
BODIES = STEPS // SLOTS
SB = -(-STEPS // P)
EP = 125
EC = E // EP
RECN = E + P
KK = N // 2 - 1
BIG = 1.0e30
assert BODIES > NT + 2 and NG * GT == NT and EP * EC == E


class Ledger:

    def __init__(self):
        self.used = [0] * 8

    def plan(self, banks, rounds):
        base = list(self.used)
        per = [banks.count(b) for b in range(8)]
        for b in range(8):
            self.used[b] += per[b] * rounds
        turns = []
        for j, b in enumerate(banks):
            turns.append((b, base[b] + banks[:j].count(b) + 1, per[b]))

        def turn(j, g):
            b, first, step = turns[j]
            return b, g * step + first

        return turn


class Core:
    pass


def group(resident, g):
    return resident[:, ds(g * (GT * D), GT * D)].rearrange("p (k c) -> p k c", c=D)


def tile_of(resident, g, k, a=0, w=D):
    return resident[:, ds(g * (GT * D) + (k * D + a), w)]


def load_tiles(eng, c, first, n=HALF):
    regs = c.regs[str(eng.engine)][:n]
    eng.reg_load(regs, c.tile_row[0:1, ds(first, n)])
    return [eng.snap(r, min_val=0, max_val=NT - 1) for r in regs]


def gate(eng, c):
    eng.sem_inc(c.gates[str(eng.engine)], 1)


def transposed(pe, c, src, turn, j0, g, ready=None):
    for h in range(KH):
        for n, (k0, m) in enumerate(CH):
            b, t = turn(j0 + 2 * h + n, g)
            pe.wait_ge(c.bank_free[b], t)
            gate(pe, c)
            for k in range(k0, k0 + m):
                last = c.nc.tensor.transpose(c.bank[b][:, (k - k0) * P:(k - k0 + 1) * P], src(k, h), c.ident[:])
            last.then_inc(c.bank_full[b], 1)


def evacuate_transposed(act, c, dst, turn, j0, g, done):
    for h in range(KH):
        for n, (k0, m) in enumerate(CH):
            b, t = turn(j0 + 2 * h + n, g)
            act.wait_ge(c.bank_full[b], t)
            c.nc.scalar.copy(dst[:, h, k0 * P:(k0 + m) * P], c.bank[b][:, 0:m * P]).then_inc(c.bank_free[b], 1)
    act.wait_ge(c.bank_free[b], t + 1)
    act.sem_inc(done, 1)


def stats(dve, c, src, g, s_bn, s_mv):
    for k in range(GT):
        c.nc.vector.bn_stats(c.bn[:, k, :], src(k)).then_inc(s_bn, 1)
    dve.wait_ge(s_bn, (g + 1) * GT)
    gate(dve, c)
    for k in range(GT):
        c.nc.vector.bn_aggr(c.mv[:, k, :], c.bn[:, k, :]).then_inc(s_mv, 1)


def rstd(pool, c, g, s_mv, s_rs, s_tmp):
    pool.wait_ge(s_mv, (g + 1) * GT)
    c.nc.gpsimd.tensor_tensor(c.ve[:], c.mv[:, :, 1], c.eps7[:], ALU.add).then_inc(s_tmp, 1)
    pool.wait_ge(s_tmp, g + 1)
    c.nc.gpsimd.tensor_tensor(c.rs[:], c.ve[:], c.pow7[:], ALU.pow).then_inc(s_rs, 1)


def normalise(dve, c, dst, src, g, s_rs, done):
    dve.wait_ge(s_rs, g + 1)
    gate(dve, c)
    for k in range(GT):
        ins = c.nc.vector.tensor_scalar(dst(k), src(k), c.mv[:, k, 0:1], c.rs[:, k:k + 1], ALU.subtract, ALU.mult)
        ins.then_inc(done, 1)


def cutter(space):
    return carver(space, space.shape[1])


def carver(resident, size=NT * D):
    at = [0]

    def cut(*shape):
        n = 1
        for s in shape:
            n *= s
        view = resident[:, at[0]:at[0] + n]
        at[0] += n
        assert at[0] <= size
        names = "abcd"[:len(shape)]
        if len(shape) == 1:
            return view
        return view.rearrange(f"p ({' '.join(names)}) -> p {' '.join(names)}", **dict(zip(names, shape)))

    return cut


class Phase:

    def __init__(self, nc, name):
        self.nc, self.name, self.held, self.stack = nc, name, [], ExitStack()

    def sem(self, name):
        self.held.append(self.nc.alloc_semaphore(f"{self.name}_{name}"))
        return self.held[-1]

    def sems(self, names):
        return [self.sem(n) for n in names.split()]

    def sb(self, name, shape, dtype=F32):
        return self.stack.enter_context(self.nc.sbuf_tensor(f"{self.name}_{name}", shape, dtype))

    def __enter__(self):
        return self

    def __exit__(self, *_):
        self.stack.close()
        self.nc.clear_and_free_semaphores(self.held)
        self.nc.all_engine_barrier()


def edge_tables(nc, c, src, dst, et4, et8):
    with Phase(nc, "edges") as ph:
        sb, sem = ph.sb, ph.sem
        e_src, e_dst, e_t4, e_t8 = (sb(n, [EP, EC], I32) for n in ("e_src", "e_dst", "e_t4", "e_t8"))
        e_rec = sb("e_rec", [EP, EC, 4], I32)
        e_tail = sb("e_tail", [P, 4], I32)
        hit = sb("hit", [EP, EC], F32)
        below = sb("below", [EP, NT + 1], F32)
        start = sb("start", [P, NT + 1], F32)
        cnt = sb("cnt", [P, NT], F32)
        cnt_i = sb("cnt_i", [P, NT], I32)
        nst = sb("nst", [P, NT], F32)
        cum = sb("cum", [P, 2, NT], F32)
        step_no = sb("step_no", [P, SB], F32)
        begun = sb("begun", [P, SB, NT], F32)
        over = sb("over", [P, SB, NT], F32)
        prod = sb("prod", [P, SB, NT], F32)
        tile_f = sb("tile_f", [P, SB], F32)
        base_f = sb("base_f", [P, SB], F32)
        s_f = sb("s_f", [P, SB], F32)
        end_f = sb("end_f", [P, SB], F32)
        e0 = sb("e0", [P, SB], F32)
        e0_i = sb("e0_i", [P, SB], I32)
        left = sb("left", [P, SB], F32)
        low = sb("low", [P, SB], F32)
        tile_i = sb("tile_i", [P, SB], I32)
        rows = c.xn[:, 0:SB * 4 * P].bitcast(I32).rearrange("p (b n) -> p b n", b=SB)
        slot_no = sb("slot_no", [P, P], F32)
        plane = c.agg[:, 0:SB * 4 * P].rearrange("p (b f s) -> p b f s", b=SB, f=4)
        valid = c.agg[:, SB * 4 * P:SB * 5 * P].rearrange("p (b s) -> p b s", b=SB)
        row8 = sb("row8", [P, SB * P], I32)
        rec_d = c.rec_d
        s_in, s_rec, s_recd, s_gat, s_tl, s_tr = (sem(n) for n in (
            "edges_in", "records_made", "records_stored", "records_gathered", "step_tiles_stored", "tile_row_loaded"))
        s_below, s_v, s_pl, s_iota, s_e0, s_ti, s_meta = (sem(n) for n in (
            "below_counted", "edge_vector_steps", "planes_made", "iotas_made", "step_starts_made",
            "step_tiles_made", "planes_copied"))
        turn = c.ledger.plan([b for b in range(7)] + [7], 1)
        with nc.Block() as block:

            @block.sync
            def _(sp):
                for to, of in ((e_src, src), (e_dst, dst), (e_t4, et4), (e_t8, et8)):
                    sp.dma_start(to[:], of.rearrange("(p n) -> p n", p=EP)).then_inc(s_in, 16)
                sp.wait_ge(s_rec, 4 + 1)
                sp.dma_start(rec_d[0:E, :].rearrange("(p n) f -> p n f", p=EP), e_rec[:]).then_inc(s_recd, 16)
                sp.dma_start(rec_d[E:RECN, :], e_tail[:]).then_inc(s_recd, 16)
                sp.wait_ge(s_ti, 1)
                sp.dma_start(c.tl_d.rearrange("(b p) -> p b", p=P), tile_i[:],
                             allow_slow_non_contiguous=True).then_inc(s_tl, 16)
                sp.wait_ge(s_tl, 16)
                sp.dma_start(c.tile_row[:], c.tl_d.rearrange("(a n) -> a n", a=1)).then_inc(s_tr, 16)
                sp.wait_ge(s_meta, 4 * SB)
                sp.dma_start(c.row8_d, row8[:]).then_inc(s_tr, 16)
                sp.wait_ge(s_tr, 32)

            @block.gpsimd
            def _(pool):
                nc.gpsimd.memset(e_tail[:], 0).then_inc(s_rec, 1)
                nc.gpsimd.iota(step_no[:], [[P, SB]], base=0, channel_multiplier=1,
                               allow_small_or_imprecise_dtypes=True).then_inc(s_iota, 1)
                nc.gpsimd.iota(slot_no[:], [[1, P]], base=0, channel_multiplier=0,
                               allow_small_or_imprecise_dtypes=True).then_inc(s_iota, 1)
                pool.wait_ge(s_recd, 32)
                pool.wait_ge(s_e0, 1)
                for b in range(SB):
                    nc.gpsimd.indirect_dma_start(
                        out=rows[:, b, :], out_offset=None, in_=rec_d,
                        in_offset=bass.IndirectOffsetOnAxis(ap=e0_i[:, b:b + 1], axis=0)).then_inc(s_gat, 16)

            @block.vector
            def _(dve):
                v = nc.vector
                done = [0]

                def then(ins):
                    done[0] += 1
                    ins.then_inc(s_v, 1)
                    dve.wait_ge(s_v, done[0])

                v.memset(below[:, 0:1], 0.0).then_inc(s_below, 1)
                dve.wait_ge(s_in, 64)
                v.scalar_tensor_tensor(e_rec[:, :, 0], e_t4[:], float(NP), e_src[:], ALU.mult, ALU.add).then_inc(s_rec, 1)
                v.scalar_tensor_tensor(e_rec[:, :, 1], e_t8[:], float(NP), e_src[:], ALU.mult, ALU.add).then_inc(s_rec, 1)
                v.tensor_copy(e_rec[:, :, 2], e_dst[:]).then_inc(s_rec, 1)
                v.tensor_copy(e_rec[:, :, 3], e_t4[:]).then_inc(s_rec, 1)
                for t in range(1, NT + 1):
                    if t > 1:
                        dve.wait_ge(s_below, t)
                    v.tensor_scalar(hit[:], e_dst[:], float(P * t), 0.0, ALU.is_lt, ALU.add,
                                    accum_out=below[:, t:t + 1]).then_inc(s_below, 1)
                dve.wait_ge(c.bank_full[0], 1)
                then(v.tensor_copy(start[:], c.bank[0][:, 0:NT + 1]))
                then(v.tensor_tensor(cnt[:], start[:, 1:NT + 1], start[:, 0:NT], ALU.subtract))
                then(v.tensor_scalar(cnt_i[:], cnt[:], float(P - 1), None, ALU.add))
                then(v.tensor_scalar(cnt_i[:], cnt_i[:], 7, None, ALU.arith_shift_right))
                then(v.tensor_copy(nst[:], cnt_i[:]))
                then(v.tensor_copy(cum[:, 0, :], nst[:]))
                s, at = 1, 0
                while s < NT:
                    then(v.tensor_copy(cum[:, 1 - at, 0:s], cum[:, at, 0:s]))
                    then(v.tensor_tensor(cum[:, 1 - at, s:NT], cum[:, at, s:NT], cum[:, at, 0:NT - s], ALU.add))
                    s, at = 2 * s, 1 - at
                incl, excl = cum[:, at, :], cum[:, 1 - at, :]
                then(v.tensor_tensor(excl, incl, nst[:], ALU.subtract))
                dve.wait_ge(s_iota, 2)
                wide = lambda a: a.unsqueeze(1).to_broadcast([P, SB, NT])
                num = step_no[:].unsqueeze(2).to_broadcast([P, SB, NT])
                then(v.tensor_tensor(over[:], wide(incl), num, ALU.is_le))
                then(v.tensor_tensor(begun[:], wide(excl), num, ALU.is_le))
                then(v.tensor_reduce(tile_f[:], over[:], AX.X, ALU.add))
                then(v.tensor_tensor(prod[:], over[:], wide(nst[:]), ALU.mult))
                then(v.tensor_reduce(base_f[:], prod[:], AX.X, ALU.add))
                then(v.tensor_tensor(prod[:], over[:], wide(cnt[:]), ALU.mult))
                then(v.tensor_reduce(s_f[:], prod[:], AX.X, ALU.add))
                then(v.tensor_tensor(prod[:], begun[:], wide(cnt[:]), ALU.mult))
                then(v.tensor_reduce(end_f[:], prod[:], AX.X, ALU.add))
                then(v.tensor_scalar(tile_f[:], tile_f[:], float(NT - 1), None, ALU.min))
                v.tensor_copy(tile_i[:], tile_f[:]).then_inc(s_ti, 1)
                then(v.tensor_tensor(e0[:], step_no[:], base_f[:], ALU.subtract))
                then(v.scalar_tensor_tensor(e0[:], e0[:], float(P), s_f[:], ALU.mult, ALU.add))
                then(v.tensor_scalar(e0[:], e0[:], float(E), None, ALU.min))
                v.tensor_copy(e0_i[:], e0[:]).then_inc(s_e0, 1)
                then(v.tensor_tensor(left[:], end_f[:], e0[:], ALU.subtract))
                then(v.tensor_scalar(low[:], tile_f[:], float(P), -1.0, ALU.mult, ALU.add))
                for b in range(SB):
                    then(v.tensor_scalar(valid[:, b, :], slot_no[:], left[:, b:b + 1], None, ALU.is_lt))
                dve.wait_ge(s_gat, 16 * SB)
                recs = rows[:].rearrange("p b (s f) -> p b s f", f=4)
                for b in range(SB):
                    for f in (0, 1):
                        then(v.tensor_scalar(plane[:, b, f, :], recs[:, b, :, f], -float(1 << 20), None, ALU.add))
                        then(v.tensor_tensor(plane[:, b, f, :], plane[:, b, f, :], valid[:, b, :], ALU.mult))
                        then(v.tensor_scalar(plane[:, b, f, :], plane[:, b, f, :], float(1 << 20), None, ALU.add))
                    then(v.tensor_scalar(plane[:, b, 2, :], recs[:, b, :, 2], low[:, b:b + 1], None, ALU.subtract))
                    then(v.tensor_tensor(plane[:, b, 2, :], plane[:, b, 2, :], valid[:, b, :], ALU.mult))
                    then(v.tensor_scalar(plane[:, b, 2, :], plane[:, b, 2, :], -1.0, None, ALU.add))
                    v.tensor_copy(plane[:, b, 3, :], recs[:, b, :, 3]).then_inc(s_pl, 1)
                for b in range(SB):
                    bb, t = turn(1 + b if b < 6 else 7, 0)
                    dve.wait_ge(c.bank_full[bb], t)
                    for f, to in enumerate((c.row4, row8, c.local, c.rel4)):
                        ins = v.tensor_copy(to[:, b * P:(b + 1) * P], c.bank[bb][:, f * P:(f + 1) * P])
                        ins.then_inc(s_meta, 1)
                    dve.wait_ge(s_meta, 4 * (b + 1))
                    dve.sem_inc(c.bank_free[bb], 1)
                dve.sem_inc(c.bank_free[0], 1)

            @block.tensor
            def _(pe):
                pe.wait_ge(s_below, NT + 1)
                nc.tensor.matmul(c.bank[0][:, 0:NT + 1], c.ones[0:EP, :], below[:], start=True, stop=True)\
                    .then_inc(c.bank_full[0], 1)
                for b in range(SB):
                    bb, t = turn(1 + b if b < 6 else 7, 0)
                    pe.wait_ge(s_pl, b + 1)
                    for f in range(4):
                        ins = nc.tensor.transpose(c.bank[bb][:, f * P:(f + 1) * P], plane[:, b, f, :], c.ident[:])
                    ins.then_inc(c.bank_full[bb], 1)


def edge_weights(nc, c):
    PARTS = 3
    W = PARTS * REL0
    with Phase(nc, "degree") as ph:
        sb = ph.sb
        hot = sb("hot", [P, 2, SLOTS, P], BF16)
        hot_t = sb("hot_t", [P, 2, SLOTS, P], BF16)
        rel = sb("rel", [P, 2, SLOTS, REL0], BF16)
        wide_rel = sb("wide_rel", [P, SLOTS, W], F32)
        picked = sb("picked", [P, SLOTS, W], F32)
        rel_no = sb("rel_no", [P, W], F32)
        count = sb("count", [P, NT, REL0], F32)
        rest = sb("rest", [P, NT, REL0], F32)
        inv = sb("inv", [P, NT, W], BF16)
        ident16 = sb("ident16", [P, P], BF16)
        zero = sb("zero", [P, NT * REL0], BF16)
        (s_set, s_hot, s_hot2, s_cnt, s_tot, s_free, s_v, s_inv, s_turned, s_ht, s_rel, s_pick, s_w, s_out) = ph.sems(
            "constants_set hot_made hot_made_again counts_summed totals_made totals_read vector_steps inverse_made hot_turned hot_copied "
            "relation_made weights_picked weights_masked weights_made")
        iota = c.iota[:].unsqueeze(1).to_broadcast([P, SLOTS, P])
        b4 = c.iota[:, 0:REL0].unsqueeze(1).to_broadcast([P, SLOTS, REL0])
        loc = lambda i: c.local[:, ds(i * SLOTS, SLOTS)].unsqueeze(2).to_broadcast([P, SLOTS, P])
        ret = lambda i, w: c.rel4[:, ds(i * SLOTS, SLOTS)].unsqueeze(2).to_broadcast([P, SLOTS, w])
        PAIRS = BODIES // 2
        assert PAIRS * 2 == BODIES
        totals = c.bank[0][:, 0:NT * REL0]
        with nc.Block() as block:

            @block.vector
            def _(dve):
                v = nc.vector
                v.tensor_copy(ident16[:], c.ident[:]).then_inc(s_set, 1)
                v.memset(zero[:], 0.0).then_inc(s_set, 1)
                for k in range(PARTS):
                    v.tensor_copy(rel_no[:, k * REL0:(k + 1) * REL0], c.iota[:, 0:REL0]).then_inc(s_set, 1)

                with dve.Fori(0, PAIRS) as q:
                    for h in range(2):
                        n = q * 2 + h
                        dve.wait_ge(s_cnt, n + 1)
                        gate(dve, c)
                        v.tensor_tensor(hot[:, h], iota, loc(n), ALU.is_equal).then_inc(s_hot, 1)
                        v.tensor_tensor(rel[:, h], b4, ret(n, REL0), ALU.is_equal).then_inc(s_hot, 1)
                done = [0]

                def then(ins):
                    done[0] += 1
                    ins.then_inc(s_v, 1)
                    dve.wait_ge(s_v, done[0])

                dve.wait_ge(s_tot, 1)
                then(v.tensor_scalar(count[:].rearrange("p t r -> p (t r)"), totals, 1.0, None, ALU.max))
                then(v.reciprocal(count[:], count[:]))
                part = lambda k: inv[:, :, k * REL0:(k + 1) * REL0]
                then(v.tensor_copy(part(0), count[:]))
                then(v.tensor_tensor(rest[:], count[:], part(0), ALU.subtract))
                then(v.tensor_copy(part(1), rest[:]))
                then(v.tensor_tensor(rest[:], rest[:], part(1), ALU.subtract))
                then(v.tensor_copy(part(2), rest[:]))
                dve.sem_inc(s_inv, 1)

                def make(n, h):
                    dve.wait_ge(s_turned, n + 1)
                    gate(dve, c)
                    v.tensor_tensor(hot[:, h], iota, loc(n), ALU.is_equal).then_inc(s_hot2, 1)

                def weigh(n, h):
                    dve.wait_ge(s_w, n + 2)
                    dve.wait_ge(s_out, n + 1)
                    gate(dve, c)
                    v.tensor_tensor(wide_rel[:], rel_no[:].unsqueeze(1).to_broadcast([P, SLOTS, W]), ret(n, W),
                                    ALU.is_equal).then_inc(s_rel, 1)
                    dve.wait_ge(s_pick, n + 3)
                    dve.wait_ge(s_rel, n + 1)
                    v.tensor_tensor(picked[:], c.bank[6 + h][:, 0:SLOTS * W].rearrange("p (s r) -> p s r", r=W),
                                    wide_rel[:], ALU.mult).then_inc(s_w, 1)
                    dve.wait_ge(s_w, n + 3)
                    gate(dve, c)
                    v.tensor_reduce(c.meta[:, ds(n * SLOTS, SLOTS), 1], picked[:], AX.X, ALU.add).then_inc(s_out, 1)

                dve.sem_inc(s_w, 2)
                dve.sem_inc(s_out, 1)
                dve.wait_ge(s_set, 2 + PARTS)
                make(0, 0)
                with dve.Fori(0, PAIRS) as q:
                    make(q * 2 + 1, 1)
                    weigh(q * 2, 0)
                    make(q * 2 + 2, 0)
                    weigh(q * 2 + 1, 1)

            @block.tensor
            def _(pe):
                pe.wait_ge(s_set, 2 + PARTS)
                nc.tensor.matmul(totals, ident16[:], zero[:], start=True, stop=False)
                pe.sem_inc(s_cnt, 2)
                with pe.Fori(0, PAIRS) as q:
                    for h in range(2):
                        n = q * 2 + h
                        tiles = load_tiles(pe, c, n * SLOTS, SLOTS)
                        pe.wait_ge(s_hot, n * 2 + 2)
                        for u in range(SLOTS):
                            ins = nc.tensor.matmul(c.bank[0][:, ds(tiles[u] * REL0, REL0)], hot[:, h, u, :],
                                                   rel[:, h, u, :], start=False, stop=False)
                        ins.then_inc(s_cnt, 1)
                nc.tensor.matmul(totals, ident16[:], zero[:], start=False, stop=True).then_inc(s_tot, 1)

                def turn(n, h):
                    pe.wait_ge(s_hot2, n + 1)
                    pe.wait_ge(s_ht, n * 2 + 2)
                    gate(pe, c)
                    for u in range(SLOTS):
                        ins = nc.tensor.transpose(c.bank[2 + 2 * h + u // HALF][:].bitcast(BF16)[:, (u % HALF) * P:(u % HALF + 1) * P],
                                                  hot[:, h, u, :], ident16[:])
                    ins.then_inc(s_turned, 1)

                def pick(n, h):
                    tiles = load_tiles(pe, c, n * SLOTS, SLOTS)
                    pe.wait_ge(s_ht, n * 2 + 6)
                    pe.wait_ge(s_w, n + 1)
                    for u in range(SLOTS):
                        ins = nc.tensor.matmul(c.bank[6 + h][:, u * W:(u + 1) * W], hot_t[:, h, u, :],
                                               inv[:].rearrange("p t r -> p (t r)")[:, ds(tiles[u] * W, W)],
                                               start=True, stop=True)
                    ins.then_inc(s_pick, 1)

                pe.wait_ge(s_inv, 1)
                pe.sem_inc(s_turned, 2)
                pe.sem_inc(s_pick, 2)
                turn(0, 0)
                with pe.Fori(0, PAIRS) as q:
                    turn(q * 2 + 1, 1)
                    pick(q * 2, 0)
                    turn(q * 2 + 2, 0)
                    pick(q * 2 + 1, 1)

            @block.scalar
            def _(act):
                act.sem_inc(s_ht, 4)
                with act.Fori(0, PAIRS) as q:
                    for h in range(2):
                        n = q * 2 + h
                        act.wait_ge(s_turned, n + 3)
                        act.wait_ge(s_pick, n + 1)
                        for b in range(2):
                            nc.scalar.copy(hot_t[:, h, b * HALF:(b + 1) * HALF, :],
                                           c.bank[2 + 2 * h + b][:].bitcast(BF16).rearrange("p (u e) -> p u e", u=HALF)).then_inc(s_ht, 1)


NEXT_HOTS = ((), (), (0,), (1,), (2,), (3,), (4, 5), (6, 7))


class EdgeSum:

    def __init__(self, nc, c):
        self.nc, self.c = nc, c
        self.landed = [c.sem(f"message{s}_landed") for s in range(SLOTS)]
        self.ring_ready, self.hot_ready, self.summed, self.added = (
            c.sem(n) for n in ("slots_copied", "hot_made", "steps_summed", "steps_added"))

    def use(self, msg, hot, row_ring, meta_ring, rows, table, weighted):
        self.msg, self.hot = msg, hot
        self.row_ring, self.meta_ring, self.rows, self.table, self.weighted = row_ring, meta_ring, rows, table, weighted

    def scalar(self, act, i, n):
        for h in range(2):
            act.wait_ge(self.summed, n * SLOTS + (h + 1) * HALF)
            gate(act, self.c)
            at = ds(i * SLOTS + h * HALF, HALF)
            self.nc.scalar.copy(self.row_ring[:, h, :], self.rows[:, at]).then_inc(self.ring_ready, 1)
            self.nc.scalar.copy(self.meta_ring[:, h, :, :], self.c.meta[:, at, :]).then_inc(self.ring_ready, 1)

    def gpsimd(self, pool, n, after=None):
        for h in range(2):
            pool.wait_ge(self.ring_ready, n * 4 + (2 * h + 2))
            gate(pool, self.c)
            for u in range(HALF):
                s = h * HALF + u
                self.nc.gpsimd.indirect_dma_start(
                    out=self.msg[:, s, :], out_offset=None, in_=self.table,
                    in_offset=bass.IndirectOffsetOnAxis(ap=self.row_ring[:, h, u:u + 1], axis=0),
                    bounds_check=self.table.shape[0] - 1, oob_is_err=False).then_inc(self.landed[s], 16)
                if after:
                    after(s)

    def one_hot(self, s):
        m = self.meta_ring[:, s // HALF, s % HALF, :]
        if self.weighted:
            ins = self.nc.vector.tensor_scalar(self.hot[:, s, :], self.c.iota[:], m[:, 0:1], m[:, 1:2], ALU.is_equal, ALU.mult)
        else:
            ins = self.nc.vector.tensor_scalar(self.hot[:, s, :], self.c.iota[:], m[:, 0:1], None, ALU.is_equal)
        ins.then_inc(self.hot_ready, 1)

    def begin_vector(self, dve, n):
        dve.wait_ge(self.ring_ready, n * 4 + 2)
        for s in range(HALF):
            self.one_hot(s)

    def vector(self, dve, i, n, after=None, last=False):
        for h in range(2):
            tiles = load_tiles(dve, self.c, i * SLOTS + h * HALF)
            for u, t in enumerate(tiles):
                s = h * HALF + u
                dve.wait_ge(self.summed, n * SLOTS + (SLOTS + s + 1))
                dve.wait_ge(self.added, n * SLOTS + (4 + s))
                at = self.c.agg[:, ds(t * D, D)]
                self.nc.vector.tensor_tensor(at, at, self.c.bank[4 + s % 4][:, 0:D], ALU.add).then_inc(self.added, 1)
                if not (last and h == 1):
                    if u == 2:
                        dve.wait_ge(self.ring_ready, n * 4 + (2 * h + 4))
                    for k in NEXT_HOTS[u]:
                        self.one_hot((1 - h) * HALF + k)
                if after:
                    after(s)

    def tensor(self, pe, n, after=None):
        for s in range(SLOTS):
            pe.wait_ge(self.landed[s], n * 16 + 16)
            pe.wait_ge(self.hot_ready, n * SLOTS + s + 1)
            pe.wait_ge(self.added, n * SLOTS + (s + 1))
            self.nc.tensor.matmul(self.c.bank[4 + s % 4][:, 0:D], self.hot[:, s, :], self.msg[:, s, :],
                                  start=True, stop=True).then_inc(self.summed, 1)
            if after:
                after(s)


def bodies(eng, body):
    body(0, True, False)
    with eng.Fori(1, NT) as i:
        body(i, True, True)
    body(NT, False, True)
    with eng.Fori(NT + 1, BODIES - 1) as i:
        body(i, False, False)
    body(BODIES - 1, False, False)


def is_last(i):
    return isinstance(i, int) and i == BODIES - 1


class Keys0:

    def __init__(self, nc, c, ph, w, ex):
        self.nc, self.c = nc, c
        cut, cut_ex = cutter(w), cutter(ex)
        self.wt, self.x, self.xt, self.er, self.rr, self.v1 = cut(KH, 2 * D), cut(D), cut(KH, P), cut(D), cut(D), cut(KH, P + 4)
        self.zero, self.kv = cut_ex(KH * (P + 1)), cut_ex(KH, P + 4)
        (self.s_in, self.s_set, self.s_x, self.s_turned, self.s_xt, self.s_mm, self.s_act, self.s_k, self.s_real, self.s_sum,
         self.s_bd, self.s_dma) = (ph.sem(f"keys_{n}") for n in (
            "weights_in", "set", "staged", "turned", "xt", "products", "results", "made", "real_made", "summed", "diagonal", "dma"))

    def sync(self, sp, a):
        c = self.c
        sp.dma_start(self.wt, c.wt_d[:, :, D:3 * D]).then_inc(self.s_in, 16)
        sp.dma_start(c.xn_d.rearrange("(t p) d -> p t d", p=P), c.xn[:].rearrange("p (t d) -> p t d", d=D)).then_inc(self.s_dma, 16)
        sp.wait_ge(self.s_bd, 9)
        sp.dma_start(c.kv_d, self.kv).then_inc(self.s_dma, 16)
        sp.wait_ge(self.s_dma, 32)

    def sums(self, start, stop):
        return self.nc.tensor.matmul(self.c.bank[2][:, 0:KH * (P + 1)], self.c.ones[:], self.zero, start=start, stop=stop)

    def begin_tensor(self, pe):
        pe.wait_ge(self.s_in, 16)
        pe.wait_ge(self.s_set, 1)
        for s in (self.s_turned, self.s_mm, self.s_sum):
            pe.sem_inc(s, 1)
        self.sums(True, False)

    def end_tensor(self, pe):
        self.sums(False, True).then_inc(self.s_sum, 1)

    def begin_scalar(self, act):
        act.sem_inc(self.s_act, 1)

    def end_scalar(self, act):
        act.wait_ge(self.s_dma, 32)

    def begin_vector(self, dve):
        self.nc.vector.memset(self.kv, 0.0).then_inc(self.s_bd, 1)
        self.nc.vector.memset(self.zero, 0.0).then_inc(self.s_set, 1)

    def end_vector(self, dve):
        v = self.nc.vector
        acc = self.c.bank[2][:, 0:KH * (P + 1)].rearrange("p (a m) -> p a m", a=KH)
        dve.wait_ge(self.s_sum, NT + 2)
        dve.wait_ge(self.s_bd, 1)
        for j in range(4):
            r = slice(32 * j, 32 * j + 32)
            v.tensor_copy(self.kv[r, :, r], acc[r, :, r]).then_inc(self.s_bd, 1)
            v.tensor_copy(self.kv[r, :, P + j:P + j + 1], acc[r, :, P:P + 1]).then_inc(self.s_bd, 1)

    def gpsimd(self, pool, i, first, second):
        return None

    def tensor(self, pe, i, first, second):
        c, t = self.c, self.nc.tensor

        def after(s):
            if s == 1 and first:
                pe.wait_ge(self.s_x, i + 1)
                gate(pe, c)
                for h in range(KH):
                    ins = t.transpose(c.bank[0][:, h * P:(h + 1) * P], self.x[:, h * P:(h + 1) * P], c.ident[:])
                ins.then_inc(self.s_turned, 1)
            if s == 4 and first:
                pe.wait_ge(self.s_xt, i + 1)
                pe.wait_ge(self.s_act, i * 3 + 1)
                for h in range(KH):
                    ins = t.matmul(c.bank[1][:], self.xt[:, h, :], self.wt[:, h, :], start=(h == 0), stop=(h == KH - 1))
                ins.then_inc(self.s_mm, 1)
            if s == 11 and first:
                pe.wait_ge(self.s_k, i + 1)
                pe.wait_ge(self.s_real, i + 1)
                for h in range(KH):
                    ins = t.matmul(c.bank[2][:, h * (P + 1):(h + 1) * (P + 1)], self.er[:, h * P:(h + 1) * P],
                                   self.v1[:, h, 0:P + 1], start=False, stop=False)
                ins.then_inc(self.s_sum, 1)
        return after

    def scalar(self, act, i, first, second):
        c, sc = self.c, self.nc.scalar
        if first:
            act.wait_ge(self.s_turned, i + 1)
            gate(act, c)
            sc.copy(self.x, c.xn[:, ds(i * D, D)]).then_inc(self.s_x, 1)
            act.wait_ge(self.s_turned, i + 2)
            act.wait_ge(self.s_mm, i + 1)
            sc.copy(self.xt.rearrange("p h r -> p (h r)"), c.bank[0][:, 0:D]).then_inc(self.s_xt, 1)
            act.wait_ge(self.s_mm, i + 2)
            act.wait_ge(self.s_sum, i + 1)
            sc.activation(self.er, c.bank[1][:, 0:D], ACT.Exp).then_inc(self.s_act, 1)
            sc.activation(self.rr, c.bank[1][:, 0:D], ACT.Relu).then_inc(self.s_act, 1)
            sc.copy(self.v1[:, :, 0:P], c.bank[1][:, D:2 * D].rearrange("p (a m) -> p a m", a=KH)).then_inc(self.s_act, 1)

    def vector(self, dve, i, first, second):
        v, c = self.nc.vector, self.c

        def after(s):
            if s == 8 and first:
                dve.wait_ge(self.s_act, i * 3 + 4)
                v.scalar_tensor_tensor(self.er, self.er, 1.0, self.rr, ALU.min, ALU.add).then_inc(self.s_k, 1)
                gate(dve, c)
                v.tensor_copy(self.v1[:, :, P:P + 1], c.real[:, ds(i, 1)].unsqueeze(1).to_broadcast([P, KH, 1]))\
                    .then_inc(self.s_real, 1)
        return after


class RowsBehind:

    def __init__(self, nc, c, ph, name, ex):
        self.nc, self.c = nc, c
        cut = self.cut_ex = cutter(ex)
        self.u = cut(D)
        self.bn, self.mv, self.ve, self.rs, self.shift = (cut(n) for n in (6, 2, 1, 1, 1))
        (self.s_in, self.s_turned, self.s_xt, self.s_mm, self.s_act, self.s_mm2, self.s_t, self.s_u, self.s_bn, self.s_mv,
         self.s_ve, self.s_pow, self.s_rs, self.s_hat, self.s_gam, self.s_bet, self.s_done, self.s_dma) = (
            ph.sem(f"{name}_{n}") for n in (
                "weights_in", "turned", "xt", "first_products", "first_results", "second_products", "rows_begun", "rows_made",
                "partial", "variance", "variance_eps", "powers", "rstd", "normal", "gamma", "beta", "done", "dma"))

    def end_first(self, dve, i):
        v, c = self.nc.vector, self.c
        dve.wait_ge(self.s_u, i + 2)
        gate(dve, c)
        v.bn_stats(self.bn, self.u).then_inc(self.s_bn, 1)
        dve.wait_ge(self.s_bn, i + 1)
        gate(dve, c)
        v.bn_aggr(self.mv, self.bn).then_inc(self.s_mv, 1)
        dve.wait_ge(self.s_mv, i + 1)
        v.tensor_scalar(self.ve, self.mv[:, 1:2], EPS, None, ALU.add).then_inc(self.s_ve, 1)

    def gpsimd(self, pool, i, first, second):
        def after(s):
            if s == 4 and second:
                pool.wait_ge(self.s_ve, i)
                self.nc.gpsimd.tensor_tensor(self.rs, self.ve, self.c.pow7[:, 0:1], ALU.pow).then_inc(self.s_pow, 1)
        return after

    def shift_mean(self, dve, i):
        dve.wait_ge(self.s_pow, i)
        self.nc.vector.scalar_tensor_tensor(self.shift, self.mv[:, 0:1], -1.0, self.rs, ALU.mult, ALU.mult).then_inc(self.s_rs, 1)

    def end_tensor(self, pe):
        pass

    def end_vector(self, dve):
        pass

    def norm(self, act, i):
        act.wait_ge(self.s_rs, i)
        self.nc.scalar.activation(self.u, self.u, ACT.Identity, bias=self.shift[:, 0:1], scale=self.rs[:, 0:1])\
            .then_inc(self.s_hat, 1)

    def turn(self, pe, x, xt_bank):
        for h in range(KH):
            ins = self.nc.tensor.transpose(xt_bank[:, h * P:(h + 1) * P], x[:, h * P:(h + 1) * P], self.c.ident[:])
        ins.then_inc(self.s_turned, 1)

    def by_columns(self, weights):
        for m in range(KH):
            for h in range(KH):
                ins = self.nc.tensor.matmul(self.c.bank[1][:, m * P:(m + 1) * P], weights[:, h, m * P:(m + 1) * P],
                                            self.xt[:, h, :], start=(h == 0), stop=(h == KH - 1))
        ins.then_inc(self.s_mm, 1)


class Attend(RowsBehind):

    def __init__(self, nc, c, ph, w, ex):
        super().__init__(nc, c, ph, "attend", ex)
        cut = cutter(w)
        self.wq, self.kv, self.vec = cut(KH, D), cut(KH, P + 4), cut(2, D)
        self.x, self.xt, self.et, self.rt, self.z = cut(D), cut(KH, P), cut(KH, P), cut(KH, P), cut(KH, 4)
        self.done = self.cut_ex(D)
        self.s_x, self.s_q, self.s_den, self.s_rec = (ph.sem(f"attend_{n}") for n in ("loaded", "queries", "denominators", "reciprocals"))

    def sync(self, sp, a):
        c = self.c
        sp.dma_start(self.wq, c.wt_d[:, :, 0:D]).then_inc(self.s_in, 16)
        sp.dma_start(self.kv, c.kv_d).then_inc(self.s_in, 16)
        for j, n in enumerate(("ln1_g", "ln1_b")):
            sp.dma_start(self.vec[:, j, :], spread(a["L0_mix_" + n])).then_inc(self.s_in, 16)
        sp.sem_inc(self.s_dma, 16)

        def load(i):
            sp.wait_ge(self.s_u, i + 1)
            sp.dma_start(self.x, c.xn_d[ds(i * P, P), :]).then_inc(self.s_x, 16)

        def store(i):
            sp.wait_ge(self.s_done, i + 1)
            sp.dma_start(c.rows_d[ds(i * P, P), :], self.done).then_inc(self.s_dma, 16)

        load(0)
        with sp.Fori(0, NT - 1) as i:
            load(i + 1)
            store(i)
        store(NT - 1)
        sp.wait_ge(self.s_dma, 16 * (NT + 1))

    def begin_tensor(self, pe):
        pe.wait_ge(self.s_in, 64)
        for s in (self.s_turned, self.s_mm, self.s_mm2):
            pe.sem_inc(s, 1)

    def begin_scalar(self, act):
        act.sem_inc(self.s_act, 1)
        act.sem_inc(self.s_hat, 1)

    def end_scalar(self, act):
        act.wait_ge(self.s_dma, 16 * (NT + 1))

    def begin_vector(self, dve):
        dve.wait_ge(self.s_in, 64)
        dve.sem_inc(self.s_u, 1)

    def tensor(self, pe, i, first, second):
        c, t = self.c, self.nc.tensor

        def after(s):
            if s == 1 and first:
                pe.wait_ge(self.s_x, i * 16 + 16)
                gate(pe, c)
                self.turn(pe, self.x, c.bank[0])
            if s == 3 and first:
                pe.wait_ge(self.s_xt, i + 1)
                pe.wait_ge(self.s_act, i * 2 + 1)
                self.by_columns(self.wq)
            if s == 8 and first:
                pe.wait_ge(self.s_q, i + 1)
                pe.wait_ge(self.s_u, i + 1)
                for h in range(KH):
                    ins = t.matmul(c.bank[2][:, h * (P + 4):(h + 1) * (P + 4)], self.et[:, h, :], self.kv[:, h, :],
                                   start=True, stop=True)
                ins.then_inc(self.s_mm2, 1)
        return after

    def scalar(self, act, i, first, second):
        c, sc = self.c, self.nc.scalar
        flat = lambda x: x.rearrange("p h r -> p (h r)")
        if first:
            act.wait_ge(self.s_turned, i + 2)
            act.wait_ge(self.s_mm, i + 1)
            sc.copy(flat(self.xt), c.bank[0][:, 0:D]).then_inc(self.s_xt, 1)
            act.wait_ge(self.s_mm, i + 2)
            act.wait_ge(self.s_mm2, i + 1)
            sc.activation(flat(self.et), c.bank[1][:, 0:D], ACT.Exp).then_inc(self.s_act, 1)
            sc.activation(flat(self.rt), c.bank[1][:, 0:D], ACT.Relu).then_inc(self.s_act, 1)
        if second:
            self.norm(act, i)

    def vector(self, dve, i, first, second):
        v, c = self.nc.vector, self.c

        def after(s):
            if s == 5 and second:
                self.shift_mean(dve, i)
            if s == 6 and first:
                dve.wait_ge(self.s_act, i * 2 + 3)
                v.scalar_tensor_tensor(self.et, self.et, 1.0, self.rt, ALU.min, ALU.add).then_inc(self.s_q, 1)
            if s == 8 and second:
                dve.wait_ge(self.s_hat, i + 1)
                v.tensor_tensor(self.u, self.u, self.vec[:, 0, :], ALU.mult).then_inc(self.s_gam, 1)
                dve.wait_ge(self.s_gam, i)
                dve.wait_ge(self.s_dma, i * 16)
                v.tensor_tensor(self.done, self.u, self.vec[:, 1, :], ALU.add).then_inc(self.s_done, 1)
            if s == 11 and first:
                both = c.bank[2][:, 0:KH * (P + 4)].rearrange("p (s m) -> p s m", s=KH)
                dve.wait_ge(self.s_mm2, i + 2)
                v.tensor_scalar(self.z, both[:, :, P:], 1e-6, None, ALU.add).then_inc(self.s_den, 1)
                dve.wait_ge(self.s_den, i + 1)
                v.reciprocal(self.z, self.z).then_inc(self.s_rec, 1)
                dve.wait_ge(self.s_rec, i + 1)
                if second:
                    dve.wait_ge(self.s_done, i)
                v.tensor_tensor(self.u.rearrange("p (s j m) -> p s j m", s=KH, j=4),
                                both[:, :, 0:P].rearrange("p s (j m) -> p s j m", j=4),
                                self.z.unsqueeze(3).to_broadcast([P, KH, 4, 32]), ALU.mult).then_inc(self.s_t, 1)
                dve.wait_ge(self.s_t, i + 1)
                v.tensor_tensor(self.u, self.u, self.x, ALU.add).then_inc(self.s_u, 1)
                self.end_first(dve, i)
        return after


class Feed(RowsBehind):

    def __init__(self, nc, c, ph, w, ex):
        super().__init__(nc, c, ph, "feed", ex)
        cut = cutter(w)
        self.w1, self.w2, self.vec = cut(KH, D), cut(KH, D), cut(3, D)
        self.x, self.xt, self.ht = cut(D), cut(KH, P), cut(KH, P)
        self.b1 = self.cut_ex(KH)

    def sync(self, sp, a):
        c = self.c
        sp.dma_start(self.w1, c.wt_d[:, :, 3 * D:4 * D]).then_inc(self.s_in, 16)
        sp.dma_start(self.w2, c.wt_d[:, :, 4 * D:5 * D]).then_inc(self.s_in, 16)
        for j, n in enumerate(("b2", "ln2_g", "ln2_b")):
            sp.dma_start(self.vec[:, j, :], spread(a["L0_mix_" + n])).then_inc(self.s_in, 16)
        sp.dma_start(self.b1, a["L0_mix_b1"].rearrange("(h p) -> p h", p=P), allow_slow_non_contiguous=True).then_inc(self.s_in, 16)
        with sp.Fori(0, NT) as i:
            sp.wait_ge(self.s_u, i + 1)
            sp.dma_start(self.x, c.rows_d[ds(i * P, P), :]).then_inc(self.s_dma, 16)
        sp.wait_ge(self.s_done, NT)

    def begin_tensor(self, pe):
        pe.wait_ge(self.s_in, 96)
        for s in (self.s_turned, self.s_mm, self.s_mm2):
            pe.sem_inc(s, 1)

    def begin_scalar(self, act):
        act.wait_ge(self.s_in, 96)
        act.sem_inc(self.s_act, 1)
        act.sem_inc(self.s_hat, 1)

    def end_scalar(self, act):
        act.wait_ge(self.s_done, NT)

    def begin_vector(self, dve):
        dve.wait_ge(self.s_in, 96)
        dve.sem_inc(self.s_u, 1)

    def tensor(self, pe, i, first, second):
        c, t = self.c, self.nc.tensor

        def after(s):
            if s == 1 and first:
                pe.wait_ge(self.s_dma, i * 16 + 16)
                gate(pe, c)
                self.turn(pe, self.x, c.bank[0])
            if s == 3 and first:
                pe.wait_ge(self.s_xt, i + 1)
                pe.wait_ge(self.s_act, i * 2 + 1)
                self.by_columns(self.w1)
            if s == 6 and first:
                pe.wait_ge(self.s_act, i * 2 + 3)
                pe.wait_ge(self.s_u, i + 1)
                for h in range(KH):
                    ins = t.matmul(c.bank[2][:, 0:D], self.ht[:, h, :], self.w2[:, h, :], start=(h == 0), stop=(h == KH - 1))
                ins.then_inc(self.s_mm2, 1)
        return after

    def scalar(self, act, i, first, second):
        c, sc = self.c, self.nc.scalar
        if first:
            act.wait_ge(self.s_turned, i + 2)
            act.wait_ge(self.s_mm, i + 1)
            sc.copy(self.xt.rearrange("p h r -> p (h r)"), c.bank[0][:, 0:D]).then_inc(self.s_xt, 1)
            act.wait_ge(self.s_mm, i + 2)
            act.wait_ge(self.s_mm2, i + 1)
            for m in range(KH):
                sc.activation(self.ht[:, m, :], c.bank[1][:, m * P:(m + 1) * P], ACT.Gelu, bias=self.b1[:, m:m + 1])\
                    .then_inc(self.s_act, 1)
        if second:
            self.norm(act, i)

    def vector(self, dve, i, first, second):
        v, c = self.nc.vector, self.c

        def after(s):
            if s == 5 and second:
                self.shift_mean(dve, i)
            if s == 8 and second:
                dve.wait_ge(self.s_hat, i + 1)
                v.tensor_tensor(self.u, self.u, self.vec[:, 1, :], ALU.mult).then_inc(self.s_gam, 1)
                dve.wait_ge(self.s_gam, i)
                v.tensor_tensor(self.u, self.u, self.vec[:, 2, :], ALU.add).then_inc(self.s_bet, 1)
                dve.wait_ge(self.s_bet, i)
                gate(dve, c)
                at = c.res[:, ds((i - 1) * D, D)]
                v.tensor_tensor(at, at, self.u, ALU.add).then_inc(self.s_done, 1)
            if s == 9 and first:
                if second:
                    dve.wait_ge(self.s_done, i)
                dve.wait_ge(self.s_mm2, i + 2)
                v.tensor_tensor(self.u, c.bank[2][:, 0:D], self.x, ALU.add).then_inc(self.s_t, 1)
                dve.wait_ge(self.s_t, i + 1)
                v.tensor_tensor(self.u, self.u, self.vec[:, 0, :], ALU.add).then_inc(self.s_u, 1)
                self.end_first(dve, i)
        return after


def gnn0(nc, c, a):
    W, roots = a["L0_gnn_weights"], a["L0_gnn_roots"]
    with Phase(nc, "gnn0") as ph:
        sb = ph.sb
        msg = sb("msg", [P, SLOTS, D], F32)
        hot = sb("hot0", [P, SLOTS, P], F32)
        ex = sb("ex", [P, GT * D], F32)
        w = sb("w0", [P, KH, (REL0 + 1) * D], F32)
        vecs = sb("vecs", [P, 3, D], F32)
        row_ring = sb("row_ring", [P, 2, HALF], I32)
        meta_ring = sb("meta_ring", [P, 2, HALF, 2], F32)
        xt = hot[:].rearrange("p s e -> p (s e)")[:, 0:KH * GR].rearrange("p (h r) -> p h r", h=KH)
        flat_msg = msg[:].rearrange("p s d -> p (s d)")
        outs = flat_msg[:, 0:6 * 2 * D].rearrange("p (o n) -> p o n", o=6)
        stage = flat_msg[:, 6 * 2 * D:]
        edges = c.edges = EdgeSum(nc, c)
        edges.use(msg, hot, row_ring, meta_ring, c.row4, c.tab0_d, True)
        names = ("weights_in", "xt_ready", "tile_made", "roots_made", "bias_added", "partial", "variance",
                 "rstd", "sum", "normal", "gamma", "beta", "exp", "exp_cut", "elu", "state", "layer_tables", "staged", "vectors_in")
        (s_w, s_xt, s_out, s_root, s_bias, s_bn, s_mv, s_rs, s_tmp, s_nrm, s_gam, s_bet, s_exp, s_cut, s_elu,
         s_state, s_tabs, s_stage, s_vec) = (ph.sem(n) for n in names)
        s_store = [ph.sem(f"tables_stored{o}") for o in range(6)]
        behind = [Keys0(nc, c, ph, w[:].rearrange("p h n -> p (h n)"), ex[:]),
                  Attend(nc, c, ph, w[:].rearrange("p h n -> p (h n)"), ex[:]),
                  Feed(nc, c, ph, w[:].rearrange("p h n -> p (h n)"), ex[:])]
        turned = c.ledger.plan([0, 1, 0, 1], DEPTH * NG)
        turn = c.ledger.plan([2 + j % 2 for j in range(3 * GT)], DEPTH * NG)
        ways = [0, 1, 2, 3, 4, 0, 1, 5, 2, 3, 0, 1, 4, 5]
        per = [ways.count(o) for o in range(6)]
        stored = lambda m, q: (q * per[ways[m]] + ways[:m].count(ways[m]) + 1) * 16
        with nc.Block() as block:

            @block.sync
            def _(sp):
                def layer(l, work=None):
                    sp.wait_ge(s_tabs, l + 1)
                    for h in range(KH):
                        sp.dma_start(w[:, h, 0:REL0 * D].rearrange("p (r o) -> p r o", r=REL0),
                                     W.rearrange("l r i o -> (l r) i o")[ds(l * REL0, REL0), h * P:(h + 1) * P, :]
                                     .rearrange("r p o -> p r o")).then_inc(s_w, 16)
                        sp.dma_start(w[:, h, REL0 * D:], roots[ds(l, 1), h * P:(h + 1) * P, :]
                                     .rearrange("l p o -> p (l o)")).then_inc(s_w, 16)
                    with sp.Fori(0, NG) as g:
                        q = l * NG + g
                        for k in range(GT):
                            at = g * GR + k * P
                            for j in range(2):
                                o = ways[2 * k + j]
                                sp.wait_ge(s_out, q * (2 * GT) + (2 * k + j + 1))
                                sp.dma_start(c.tab0_d.rearrange("(r n) d -> n r d", n=NP)[ds(at, P), 2 * j:2 * j + 2, :],
                                             outs[:, o, :].rearrange("p (r d) -> p r d", d=D)).then_inc(s_store[o], 16)
                    sp.wait_ge(s_state, l * NG + NG)
                    for j, n in enumerate(("L0_gnn_biases", "L0_gnn_ln_gamma", "L0_gnn_ln_beta")):
                        sp.dma_start(vecs[:, j, :], a[n][ds(l, 1), :].to_broadcast([P, D])).then_inc(s_vec, 16)
                    if work:
                        sp.wait_ge(s_tabs, l + 2)
                        work.sync(sp, a)

                for l, work in enumerate(behind):
                    layer(l, work)
                with sp.Fori(len(behind), DEPTH) as l:
                    layer(l)

            @block.tensor
            def _(pe):
                def turn_chunk(n, q):
                    k0, m = CH[n]
                    pe.wait_ge(s_stage, q * 2 + (n + 1))
                    for h in range(KH):
                        b, t = turned(2 * n + h, q)
                        pe.wait_ge(c.bank_free[b], t)
                        gate(pe, c)
                        for k in range(k0, k0 + m):
                            ins = nc.tensor.transpose(c.bank[b][:, (k - k0) * P:(k - k0 + 1) * P],
                                                      stage[:, (k - k0) * D + h * P:(k - k0) * D + (h + 1) * P], c.ident[:])
                        ins.then_inc(c.bank_full[b], 1)

                def multiply(n, q):
                    k0, m = CH[n]
                    pe.wait_ge(s_xt, q * 2 + (n + 1))
                    for k in range(k0, k0 + m):
                        for j in range(3):
                            b, t = turn(3 * k + j, q)
                            pe.wait_ge(c.bank_free[b], t)
                            width = 512 if j < 2 else D
                            for h in range(KH):
                                ins = nc.tensor.matmul(c.bank[b][:, 0:width], xt[:, h, k * P:(k + 1) * P],
                                                       w[:, h, j * 512:j * 512 + width], start=(h == 0), stop=(h == KH - 1))
                            ins.then_inc(c.bank_full[b], 1)
                    return b, t

                pe.sem_inc(s_tabs, 1)
                pe.sem_inc(edges.summed, SLOTS)
                def layer(l, work=None):
                    pe.wait_ge(s_w, l * 64 + 64)
                    turn_chunk(0, l * NG)
                    with pe.Fori(0, NG - 1) as g:
                        turn_chunk(1, l * NG + g)
                        multiply(0, l * NG + g)
                        turn_chunk(0, l * NG + g + 1)
                        multiply(1, l * NG + g)
                    turn_chunk(1, l * NG + (NG - 1))
                    multiply(0, l * NG + (NG - 1))
                    b, t = multiply(1, l * NG + (NG - 1))
                    pe.wait_ge(c.bank_full[b], t)
                    pe.sem_inc(s_tabs, 1)
                    if work:
                        for b, t in (turned(2, l * NG + (NG - 1)), turned(3, l * NG + (NG - 1)),
                                     turn(3 * GT - 1, l * NG + (NG - 1))):
                            pe.wait_ge(c.bank_free[b], t + 1)
                        work.begin_tensor(pe)
                        bodies(pe, lambda i, first, second: edges.tensor(pe, l * BODIES + i, work.tensor(pe, i, first, second)))
                        work.end_tensor(pe)
                    else:
                        with pe.Fori(0, BODIES) as i:
                            edges.tensor(pe, l * BODIES + i)

                for l, work in enumerate(behind):
                    layer(l, work)
                with pe.Fori(len(behind), DEPTH) as l:
                    layer(l)

            @block.scalar
            def _(act):
                for o in range(6):
                    act.sem_inc(s_store[o], 16)
                def prepare(n, g, q):
                    k0, m = CH[n]
                    act.wait_ge(s_state, q + 1)
                    gate(act, c)
                    nc.scalar.copy(stage[:, 0:m * D], c.xn[:, ds(g * (GT * D) + k0 * D, m * D)]).then_inc(s_stage, 1)
                    for h in range(KH):
                        b, t = turned(2 * n + h, q)
                        act.wait_ge(c.bank_full[b], t)
                        nc.scalar.copy(xt[:, h, k0 * P:(k0 + m) * P], c.bank[b][:, 0:m * P]).then_inc(c.bank_free[b], 1)
                    act.wait_ge(c.bank_free[b], t + 1)
                    act.sem_inc(s_xt, 1)

                def way_out(n, g, q):
                    k0, m = CH[n]
                    for k in range(k0, k0 + m):
                        for j in range(2):
                            b, t = turn(3 * k + j, q)
                            o = ways[2 * k + j]
                            act.wait_ge(s_store[o], stored(2 * k + j, q))
                            act.wait_ge(c.bank_full[b], t)
                            nc.scalar.copy(outs[:, o, :], c.bank[b][:]).then_inc(s_out, 1)
                            act.wait_ge(s_out, q * (2 * GT) + (2 * k + j + 1))
                            act.sem_inc(c.bank_free[b], 1)
                        b, t = turn(3 * k + 2, q)
                        act.wait_ge(c.bank_full[b], t)
                        gate(act, c)
                        nc.scalar.copy(tile_of(c.agg, g, k), c.bank[b][:, 0:D]).then_inc(s_root, 1)
                        act.wait_ge(s_root, q * GT + (k + 1))
                        act.sem_inc(c.bank_free[b], 1)

                def tables(g, q):
                    prepare(1, g, q)
                    way_out(0, g, q)
                    prepare(0, g + 1, q + 1)
                    way_out(1, g, q)

                def last_tables(q):
                    prepare(1, NG - 1, q)
                    way_out(0, NG - 1, q)
                    way_out(1, NG - 1, q)

                def exponential(g, q):
                    act.wait_ge(s_bet, q + 1)
                    act.wait_ge(s_elu, q + 1)
                    gate(act, c)
                    nc.scalar.activation(ex[:], c.agg[:, ds(g * (GT * D), GT * D)], ACT.Exp).then_inc(s_exp, 1)

                prepare(0, 0, 0)
                with act.Fori(0, NG - 1) as g:
                    tables(g, g)
                last_tables(NG - 1)
                def layer(l, work=None):
                    if work:
                        work.begin_scalar(act)

                        def body(i, first, second):
                            edges.scalar(act, i, l * BODIES + i)
                            work.scalar(act, i, first, second)

                        bodies(act, body)
                        work.end_scalar(act)
                    else:
                        with act.Fori(0, BODIES) as i:
                            edges.scalar(act, i, l * BODIES + i)
                    for g in range(2):
                        exponential(g, l * NG + g)
                    prepare(0, 0, l * NG + NG)
                    with act.Fori(0, NG - 2) as g:
                        exponential(g + 2, l * NG + g + 2)
                        tables(g, l * NG + g + NG)
                    tables(NG - 2, l * NG + (2 * NG - 2))
                    last_tables(l * NG + (2 * NG - 1))

                for l, work in enumerate(behind):
                    layer(l, work)
                for l in range(len(behind), DEPTH - 1):
                    layer(l)
                with act.Fori(0, BODIES) as i:
                    edges.scalar(act, i, (DEPTH - 1) * BODIES + i)
                with act.Fori(0, NG) as g:
                    exponential(g, (DEPTH - 1) * NG + g)

            @block.gpsimd
            def _(pool):
                def layer(l, work=None):
                    for o in range(6):
                        pool.wait_ge(s_store[o], (l + 1) * (NG * per[o] * 16) + 16)
                    gate(pool, c)
                    if work:
                        bodies(pool, lambda i, first, second: edges.gpsimd(pool, l * BODIES + i,
                                                                   work.gpsimd(pool, i, first, second)))
                    else:
                        with pool.Fori(0, BODIES) as i:
                            edges.gpsimd(pool, l * BODIES + i)
                    pool.wait_ge(edges.added, (l + 1) * STEPS + 4)
                    pool.wait_ge(s_vec, l * 48 + 48)
                    gate(pool, c)
                    with pool.Fori(0, NG) as g:
                        q = l * NG + g
                        gate(pool, c)
                        x = group(c.agg, g)
                        nc.gpsimd.tensor_tensor(x, x, vecs[:, 0:1, :].to_broadcast([P, GT, D]), ALU.add).then_inc(s_bias, 1)
                        rstd(pool, c, q, s_mv, s_rs, s_tmp)
                        pool.wait_ge(s_nrm, (q + 1) * GT)
                        gate(pool, c)
                        nc.gpsimd.tensor_tensor(x, x, vecs[:, 1:2, :].to_broadcast([P, GT, D]), ALU.mult).then_inc(s_gam, 1)

                for l, work in enumerate(behind):
                    layer(l, work)
                with pool.Fori(len(behind), DEPTH) as l:
                    layer(l)

            @block.vector
            def _(dve):
                v = nc.vector
                dve.sem_inc(edges.added, 4)
                dve.sem_inc(s_state, NG)
                dve.sem_inc(s_elu, 1)
                def layer(l, work=None):
                    dve.wait_ge(s_root, (l + 1) * NT)
                    gate(dve, c)
                    edges.begin_vector(dve, l * BODIES)
                    if work:
                        work.begin_vector(dve)
                        bodies(dve, lambda i, first, second: edges.vector(dve, i, l * BODIES + i,
                                                                   work.vector(dve, i, first, second), is_last(i)))
                        work.end_vector(dve)
                    else:
                        with dve.Fori(0, BODIES - 1) as i:
                            edges.vector(dve, i, l * BODIES + i)
                        edges.vector(dve, BODIES - 1, l * BODIES + (BODIES - 1), last=True)
                    with dve.Fori(0, NG) as g:
                        q = l * NG + g
                        tile = lambda k: tile_of(c.agg, g, k)
                        dve.wait_ge(s_bias, q + 1)
                        gate(dve, c)
                        stats(dve, c, tile, q, s_bn, s_mv)
                        normalise(dve, c, tile, tile, q, s_rs, s_nrm)
                        dve.wait_ge(s_gam, q + 1)
                        x = group(c.agg, g)
                        v.tensor_tensor(x, x, vecs[:, 2:3, :].to_broadcast([P, GT, D]), ALU.add).then_inc(s_bet, 1)
                        dve.wait_ge(s_exp, q + 1)
                        v.tensor_scalar(ex[:], ex[:], 1.0, -1.0, ALU.min, ALU.add).then_inc(s_cut, 1)
                        dve.wait_ge(s_cut, q + 1)
                        flat = lambda r: r[:, ds(g * (GT * D), GT * D)]
                        v.scalar_tensor_tensor(flat(c.agg), flat(c.agg), 0.0, ex[:], ALU.max, ALU.add).then_inc(s_elu, 1)
                        dve.wait_ge(s_elu, q + 2)
                        v.tensor_tensor(flat(c.xn), flat(c.xn), flat(c.agg), ALU.add).then_inc(s_state, 1)

                for l, work in enumerate(behind):
                    layer(l, work)
                with dve.Fori(len(behind), DEPTH) as l:
                    layer(l)


def spread(dram_vec, n=D):
    return dram_vec.rearrange("(a n) -> a n", a=1).to_broadcast([P, n])


def weights0(nc, c, a, wt):
    nat = c.agg[:, 0:10 * D].rearrange("p (b i) -> p b i", i=D)
    with Phase(nc, "weights0") as ph:
        s_in, = ph.sems("natural_in")
        turn = c.ledger.plan([0, 1, 2, 3, 4], 1)
        with nc.Block() as block:

            @block.sync
            def _(sp):
                for name, b, n in (("L0_mix_Wqkv", 0, 6), ("L0_mix_W1", 6, 2), ("L0_mix_W2", 8, 2)):
                    sp.dma_start(nat[:, b:b + n, :], a[name].rearrange("(b p) i -> p b i", p=P)).then_inc(s_in, 16)

            @block.tensor
            def _(pe):
                pe.wait_ge(s_in, 48)
                for j in range(5):
                    b, t = turn(j, 0)
                    pe.wait_ge(c.bank_free[b], t)
                    for h in range(KH):
                        for n in range(2):
                            ins = nc.tensor.transpose(c.bank[b][:, (2 * h + n) * P:(2 * h + n + 1) * P],
                                                      nat[:, 2 * j + n, h * P:(h + 1) * P], c.ident[:])
                    ins.then_inc(c.bank_full[b], 1)

            @block.scalar
            def _(act):
                for j in range(5):
                    b, t = turn(j, 0)
                    act.wait_ge(c.bank_full[b], t)
                    nc.scalar.copy(wt[:, :, j * D:(j + 1) * D],
                                   c.bank[b][:].rearrange("p (h o) -> p h o", h=KH)).then_inc(c.bank_free[b], 1)


def norm0(nc, c, wt):
    with Phase(nc, "norm0") as ph:
        s_bn, s_mv, s_rs, s_tmp, s_nrm, s_out = ph.sems("partial variance rstd sum normal weights_parked")
        with nc.Block() as block:

            @block.sync
            def _(sp):
                sp.dma_start(c.wt_d, wt[:]).then_inc(s_out, 16)
                sp.wait_ge(s_out, 16)

            @block.gpsimd
            def _(pool):
                with pool.Fori(0, NG) as g:
                    rstd(pool, c, g, s_mv, s_rs, s_tmp)

            @block.vector
            def _(dve):
                with dve.Fori(0, NG) as g:
                    stats(dve, c, lambda k: tile_of(c.res, g, k), g, s_bn, s_mv)
                    normalise(dve, c, lambda k: tile_of(c.xn, g, k), lambda k: tile_of(c.res, g, k), g, s_rs, s_nrm)


class Mlp:
    NU = 4 + 16 + 4
    BANKS = [j % 8 for j in range(NU)]

    def __init__(self, nc, c, ph, turn, stage, cut, w1, w2, b1, act_fn):
        self.nc, self.c, self.turn, self.stage, self.w1, self.w2, self.b1, self.fn = nc, c, turn, stage, w1, w2, b1, act_fn
        self.xt = cut(KH, GR)
        self.ht = [cut(8, w * P) for _, w in CH]
        self.s_xt, self.s_hid, self.s_used = ph.sems("mlp_xt mlp_hidden mlp_hidden_used")

    def tensor(self, pe, g):
        nc, c, turn = self.nc, self.c, self.turn
        transposed(pe, c, lambda k, h: self.stage[:, k, h * P:(h + 1) * P], turn, 0, g)
        pe.wait_ge(self.s_xt, g + 1)
        for n, (k0, w) in enumerate(CH):
            for m in range(8):
                b, t = turn(4 + 8 * n + m, g)
                pe.wait_ge(c.bank_free[b], t)
                for h in range(KH):
                    ins = nc.tensor.matmul(c.bank[b][:, 0:w * P], self.w1[:, h, m * P:(m + 1) * P],
                                           self.xt[:, h, k0 * P:(k0 + w) * P], start=(h == 0), stop=(h == KH - 1))
                ins.then_inc(c.bank_full[b], 1)
        for n, (k0, w) in enumerate(CH):
            pe.wait_ge(self.s_hid, g * 16 + (8 * n + 8))
            for r in range(2):
                b, t = turn(20 + 2 * n + r, g)
                pe.wait_ge(c.bank_free[b], t)
                for k in range(2 * r, min(2 * r + 2, w)):
                    for m in range(8):
                        ins = nc.tensor.matmul(c.bank[b][:, (k % 2) * D:(k % 2 + 1) * D], self.ht[n][:, m, k * P:(k + 1) * P],
                                               self.w2[:, m, :], start=(m == 0), stop=(m == 7))
                ins.then_inc(c.bank_full[b], 1)
        pe.wait_ge(c.bank_full[b], t)
        pe.sem_inc(self.s_used, 1)

    def scalar(self, act, g):
        nc, c, turn = self.nc, self.c, self.turn
        act.wait_ge(self.s_used, g + 1)
        evacuate_transposed(act, c, self.xt, turn, 0, g, self.s_xt)
        for n, (k0, w) in enumerate(CH):
            for m in range(8):
                b, t = turn(4 + 8 * n + m, g)
                act.wait_ge(c.bank_full[b], t)
                nc.scalar.activation(self.ht[n][:, m, :], c.bank[b][:, 0:w * P], self.fn, bias=self.b1[:, m:m + 1])\
                    .then_inc(self.s_hid, 1)
                act.wait_ge(self.s_hid, g * 16 + (8 * n + m + 1))
                act.sem_inc(c.bank_free[b], 1)

    def pairs(self):
        return [(20 + 2 * n + r, k0 + 2 * r, min(2, w - 2 * r)) for n, (k0, w) in enumerate(CH) for r in range(2)]


def ffn0(nc, c, a, score):
    with Phase(nc, "ffn0") as ph:
        cut = carver(c.agg)
        stage, junk = cut(GT, D), cut(D)
        w1, w2, b1 = ph.sb("w1", [P, KH, 4 * D]), ph.sb("w2", [P, 8, D]), ph.sb("b1", [P, 8])
        vec, br, sc = ph.sb("vec", [P, 2, D]), ph.sb("br", [P, 1]), ph.sb("sc", [P, GT])
        turn = c.ledger.plan(Mlp.BANKS, NG)
        mlp = Mlp(nc, c, ph, turn, stage, cut, w1, w2, b1, ACT.Gelu_apprx_tanh)
        s_in, s_x1, s_bn, s_mv, s_rs, s_tmp, s_nrm, s_sc, s_scb, s_base, s_yb, s_y = ph.sems(
            "weights_in sum_made partial variance rstd sum normal score score_biased base_made y_biased y_scaled")
        with nc.Block() as block:

            @block.sync
            def _(sp):
                for h in range(KH):
                    sp.dma_start(w1[:, h, :], a["L0_ffn_w1"][h * P:(h + 1) * P, :]).then_inc(s_in, 16)
                sp.dma_start(w2[:], a["L0_ffn_w2"].rearrange("(m p) o -> p m o", p=P)).then_inc(s_in, 16)
                sp.dma_start(b1[:], a["L0_ffn_b1"].rearrange("(m p) -> p m", p=P), allow_slow_non_contiguous=True).then_inc(s_in, 16)
                sp.dma_start(vec[:, 0, :], a["L0_ffn_wr"].rearrange("d o -> o d").to_broadcast([P, D]),
                             allow_slow_non_contiguous=True).then_inc(s_in, 16)
                sp.dma_start(vec[:, 1, :], spread(a["L0_ffn_b2"])).then_inc(s_in, 16)
                sp.dma_start(br[:], spread(a["L0_ffn_br"], 1)).then_inc(s_in, 16)

            @block.tensor
            def _(pe):
                pe.sem_inc(mlp.s_used, 1)
                pe.wait_ge(s_in, 7 * 16)
                with pe.Fori(0, NG) as g:
                    pe.wait_ge(s_nrm, (g + 1) * GT)
                    mlp.tensor(pe, g)

            @block.scalar
            def _(act):
                act.wait_ge(s_in, 7 * 16)
                with act.Fori(0, NG) as g:
                    mlp.scalar(act, g)

            @block.gpsimd
            def _(pool):
                with pool.Fori(0, NG) as g:
                    rstd(pool, c, g, s_mv, s_rs, s_tmp)

            @block.vector
            def _(dve):
                v = nc.vector
                dve.wait_ge(s_in, 7 * 16)
                with dve.Fori(0, NG) as g:
                    v.tensor_tensor(group(c.res, g), group(c.res, g), group(c.xn, g), ALU.add).then_inc(s_x1, 1)
                    dve.wait_ge(s_x1, g + 1)
                    gate(dve, c)
                    stats(dve, c, lambda k: tile_of(c.res, g, k), g, s_bn, s_mv)
                    normalise(dve, c, lambda k: stage[:, k, :], lambda k: tile_of(c.res, g, k), g, s_rs, s_nrm)
                    dve.wait_ge(s_nrm, (g + 1) * GT)
                    for k in range(GT):
                        if k:
                            dve.wait_ge(s_sc, g * GT + k)
                        v.tensor_tensor_reduce(junk, stage[:, k, :], vec[:, 0, :], 1.0, 0.0, ALU.mult, ALU.add,
                                               sc[:, k:k + 1]).then_inc(s_sc, 1)
                    dve.wait_ge(s_sc, g * GT + GT)
                    v.tensor_scalar(sc[:], sc[:], br[:, 0:1], None, ALU.add).then_inc(s_scb, 1)
                    dve.wait_ge(s_scb, g * 2 + 1)
                    v.tensor_scalar(score[:, ds(g * GT, GT)], sc[:], 1.0, None, ALU.mult).then_inc(s_scb, 1)
                    v.tensor_tensor(group(c.res, g), group(c.res, g), stage[:], ALU.add).then_inc(s_base, 1)
                    dve.wait_ge(s_base, g + 1)
                    for n, (j, k, w) in enumerate(mlp.pairs()):
                        b, t = turn(j, g)
                        dve.wait_ge(c.bank_full[b], t)
                        v.tensor_tensor(stage[:, k:k + w, :], c.bank[b][:, 0:w * D].rearrange("p (k d) -> p k d", d=D),
                                        vec[:, 1:2, :].to_broadcast([P, w, D]), ALU.add).then_inc(s_yb, 1)
                        dve.wait_ge(s_yb, g * 4 + (n + 1))
                        dve.sem_inc(c.bank_free[b], 1)
                        for i in range(k, k + w):
                            v.tensor_scalar(tile_of(c.xn, g, i), stage[:, i, :], sc[:, i:i + 1], None, ALU.mult).then_inc(s_y, 1)
                    dve.wait_ge(s_y, (g + 1) * GT)
                    gate(dve, c)


def select(nc, c, score, take):
    ROUNDS = 64
    with Phase(nc, "select") as ph:
        lo, hi, mid, cnt, up, dn, top = (ph.sb(n, [P, 1]) for n in ("lo", "hi", "mid", "cnt", "up", "dn", "top"))
        junk, above, equal, off, off2, lim = (ph.sb(n, [P, NT]) for n in ("junk", "above", "equal", "off", "off2", "lim"))
        before = ph.sb("before", [P, P])
        s_v, s_max, s_cnt, s_tot = ph.sems("vector_steps maximum counted totalled")
        s_hi, s_lo, s_mid, s_ud = ph.sems("high low middle up_down")
        s_rank, = ph.sems("ranked")
        turn = c.ledger.plan([0, 1], 1)
        with nc.Block() as block:

            @block.gpsimd
            def _(pool):
                pool.wait_ge(s_v, 2)
                nc.gpsimd.partition_all_reduce(hi[:], top[:], P, bass.bass_isa.ReduceOp.max).then_inc(s_max, 1)

            @block.tensor
            def _(pe):
                with pe.Fori(0, ROUNDS) as i:
                    pe.wait_ge(s_cnt, i + 1)
                    nc.tensor.matmul(c.bank[2][:, 0:1], c.ones[:], cnt[:], start=True, stop=True).then_inc(s_tot, 1)
                pe.wait_ge(s_rank, 1)
                nc.tensor.matmul(c.bank[0][:, 0:NT], before[:], equal[:], start=True, stop=True)
                nc.tensor.matmul(c.bank[0][:, 64:64 + NT], c.ones[:], equal[:], start=True, stop=True)
                nc.tensor.matmul(c.bank[0][:, 128:129], c.ones[:], cnt[:], start=True, stop=True).then_inc(c.bank_full[0], 1)

            @block.vector
            def _(dve):
                v = nc.vector
                done = [0]

                def then(ins):
                    done[0] += 1
                    ins.then_inc(s_v, 1)
                    dve.wait_ge(s_v, done[0])

                then(v.tensor_tensor(junk[:], score[:], c.real[:], ALU.mult))
                then(v.tensor_reduce(top[:], junk[:], AX.X, ALU.max, apply_absolute_value=True))
                then(v.tensor_scalar(off[:], c.real[:], -1.0, BIG, ALU.add, ALU.mult))
                then(v.tensor_tensor(score[:], junk[:], off[:], ALU.add))
                then(v.tensor_scalar(before[:], c.iota[:], c.row_no[:, 0:1], None, ALU.is_gt))
                dve.wait_ge(s_max, 1)
                then(v.tensor_scalar(lo[:], hi[:], -1.0, None, ALU.mult))
                then(v.tensor_scalar(hi[:], hi[:], 1.0001, 1e-30, ALU.mult, ALU.add))
                dve.sem_inc(s_hi, 1)
                dve.sem_inc(s_lo, 1)
                with dve.Fori(0, ROUNDS) as i:
                    dve.wait_ge(s_hi, i + 1)
                    dve.wait_ge(s_lo, i + 1)
                    v.tensor_scalar(mid[:], lo[:], hi[:, 0:1], 0.5, ALU.add, ALU.mult).then_inc(s_mid, 1)
                    dve.wait_ge(s_mid, i + 1)
                    v.tensor_scalar(junk[:], score[:], mid[:, 0:1], 0.0, ALU.is_ge, ALU.add, accum_out=cnt[:]).then_inc(s_cnt, 1)
                    dve.wait_ge(s_tot, i + 1)
                    v.tensor_scalar(up[:], c.bank[2][:, 0:1], float(KK), BIG, ALU.is_ge, ALU.mult).then_inc(s_ud, 1)
                    v.tensor_scalar(dn[:], c.bank[2][:, 0:1], float(KK), -BIG, ALU.is_lt, ALU.mult).then_inc(s_ud, 1)
                    dve.wait_ge(s_ud, i * 2 + 2)
                    v.scalar_tensor_tensor(hi[:], up[:], mid[:, 0:1], hi[:], ALU.add, ALU.min).then_inc(s_hi, 1)
                    v.scalar_tensor_tensor(lo[:], dn[:], mid[:, 0:1], lo[:], ALU.add, ALU.max).then_inc(s_lo, 1)
                dve.wait_ge(s_hi, ROUNDS + 1)
                dve.wait_ge(s_lo, ROUNDS + 1)
                then(v.tensor_scalar(above[:], score[:], hi[:, 0:1], 0.0, ALU.is_ge, ALU.add, accum_out=cnt[:]))
                then(v.tensor_scalar(equal[:], score[:], lo[:, 0:1], None, ALU.is_ge))
                v.tensor_tensor(equal[:], equal[:], above[:], ALU.subtract).then_inc(s_rank, 1)
                dve.wait_ge(c.bank_full[0], turn(0, 0)[1])
                then(v.tensor_copy(off[:], c.bank[0][:, 64:64 + NT]))
                x, y, s = off, off2, 1
                while s < NT:
                    then(v.tensor_copy(y[:, 0:s], x[:, 0:s]))
                    then(v.tensor_tensor(y[:, s:NT], x[:, s:NT], x[:, 0:NT - s], ALU.add))
                    x, y, s = y, x, 2 * s
                then(v.tensor_tensor(x[:], x[:], c.bank[0][:, 64:64 + NT], ALU.subtract))
                then(v.tensor_tensor(x[:], x[:], c.bank[0][:, 0:NT], ALU.add))
                then(v.tensor_scalar(x[:], x[:], c.bank[0][:, 128:129], float(KK), ALU.add, ALU.is_lt))
                then(v.tensor_tensor(x[:], x[:], equal[:], ALU.mult))
                then(v.tensor_tensor(take[:], x[:], above[:], ALU.add))
                dve.sem_inc(c.bank_free[0], 1)
                dve.sem_inc(c.bank_free[1], 1)
                dve.sem_inc(c.bank_full[1], 1)


def weights1(nc, c, a, names, nat, wt):
    J = len(names)
    with Phase(nc, "weights1" + names[0]) as ph:
        s_in, = ph.sems("natural_in")
        turn = c.ledger.plan(list(range(J)), 1)
        with nc.Block() as block:

            @block.sync
            def _(sp):
                for j, n in enumerate(names):
                    sp.dma_start(nat[:, 2 * j:2 * j + 2, :], a["L1_mix_" + n].rearrange("(b p) i -> p b i", p=P)).then_inc(s_in, 16)

            @block.tensor
            def _(pe):
                pe.wait_ge(s_in, 16 * J)
                for j in range(J):
                    b, t = turn(j, 0)
                    pe.wait_ge(c.bank_free[b], t)
                    for h in range(KH):
                        for n in range(2):
                            ins = nc.tensor.transpose(c.bank[b][:, (2 * h + n) * P:(2 * h + n + 1) * P],
                                                      nat[:, 2 * j + n, h * P:(h + 1) * P], c.ident[:])
                    ins.then_inc(c.bank_full[b], 1)

            @block.scalar
            def _(act):
                for j in range(J):
                    b, t = turn(j, 0)
                    act.wait_ge(c.bank_full[b], t)
                    nc.scalar.copy(wt[:, :, j * D:(j + 1) * D],
                                   c.bank[b][:].rearrange("p (h o) -> p h o", h=KH)).then_inc(c.bank_free[b], 1)


def tables1(nc, c, a, take):
    W = a["L1_gnn_weight"]
    with Phase(nc, "tables1") as ph:
        cut = carver(c.agg)
        stage, xt, outs = cut(GT, D), cut(KH, GR), cut(4, 4 * D)
        w = ph.sb("w", [P, KH, REL1 * D])
        s_in, s_xt, s_half, s_half2, s_xtu, s_copy, s_x2, s_bn, s_mv, s_rs, s_tmp, s_nrm, s_msk = ph.sems(
            "weights_in xt halves_made other_halves_made xt_used copied x_made partial variance rstd sum normal masked")
        s_store = [ph.sem(f"stored{o}") for o in range(4)]
        turn = c.ledger.plan([j % 8 for j in range(4 + 4 * GT)], NG)
        per = [4, 4, 3, 3]
        with nc.Block() as block:

            @block.sync
            def _(sp):
                for h in range(KH):
                    sp.dma_start(w[:, h, :].rearrange("p (r o) -> p r o", r=REL1),
                                 W[:, h * P:(h + 1) * P, :].rearrange("r p o -> p r o")).then_inc(s_in, 16)
                for o in range(4):
                    sp.sem_inc(s_store[o], 16)
                tab = c.tab1_d.rearrange("(r n) d -> n r d", n=NP)
                with sp.Fori(0, NG) as g:
                    for k in range(GT):
                        at = ds(g * GR + k * P, P)
                        for half, s in ((0, s_half), (1, s_half2)):
                            o = (k % 2) * 2 + half
                            sp.wait_ge(s, g * (2 * GT) + (2 * k + 2))
                            sp.dma_start(tab[at, 4 * half:4 * half + 4, :], outs[:, o, :].rearrange("p (r d) -> p r d", d=D))\
                                .then_inc(s_store[o], 16)
                for o in range(4):
                    sp.wait_ge(s_store[o], 16 + 16 * NG * per[o])

            @block.tensor
            def _(pe):
                pe.sem_inc(s_xtu, 1)
                pe.wait_ge(s_in, 32)
                with pe.Fori(0, NG) as g:
                    pe.wait_ge(s_nrm, (g + 1) * GT)
                    pe.wait_ge(s_msk, g + 1)
                    transposed(pe, c, lambda k, h: stage[:, k, h * P:(h + 1) * P], turn, 0, g)
                    pe.wait_ge(s_xt, g + 2)
                    for k in range(GT):
                        for j in range(4):
                            b, t = turn(4 + 4 * k + j, g)
                            pe.wait_ge(c.bank_free[b], t)
                            for h in range(KH):
                                ins = nc.tensor.matmul(c.bank[b][:], xt[:, h, k * P:(k + 1) * P], w[:, h, j * 512:(j + 1) * 512],
                                                       start=(h == 0), stop=(h == KH - 1))
                            ins.then_inc(c.bank_full[b], 1)
                    pe.wait_ge(c.bank_full[b], t)
                    pe.sem_inc(s_xtu, 1)

            def out(eng, copy, g, k, j, s):
                b, t = turn(4 + 4 * k + j, g)
                o = (k % 2) * 2 + j // 2
                if j % 2 == 0:
                    eng.wait_ge(s_store[o], (g * per[o] + k // 2 + 1) * 16)
                eng.wait_ge(c.bank_full[b], t)
                copy(outs[:, o, (j % 2) * 512:(j % 2 + 1) * 512], c.bank[b][:]).then_inc(s, 1)
                eng.wait_ge(s, g * (2 * GT) + (2 * k + j % 2 + 1))
                eng.sem_inc(c.bank_free[b], 1)

            @block.scalar
            def _(act):
                act.sem_inc(s_xt, 1)
                act.sem_inc(s_copy, 1)
                with act.Fori(0, NG) as g:
                    act.wait_ge(s_xtu, g + 1)
                    evacuate_transposed(act, c, xt, turn, 0, g, s_xt)
                    act.wait_ge(s_nrm, (g + 1) * GT)
                    act.wait_ge(s_msk, g + 1)
                    gate(act, c)
                    nc.scalar.copy(group(c.xn, g), stage).then_inc(s_copy, 1)
                    for k in range(GT):
                        for j in range(2):
                            out(act, nc.scalar.copy, g, k, j, s_half)

            @block.gpsimd
            def _(pool):
                with pool.Fori(0, NG) as g:
                    rstd(pool, c, g, s_mv, s_rs, s_tmp)

            @block.vector
            def _(dve):
                v = nc.vector

                def norm(g):
                    for k in range(GT):
                        v.scalar_tensor_tensor(tile_of(c.res, g, k), tile_of(c.xn, g, k), take[:, ds(g * GT + k, 1)],
                                               tile_of(c.res, g, k), ALU.mult, ALU.add).then_inc(s_x2, 1)
                    dve.wait_ge(s_x2, (g + 1) * GT)
                    gate(dve, c)
                    stats(dve, c, lambda k: tile_of(c.res, g, k), g, s_bn, s_mv)
                    dve.wait_ge(s_copy, g + 1)
                    dve.wait_ge(s_xt, g + 1)
                    normalise(dve, c, lambda k: stage[:, k, :], lambda k: tile_of(c.res, g, k), g, s_rs, s_nrm)
                    dve.wait_ge(s_nrm, (g + 1) * GT)
                    last = stage[:, GT - 1, :]
                    gate(dve, c)
                    v.tensor_scalar(last, last, c.real[:, ds(g * GT + (GT - 1), 1)], None, ALU.mult).then_inc(s_msk, 1)

                def outs_of(g, k):
                    for j in range(2, 4):
                        out(dve, v.tensor_copy, g, k, j, s_half2)

                norm(0)
                with dve.Fori(0, NG - 1) as g:
                    for k in range(GT):
                        outs_of(g, k)
                        if k == 1:
                            norm(g + 1)
                for k in range(GT):
                    outs_of(NG - 1, k)


class Keys1:
    HD, NH = 64, 8

    def __init__(self, nc, c, ph, wt):
        self.nc, self.c, self.wt = nc, c, wt
        NH = self.NH
        self.x, self.xt = ph.sb("x", [P, D]), ph.sb("xt", [P, KH, P])
        self.hat = ph.sb("hat", [P, NH, self.HD])
        self.bn, self.mv = ph.sb("kv_bn", [P, NH, 6]), ph.sb("kv_mv", [P, NH, 2])
        self.ve, self.rs, self.shift, self.power = (ph.sb(n, [P, NH]) for n in ("kv_ve", "kv_rs", "kv_shift", "kv_power"))
        self.zero = ph.sb("zero", [P, D + KH])
        (self.s_set, self.s_x, self.s_turned, self.s_xt, self.s_kv, self.s_bn, self.s_mv, self.s_ve, self.s_rs, self.s_hat,
         self.s_sum, self.s_pow) = ph.sems("kv_set tile_staged tile_turned tile_xt keys_made keys_partial keys_variance keys_variance_eps keys_rstd "
                               "keys_normal keys_summed powers")

    def scalar(self, act, i, first, second):
        if first:
            self.stage(act, i)
        if second:
            act.wait_ge(self.s_sum, i)
            act.wait_ge(self.s_rs, i)
            for n in range(self.NH):
                self.nc.scalar.activation(self.hat[:, n, :], self.c.bank[1][:, n * self.HD:(n + 1) * self.HD], ACT.Identity,
                                          bias=self.shift[:, n:n + 1], scale=self.rs[:, n:n + 1]).then_inc(self.s_hat, 1)

    def stage(self, act, i):
        act.wait_ge(self.s_turned, i + 1)
        gate(act, self.c)
        self.nc.scalar.copy(self.x[:], self.c.xn[:, ds(i * D, D)]).then_inc(self.s_x, 1)
        act.wait_ge(self.s_turned, i + 2)
        act.wait_ge(self.s_kv, i + 1)
        self.nc.scalar.copy(self.xt[:].rearrange("p h r -> p (h r)"), self.c.bank[0][:, 0:D]).then_inc(self.s_xt, 1)

    def begin_tensor(self, pe):
        t = self.nc.tensor
        pe.sem_inc(self.s_turned, 1)
        pe.sem_inc(self.s_kv, 1)
        pe.sem_inc(self.s_sum, 1)
        pe.wait_ge(self.s_set, 2)
        t.matmul(self.c.bank[2][:, 0:D + KH], self.c.ones[:], self.zero[:], start=True, stop=False)
        t.matmul(self.c.bank[3][:, 0:D], self.c.ones[:], self.zero[:, 0:D], start=True, stop=False)

    def end_tensor(self, pe):
        t = self.nc.tensor
        t.matmul(self.c.bank[2][:, 0:D + KH], self.c.ones[:], self.zero[:], start=False, stop=True)
        t.matmul(self.c.bank[3][:, 0:D], self.c.ones[:], self.zero[:, 0:D], start=False, stop=True).then_inc(self.s_sum, 1)

    def turn(self, pe, i):
        pe.wait_ge(self.s_x, i + 1)
        gate(pe, self.c)
        for h in range(KH):
            ins = self.nc.tensor.transpose(self.c.bank[0][:, h * P:(h + 1) * P], self.x[:, h * P:(h + 1) * P], self.c.ident[:])
        ins.then_inc(self.s_turned, 1)

    def keys(self, pe, i):
        pe.wait_ge(self.s_xt, i + 1)
        pe.wait_ge(self.s_hat, i * self.NH + 1)
        for h in range(KH):
            ins = self.nc.tensor.matmul(self.c.bank[1][:], self.xt[:, h, :], self.wt[:, h, :], start=(h == 0), stop=(h == KH - 1))
        ins.then_inc(self.s_kv, 1)

    def sums(self, pe, i):
        t, c = self.nc.tensor, self.c
        flat = self.hat[:].rearrange("p i e -> p (i e)")
        pe.wait_ge(self.s_hat, (i + 1) * self.NH + 1)
        for s in range(KH):
            vs = flat[:, D + s * P:D + (s + 1) * P]
            t.matmul(c.bank[2][:, s * P:(s + 1) * P], vs, flat[:, s * P:(s + 1) * P], start=False, stop=False)
            t.matmul(c.bank[2][:, D + s:D + s + 1], vs, c.ones[:, 0:1], start=False, stop=False)
        t.matmul(c.bank[3][:, 0:D], c.ones[:], flat[:, 0:D], start=False, stop=False).then_inc(self.s_sum, 1)

    def tensor(self, pe, i, first, second):
        def after(s):
            if s == 1 and first:
                self.turn(pe, i)
            if s == 8 and second:
                self.sums(pe, i - 1)
            if s == 10 and first:
                self.keys(pe, i)
        return after

    def gpsimd(self, pool, i, second):
        def after(s):
            if s == 4 and second:
                pool.wait_ge(self.s_ve, i)
                self.nc.gpsimd.tensor_tensor(self.rs[:], self.ve[:], self.power[:], ALU.pow).then_inc(self.s_pow, 1)
        return after

    def begin_vector(self, dve):
        v = self.nc.vector
        dve.sem_inc(self.s_hat, 1)
        v.memset(self.power[:], -0.5).then_inc(self.s_set, 1)
        v.memset(self.zero[:], 0.0).then_inc(self.s_set, 1)

    def vector(self, dve, i, first, second):
        v, c, NH = self.nc.vector, self.c, self.NH
        kv = c.bank[1][:].rearrange("p (i e) -> p i e", i=NH)

        def after(s):
            if s == 5 and second:
                dve.wait_ge(self.s_pow, i)
                v.scalar_tensor_tensor(self.shift[:], self.mv[:, :, 0], -1.0, self.rs[:], ALU.mult, ALU.mult)\
                    .then_inc(self.s_rs, 1)
            if s == 13 and first:
                dve.wait_ge(self.s_kv, i + 2)
                for n in range(NH):
                    v.bn_stats(self.bn[:, n, :], kv[:, n, :]).then_inc(self.s_bn, 1)
                dve.wait_ge(self.s_bn, (i + 1) * NH)
                gate(dve, c)
                for n in range(NH):
                    v.bn_aggr(self.mv[:, n, :], self.bn[:, n, :]).then_inc(self.s_mv, 1)
                dve.wait_ge(self.s_mv, (i + 1) * NH)
                v.tensor_scalar(self.ve[:], self.mv[:, :, 1], EPS, None, ALU.add).then_inc(self.s_ve, 1)
        return after


def gnn1(nc, c, wt, acc):
    with Phase(nc, "gnn1") as ph:
        msg, hot, row_ring, meta_ring = (ph.sb(n, s, d) for n, s, d in (
            ("msg", [P, SLOTS, D], F32), ("hot", [P, SLOTS, P], F32), ("row_ring", [P, 2, HALF], I32),
            ("meta_ring", [P, 2, HALF, 2], F32)))
        edges = c.edges
        edges.use(msg, hot, row_ring, meta_ring, c.row4, c.tab1_d, False)
        keys = Keys1(nc, c, ph, wt)
        s_in, s_zero, s_agg, s_acc = ph.sems("rows_in cleared sums_cleared sums_read")
        n0 = DEPTH * BODIES

        with nc.Block() as block:

            @block.sync
            def _(sp):
                sp.dma_start(c.row4[:], c.row8_d).then_inc(s_in, 16)

            @block.tensor
            def _(pe):
                keys.begin_tensor(pe)
                bodies(pe, lambda i, first, second: edges.tensor(pe, i + n0, keys.tensor(pe, i, first, second)))
                keys.end_tensor(pe)

            @block.scalar
            def _(act):
                act.wait_ge(s_in, 16)
                gate(act, c)

                def body(i, first, second):
                    edges.scalar(act, i, i + n0)
                    keys.scalar(act, i, first, second)

                bodies(act, body)

            @block.gpsimd
            def _(pool):
                nc.gpsimd.memset(msg[:], 0.0).then_inc(s_zero, 1)
                pool.wait_ge(s_zero, 1)
                pool.wait_ge(keys.s_set, 2)
                gate(pool, c)
                bodies(pool, lambda i, first, second: edges.gpsimd(pool, i + n0, keys.gpsimd(pool, i, second)))

            @block.vector
            def _(dve):
                keys.begin_vector(dve)
                nc.vector.memset(c.agg[:], 0.0).then_inc(s_agg, 1)
                dve.wait_ge(s_agg, 1)
                gate(dve, c)
                edges.begin_vector(dve, n0)
                bodies(dve, lambda i, first, second: edges.vector(dve, i, i + n0, keys.vector(dve, i, first, second), is_last(i)))
                dve.wait_ge(keys.s_sum, NT + 2)
                nc.vector.tensor_copy(acc[:, 0:D + KH], c.bank[2][:, 0:D + KH]).then_inc(s_acc, 1)
                nc.vector.tensor_copy(acc[:, D + KH:], c.bank[3][:, 0:D]).then_inc(s_acc, 1)


def mix1_matrix(nc, c, a, acc, wo, mx):
    HD = Keys1.HD
    with Phase(nc, "matrix1") as ph:
        wq, t1, bd = ph.sb("wq", [P, KH, D]), ph.sb("t1", [P, KH, D]), ph.sb("bd", [P, KH, P])
        gk, bk, s1, s2 = (ph.sb(n, [P, P]) for n in ("gk", "bk", "s1", "s2"))
        gv = ph.sb("gv", [P, 2])
        s_in, s_v, s_m = ph.sems("weights_in vector_steps factors_made")
        tail = c.ledger.plan([0, 1], 1)
        with nc.Block() as block:

            @block.sync
            def _(sp):
                for h in range(2):
                    r = slice(h * HD, (h + 1) * HD)
                    sp.dma_start(gk[:, r], spread(a["L1_mix_ln_k_g"], HD)).then_inc(s_in, 16)
                    sp.dma_start(bk[:, r], spread(a["L1_mix_ln_k_b"], HD)).then_inc(s_in, 16)
                    for j, n in enumerate(("g", "b")):
                        sp.dma_start(gv[r, j:j + 1], a["L1_mix_ln_v_" + n].rearrange("(p a) -> p a", a=1)).then_inc(s_in, 16)
                sp.dma_start(wq[:], a["L1_mix_wq"].rearrange("(b p) i -> p b i", p=P)).then_inc(s_in, 16)

            @block.vector
            def _(dve):
                v = nc.vector
                done = [0]

                def then(ins):
                    done[0] += 1
                    ins.then_inc(s_v, 1)
                    dve.wait_ge(s_v, done[0])

                then(v.memset(bd[:], 0.0))
                dve.wait_ge(s_in, 9 * 16)
                for s in range(KH):
                    then(v.tensor_tensor(s1[:], acc[:, s * P:(s + 1) * P], gk[:], ALU.mult))
                    then(v.scalar_tensor_tensor(s1[:], bk[:], acc[:, D + s:D + s + 1], s1[:], ALU.mult, ALU.add))
                    then(v.tensor_tensor(s2[:], acc[:, D + 2 + s * P:D + 2 + (s + 1) * P], gk[:], ALU.mult))
                    then(v.scalar_tensor_tensor(s2[:], bk[:], float(N), s2[:], ALU.mult, ALU.add))
                    then(v.tensor_scalar(s1[:], s1[:], gv[:, 0:1], 1.0 / N, ALU.mult, ALU.mult))
                    then(v.tensor_scalar(s2[:], s2[:], gv[:, 1:2], 1.0 / N, ALU.mult, ALU.mult))
                    then(v.tensor_tensor(s1[:], s1[:], s2[:], ALU.add))
                    for j in range(2):
                        r = slice(j * HD, (j + 1) * HD)
                        then(v.tensor_copy(bd[r, s, r], s1[r, r]))
                dve.sem_inc(s_m, 1)
                for j, to in enumerate((t1, mx)):
                    b, t = tail(j, 0)
                    dve.wait_ge(c.bank_full[b], t)
                    then(v.tensor_copy(to[:].rearrange("p s o -> p (s o)"), c.bank[b][:]))
                    dve.sem_inc(c.bank_free[b], 1)
                    dve.sem_inc(s_m, 1)

            @block.tensor
            def _(pe):
                pe.wait_ge(s_m, 1)
                b, t = tail(0, 0)
                pe.wait_ge(c.bank_free[b], t)
                for s in range(KH):
                    ins = nc.tensor.matmul(c.bank[b][:, s * D:(s + 1) * D], bd[:, s, :], wo[:, s, :], start=True, stop=True)
                ins.then_inc(c.bank_full[b], 1)
                pe.wait_ge(s_m, 2)
                pe.wait_ge(s_in, 9 * 16)
                b, t = tail(1, 0)
                pe.wait_ge(c.bank_free[b], t)
                for h in range(KH):
                    for s in range(KH):
                        ins = nc.tensor.matmul(c.bank[b][:, h * D:(h + 1) * D], wq[:, s, h * P:(h + 1) * P], t1[:, s, :],
                                               start=(s == 0), stop=(s == KH - 1))
                ins.then_inc(c.bank_full[b], 1)


def batch_norm(nc, c, a, scale):
    with Phase(nc, "batch") as ph:
        sq = ph.sb("sq", [P, GT, D])
        acc, mean, gam, eps, power = (ph.sb(n, [P, D]) for n in ("acc", "mean", "gam", "eps", "power"))
        s_in, s_acc, s_v, s_cen, s_msk, s_sq, s_squ, s_p, s_mean = ph.sems(
            "gamma_in accumulated vector_steps centred masked squares squares_used pool_steps mean_made")
        turn = c.ledger.plan([0], NG)
        turn2 = c.ledger.plan([1], NG)
        with nc.Block() as block:

            @block.sync
            def _(sp):
                sp.dma_start(gam[:], spread(a["L1_gnn_gamma"])).then_inc(s_in, 16)

            @block.tensor
            def _(pe):
                pe.sem_inc(s_squ, 1)
                with pe.Fori(0, NG) as g:
                    b, t = turn(0, g)
                    pe.wait_ge(c.bank_free[b], t)
                    gate(pe, c)
                    for k in range(GT):
                        ins = nc.tensor.matmul(c.bank[b][:, 0:D], c.ones[:], tile_of(c.agg, g, k), start=(k == 0), stop=(k == GT - 1))
                    ins.then_inc(c.bank_full[b], 1)
                with pe.Fori(0, NG) as g:
                    b, t = turn2(0, g)
                    pe.wait_ge(c.bank_free[b], t)
                    pe.wait_ge(s_sq, g + 1)
                    for k in range(GT):
                        ins = nc.tensor.matmul(c.bank[b][:, 0:D], c.ones[:], sq[:, k, :], start=(k == 0), stop=(k == GT - 1))
                    ins.then_inc(c.bank_full[b], 1)
                    pe.wait_ge(c.bank_full[b], t)
                    pe.sem_inc(s_squ, 1)

            @block.scalar
            def _(act):
                with act.Fori(0, NG) as g:
                    act.wait_ge(s_msk, g + 1)
                    act.wait_ge(s_squ, g + 1)
                    gate(act, c)
                    nc.scalar.activation(sq[:], group(c.agg, g), ACT.Square).then_inc(s_sq, 1)

            @block.vector
            def _(dve):
                v = nc.vector
                v.memset(acc[:], 0.0).then_inc(s_acc, 1)
                v.memset(eps[:], EPS).then_inc(s_v, 1)
                v.memset(power[:], -0.5).then_inc(s_v, 1)

                def add_up(turn_, g, n):
                    b, t = turn_(0, g)
                    dve.wait_ge(c.bank_full[b], t)
                    dve.wait_ge(s_acc, g + n)
                    v.tensor_tensor(acc[:], acc[:], c.bank[b][:, 0:D], ALU.add).then_inc(s_acc, 1)
                    dve.wait_ge(s_acc, g + (n + 1))
                    dve.sem_inc(c.bank_free[b], 1)

                with dve.Fori(0, NG) as g:
                    add_up(turn, g, 1)
                v.tensor_scalar(mean[:], acc[:], 1.0 / N, None, ALU.mult).then_inc(s_mean, 1)
                dve.wait_ge(s_mean, 1)
                v.memset(acc[:], 0.0).then_inc(s_mean, 1)
                dve.wait_ge(s_mean, 2)
                gate(dve, c)
                with dve.Fori(0, NG) as g:
                    v.tensor_tensor(group(c.agg, g), group(c.agg, g), mean[:].unsqueeze(1).to_broadcast([P, GT, D]),
                                    ALU.subtract).then_inc(s_cen, 1)
                    dve.wait_ge(s_cen, g + 1)
                    last = tile_of(c.agg, g, GT - 1)
                    v.tensor_scalar(last, last, c.real[:, ds(g * GT + (GT - 1), 1)], None, ALU.mult).then_inc(s_msk, 1)
                    add_up(turn2, g, NG + 1)
                dve.wait_ge(s_v, 2)
                v.tensor_scalar(acc[:], acc[:], 1.0 / N, None, ALU.mult).then_inc(s_v, 1)
                dve.wait_ge(s_p, 2)
                dve.wait_ge(s_in, 16)
                v.tensor_tensor(scale[:], acc[:], gam[:], ALU.mult).then_inc(s_v, 1)

            @block.gpsimd
            def _(pool):
                pool.wait_ge(s_v, 3)
                nc.gpsimd.tensor_tensor(acc[:], acc[:], eps[:], ALU.add).then_inc(s_p, 1)
                pool.wait_ge(s_p, 1)
                nc.gpsimd.tensor_tensor(acc[:], acc[:], power[:], ALU.pow).then_inc(s_p, 1)


def mix1_main(nc, c, a, scale, mx, total):
    with Phase(nc, "mix1") as ph:
        stage, nrm = ph.sb("stage", [P, GT, D]), ph.sb("norm", [P, GT, D])
        xt = ph.sb("xt", [P, KH, GR])
        bias, bo = ph.sb("bias", [P, 1, D]), ph.sb("bo", [P, 1, D])
        (s_in, s_bias, s_stage, s_xt, s_xtu, s_sc, s_bb, s_r, s_y, s_bn, s_mv, s_rs, s_tmp, s_nrm, s_msk, s_copy, s_acc,
         s_nu) = ph.sems("vectors_in bias_made staged xt xt_used scaled biased sum_made products_added partial variance rstd "
                         "sum normal masked copied accumulated norm_used")
        turn = c.ledger.plan([j % 8 for j in range(4 + 4)] + [0], NG)
        with nc.Block() as block:

            @block.sync
            def _(sp):
                sp.dma_start(bias[:, 0, :], spread(a["L1_gnn_beta"])).then_inc(s_in, 16)
                sp.dma_start(bo[:, 0, :], spread(a["L1_mix_bo"])).then_inc(s_in, 16)

            @block.tensor
            def _(pe):
                pe.sem_inc(s_xtu, 1)
                pe.sem_inc(s_nu, 1)
                with pe.Fori(0, NG) as g:
                    pe.wait_ge(s_stage, g + 1)
                    transposed(pe, c, lambda k, h: stage[:, k, h * P:(h + 1) * P], turn, 0, g)
                    pe.wait_ge(s_xt, g + 1)
                    for n in range(4):
                        b, t = turn(4 + n, g)
                        pe.wait_ge(c.bank_free[b], t)
                        for k in range(2 * n, min(2 * n + 2, GT)):
                            for h in range(KH):
                                ins = nc.tensor.matmul(c.bank[b][:, (k % 2) * D:(k % 2 + 1) * D], xt[:, h, k * P:(k + 1) * P],
                                                       mx[:, h, :], start=(h == 0), stop=(h == KH - 1))
                        ins.then_inc(c.bank_full[b], 1)
                    pe.wait_ge(c.bank_full[b], t)
                    pe.sem_inc(s_xtu, 1)
                    b, t = turn(8, g)
                    pe.wait_ge(c.bank_free[b], t)
                    pe.wait_ge(s_nrm, (g + 1) * GT)
                    pe.wait_ge(s_msk, g + 1)
                    for k in range(GT):
                        ins = nc.tensor.matmul(c.bank[b][:, 0:D], c.ones[:], nrm[:, k, :], start=(k == 0), stop=(k == GT - 1))
                    ins.then_inc(c.bank_full[b], 1)
                    pe.wait_ge(c.bank_full[b], t)
                    pe.sem_inc(s_nu, 1)

            @block.scalar
            def _(act):
                with act.Fori(0, NG) as g:
                    act.wait_ge(s_xtu, g + 1)
                    gate(act, c)
                    nc.scalar.copy(stage[:], group(c.xn, g)).then_inc(s_stage, 1)
                    evacuate_transposed(act, c, xt, turn, 0, g, s_xt)
                    act.wait_ge(s_msk, g + 1)
                    gate(act, c)
                    nc.scalar.copy(group(c.xn, g), nrm[:]).then_inc(s_copy, 1)

            @block.gpsimd
            def _(pool):
                p = nc.gpsimd
                pool.wait_ge(s_in, 32)
                p.tensor_tensor(bias[:], bias[:], bo[:], ALU.add).then_inc(s_bias, 1)
                pool.wait_ge(s_bias, 1)
                gate(pool, c)
                with pool.Fori(0, NG) as g:
                    x = group(c.agg, g)
                    p.tensor_tensor(x, x, scale[:].unsqueeze(1).to_broadcast([P, GT, D]), ALU.mult).then_inc(s_sc, 1)
                    pool.wait_ge(s_sc, g + 1)
                    gate(pool, c)
                    p.tensor_tensor(x, x, bias[:].to_broadcast([P, GT, D]), ALU.add).then_inc(s_bb, 1)
                    rstd(pool, c, g, s_mv, s_rs, s_tmp)

            @block.vector
            def _(dve):
                v = nc.vector
                v.memset(total[:], 0.0).then_inc(s_acc, 1)
                with dve.Fori(0, NG) as g:
                    dve.wait_ge(s_bb, g + 1)
                    v.tensor_tensor(group(c.res, g), group(c.res, g), group(c.agg, g), ALU.add).then_inc(s_r, 1)
                    dve.wait_ge(s_r, g + 1)
                    for n in range(4):
                        b, t = turn(4 + n, g)
                        w = min(2, GT - 2 * n)
                        dve.wait_ge(c.bank_full[b], t)
                        x = tile_of(c.res, g, 2 * n, 0, w * D)
                        v.tensor_tensor(x, x, c.bank[b][:, 0:w * D], ALU.add).then_inc(s_y, 1)
                        dve.wait_ge(s_y, g * 4 + (n + 1))
                        dve.sem_inc(c.bank_free[b], 1)
                    stats(dve, c, lambda k: tile_of(c.res, g, k), g, s_bn, s_mv)
                    dve.wait_ge(s_nu, g + 1)
                    normalise(dve, c, lambda k: nrm[:, k, :], lambda k: tile_of(c.res, g, k), g, s_rs, s_nrm)
                    dve.wait_ge(s_nrm, (g + 1) * GT)
                    v.tensor_scalar(nrm[:, GT - 1, :], nrm[:, GT - 1, :], c.real[:, ds(g * GT + (GT - 1), 1)], None,
                                    ALU.mult).then_inc(s_msk, 1)
                    b, t = turn(8, g)
                    dve.wait_ge(c.bank_full[b], t)
                    dve.wait_ge(s_acc, g + 1)
                    v.tensor_tensor(total[:], total[:], c.bank[b][:, 0:D], ALU.add).then_inc(s_acc, 1)
                    dve.wait_ge(s_acc, g + 2)
                    dve.sem_inc(c.bank_free[b], 1)
                    dve.wait_ge(s_copy, g + 1)


def router(nc, c, a, total, chosen, share):
    NE = 8
    CAP = float(-(-N * 5 // (4 * NE)))
    with Phase(nc, "router") as ph:
        wr = ph.sb("wr", [1, NE, D])
        em, junk = ph.sb("em", [1, D]), ph.sb("junk", [1, D])
        lg, br, ex = (ph.sb(n, [1, NE]) for n in ("lg", "br", "ex"))
        m1, sm = ph.sb("m1", [1, 1]), ph.sb("sm", [1, 1])
        gt, tri, rank = ph.sb("gt", [1, NE, NE]), ph.sb("tri", [1, NE, NE]), ph.sb("rank", [1, NE])
        two, pick, val = ph.sb("two", [1, 2, NE]), ph.sb("pick", [1, 2]), ph.sb("val", [1, 2])
        s_in, s_v, s_e, s_w, s_bc = ph.sems("weights_in vector_steps differences_made shares_made exponentials")
        turn = c.ledger.plan([0, 1], 1)
        with nc.Block() as block:

            @block.sync
            def _(sp):
                sp.dma_start(wr[:],
                             a["L1_ffn_Wr"].rearrange("(a d) e -> a e d", a=1), allow_slow_non_contiguous=True).then_inc(s_in, 16)
                sp.dma_start(br[:], a["L1_ffn_br"].rearrange("(a e) -> a e", a=1)).then_inc(s_in, 16)

            @block.tensor
            def _(pe):
                pe.wait_ge(s_w, 1)
                nc.tensor.matmul(c.bank[0][:, 0:2], c.ones[0:1, :], val[:], start=True, stop=True).then_inc(c.bank_full[0], 1)
                pe.sem_inc(c.bank_full[1], 1)

            @block.scalar
            def _(act):
                act.wait_ge(s_e, 1)
                nc.scalar.activation(ex[:], lg[:], ACT.Exp).then_inc(s_bc, 1)
                act.wait_ge(s_e, 2)
                nc.scalar.activation(ex[:], lg[:], ACT.Exp).then_inc(s_bc, 1)
                act.wait_ge(s_e, 3)
                nc.scalar.activation(val[:], val[:], ACT.Exp).then_inc(s_bc, 1)

            @block.vector
            def _(dve):
                v = nc.vector
                done = [0]

                def then(ins):
                    done[0] += 1
                    ins.then_inc(s_v, 1)
                    dve.wait_ge(s_v, done[0])

                dve.wait_ge(s_in, 32)
                then(v.tensor_scalar(em[:], total[0:1, :], 1.0 / N, None, ALU.mult))
                for e in range(NE):
                    then(v.tensor_tensor_reduce(junk[:], em[:], wr[:, e, :], 1.0, 0.0, ALU.mult, ALU.add, lg[:, e:e + 1]))
                then(v.tensor_tensor(lg[:], lg[:], br[:], ALU.add))

                def softmax(n, x, y):
                    then(v.tensor_reduce(m1[:], x[:], AX.X, ALU.max))
                    then(v.tensor_scalar(x[:], x[:], m1[:, 0:1], None, ALU.subtract))
                    dve.sem_inc(s_e, 1)
                    dve.wait_ge(s_bc, n)
                    then(v.tensor_reduce(sm[:], y[:], AX.X, ALU.add))
                    then(v.reciprocal(sm[:], sm[:]))
                    then(v.tensor_scalar(x[:], y[:], sm[:, 0:1], None, ALU.mult))

                softmax(1, lg, ex)
                then(v.tensor_scalar(lg[:], lg[:], CAP / N, None, ALU.min))
                softmax(2, lg, ex)
                me = lg[:].unsqueeze(2).to_broadcast([1, NE, NE])
                other = lg[:].unsqueeze(1).to_broadcast([1, NE, NE])
                no = c.iota[0:1, 0:NE]
                then(v.tensor_tensor(gt[:], other, me, ALU.is_equal))
                then(v.tensor_tensor(tri[:], no.unsqueeze(1).to_broadcast([1, NE, NE]), no.unsqueeze(2).to_broadcast([1, NE, NE]),
                                     ALU.is_lt))
                then(v.tensor_tensor(tri[:], tri[:], gt[:], ALU.mult))
                then(v.tensor_tensor(gt[:], other, me, ALU.is_gt))
                then(v.tensor_tensor(gt[:], gt[:], tri[:], ALU.add))
                then(v.tensor_reduce(rank[:], gt[:], AX.X, ALU.add))
                then(v.tensor_tensor(two[:], rank[:].unsqueeze(1).to_broadcast([1, 2, NE]),
                                     c.iota[0:1, 0:2].unsqueeze(2).to_broadcast([1, 2, NE]), ALU.is_equal))
                then(v.tensor_tensor(gt[:, 0:2, :], two[:], no.unsqueeze(1).to_broadcast([1, 2, NE]), ALU.mult))
                then(v.tensor_reduce(pick[:], gt[:, 0:2, :], AX.X, ALU.add))
                then(v.tensor_copy(chosen[:], pick[:]))
                then(v.tensor_tensor(gt[:, 0:2, :], two[:], lg[:].unsqueeze(1).to_broadcast([1, 2, NE]), ALU.mult))
                then(v.tensor_reduce(val[:], gt[:, 0:2, :], AX.X, ALU.add))
                softmax(3, val, val)
                dve.sem_inc(s_w, 1)
                dve.wait_ge(c.bank_full[0], turn(0, 0)[1])
                then(v.tensor_copy(share[:], c.bank[0][:, 0:2]))
                dve.sem_inc(c.bank_free[0], 1)
                dve.sem_inc(c.bank_free[1], 1)


def experts(nc, c, a, chosen, share, out):
    with Phase(nc, "experts") as ph:
        cut = carver(c.agg)
        stage = cut(GT, D)
        w1, w2, b1 = ph.sb("w1", [P, KH, 4 * D]), ph.sb("w2", [P, 8, D]), ph.sb("b1", [P, 8])
        u = ph.sb("rows", [P, GT, D])
        done_rows = ph.sb("done", [P, GT, D])
        vec, b2 = ph.sb("vec", [P, 2, D]), ph.sb("b2", [P, 2, D])
        turn = c.ledger.plan(Mlp.BANKS, NG)
        mlp = Mlp(nc, c, ph, turn, stage, cut, w1, w2, b1, ACT.Gelu)
        (s_in, s_w, s_stage, s_u, s_y, s_bn, s_mv, s_rs, s_tmp, s_nrm, s_gam, s_bet, s_out, s_store) = ph.sems(
            "weights_in weighted staged rows_biased rows_summed partial variance rstd sum normal gamma beta rows_done stored")
        with nc.Block() as block:

            @block.sync
            def _(sp):
                for i in range(2):
                    e = sp.value_load(chosen[0:1, i:i + 1], min_val=0, max_val=7)
                    one = ds(e, 1)
                    for h in range(KH):
                        sp.dma_start(w1[:, h, i * 2 * D:(i + 1) * 2 * D],
                                     a["L1_ffn_W1"][one, h * P:(h + 1) * P, :].rearrange("e p f -> p (e f)")).then_inc(s_in, 16)
                    for m in range(4):
                        sp.dma_start(w2[:, 4 * i + m, :],
                                     a["L1_ffn_W2"][one, m * P:(m + 1) * P, :].rearrange("e p o -> p (e o)")).then_inc(s_in, 16)
                        sp.dma_start(b1[:, 4 * i + m:4 * i + m + 1],
                                     a["L1_ffn_b1"][one, m * P:(m + 1) * P].rearrange("e p -> p e"),
                                     allow_slow_non_contiguous=True).then_inc(s_in, 16)
                    sp.dma_start(b2[:, i, :], a["L1_ffn_b2"][one, :].to_broadcast([P, D])).then_inc(s_in, 16)
                for j, n in enumerate(("gamma", "beta")):
                    sp.dma_start(vec[:, j, :], spread(a["L1_ffn_" + n])).then_inc(s_in, 16)
                sp.sem_inc(s_store, 16)
                with sp.Fori(0, NG - 1) as g:
                    sp.wait_ge(s_out, g + 1)
                    sp.dma_start(out[ds(g * GR, GR), :].rearrange("(k p) d -> p k d", p=P), done_rows[:]).then_inc(s_store, 16)
                sp.wait_ge(s_out, NG)
                at = (NG - 1) * GR
                sp.dma_start(out[at:at + (GT - 1) * P, :].rearrange("(k p) d -> p k d", p=P), done_rows[:, 0:GT - 1, :])\
                    .then_inc(s_store, 16)
                sp.dma_start(out[N - LAST:N, :], done_rows[0:LAST, GT - 1, :]).then_inc(s_store, 16)
                sp.wait_ge(s_store, 16 * (NG + 2))

            @block.tensor
            def _(pe):
                pe.sem_inc(mlp.s_used, 1)
                pe.wait_ge(s_w, 4)
                with pe.Fori(0, NG) as g:
                    pe.wait_ge(s_stage, g + 1)
                    mlp.tensor(pe, g)

            @block.scalar
            def _(act):
                act.wait_ge(s_in, 24 * 16)
                with act.Fori(0, NG) as g:
                    act.wait_ge(mlp.s_used, g + 1)
                    act.wait_ge(s_u, g + 1)
                    gate(act, c)
                    nc.scalar.copy(stage, group(c.xn, g)).then_inc(s_stage, 1)
                    mlp.scalar(act, g)

            @block.gpsimd
            def _(pool):
                p = nc.gpsimd
                pool.wait_ge(s_w, 4)
                pool.sem_inc(s_u, 1)
                with pool.Fori(0, NG) as g:
                    pool.wait_ge(s_stage, g + 1)
                    pool.wait_ge(s_y, g * 5 + 1)
                    p.tensor_tensor(u[:], stage, b2[:, 0:1, :].to_broadcast([P, GT, D]), ALU.add).then_inc(s_u, 1)
                    rstd(pool, c, g, s_mv, s_rs, s_tmp)
                    pool.wait_ge(s_nrm, (g + 1) * GT)
                    p.tensor_tensor(u[:], u[:], vec[:, 0:1, :].to_broadcast([P, GT, D]), ALU.mult).then_inc(s_gam, 1)

            @block.vector
            def _(dve):
                v = nc.vector
                dve.wait_ge(s_in, 24 * 16)
                for i in range(2):
                    x = w2[:, 4 * i:4 * i + 4, :]
                    v.tensor_scalar(x, x, share[:, i:i + 1], None, ALU.mult).then_inc(s_w, 1)
                v.tensor_scalar(b2[:, 0, :], b2[:, 0, :], share[:, 0:1], None, ALU.mult).then_inc(s_w, 1)
                dve.wait_ge(s_w, 3)
                v.scalar_tensor_tensor(b2[:, 0, :], b2[:, 1, :], share[:, 1:2], b2[:, 0, :], ALU.mult, ALU.add).then_inc(s_w, 1)
                dve.sem_inc(s_y, 1)
                tile = lambda k: u[:, k, :]
                with dve.Fori(0, NG) as g:
                    dve.wait_ge(s_u, g + 2)
                    for n, (j, k, w) in enumerate(mlp.pairs()):
                        b, t = turn(j, g)
                        dve.wait_ge(c.bank_full[b], t)
                        x = u[:, k:k + w, :].rearrange("p k d -> p (k d)")
                        v.tensor_tensor(x, x, c.bank[b][:, 0:w * D], ALU.add).then_inc(s_y, 1)
                        dve.wait_ge(s_y, g * 5 + (n + 2))
                        dve.sem_inc(c.bank_free[b], 1)
                    stats(dve, c, tile, g, s_bn, s_mv)
                    normalise(dve, c, tile, tile, g, s_rs, s_nrm)
                    dve.wait_ge(s_gam, g + 1)
                    v.tensor_tensor(u[:], u[:], vec[:, 1:2, :].to_broadcast([P, GT, D]), ALU.add).then_inc(s_bet, 1)
                    dve.wait_ge(s_bet, g + 1)
                    dve.wait_ge(s_store, (g + 1) * 16)
                    gate(dve, c)
                    v.tensor_tensor(done_rows[:], u[:], group(c.res, g), ALU.add).then_inc(s_out, 1)
                    dve.wait_ge(s_out, g + 1)
                    dve.sem_inc(s_y, 1)


def program(nc, a, out):
    c = Core()
    c.nc = nc
    ctx = ExitStack()
    with ctx:
        sb = lambda n, s, d: ctx.enter_context(nc.sbuf_tensor(n, s, d))
        c.sem = lambda n: ctx.enter_context(nc.semaphore(n))
        c.ledger = Ledger()
        c.bank = [ctx.enter_context(nc.psum_tensor(f"bank{b}", [P, 512], F32)) for b in range(8)]
        c.bank_full = [c.sem(f"bank_full{b}") for b in range(8)]
        c.bank_free = [c.sem(f"bank_free{b}") for b in range(8)]
        c.gates = {str(e.engine): c.sem(f"waits_passed_{n}") for n, e in
                   (("pe", nc.tensor), ("act", nc.scalar), ("dve", nc.vector), ("pool", nc.gpsimd), ("sp", nc.sync))}
        c.regs = {str(e.engine): [e.alloc_register(f"tile{u}") for u in range(SLOTS)] for e in (nc.vector, nc.tensor)}
        c.res = sb("residual", [P, NT * D], F32)
        c.xn = sb("state", [P, NT * D], F32)
        c.agg = sb("sums", [P, NT * D], F32)
        c.ident = sb("ident", [P, P], F32)
        c.ones = sb("ones", [P, P], F32)
        c.iota = sb("iota", [P, P], F32)
        c.eps7 = sb("eps7", [P, GT], F32)
        c.pow7 = sb("pow7", [P, GT], F32)
        c.bn = sb("bn", [P, GT, 6], F32)
        c.mv = sb("mv", [P, GT, 2], F32)
        c.ve = sb("ve", [P, GT], F32)
        c.rs = sb("rs", [P, GT], F32)
        c.row_no = sb("row_no", [P, 1], F32)
        c.real = sb("real", [P, NT], F32)
        c.meta = sb("meta", [P, SB * P, 2], F32)
        c.local = c.meta[:, :, 0]
        c.tile_row = sb("tile_row", [1, SB * P], I32)
        c.row4 = sb("row4", [P, SB * P], I32)
        c.rec_d = nc.dram_tensor("edge_records", (RECN, 4), I32, kind="Internal").ap()
        c.tl_d = nc.dram_tensor("step_tiles", (SB * P,), I32, kind="Internal").ap()
        c.row8_d = nc.dram_tensor("table_rows_1", (P, SB * P), I32, kind="Internal").ap()
        c.wt_d = nc.dram_tensor("mixer_weights", (P, KH, 5 * D), F32, kind="Internal").ap()
        c.xn_d = nc.dram_tensor("first_norm", (NP, D), F32, kind="Internal").ap()
        c.kv_d = nc.dram_tensor("mixer_sums", (P, KH, P + 4), F32, kind="Internal").ap()
        c.rows_d = nc.dram_tensor("mixer_rows", (NP, D), F32, kind="Internal").ap()
        c.tab0_d = nc.dram_tensor("tables0", (REL0 * NP, D), F32, kind="Internal").ap()
        c.tab1_d = nc.dram_tensor("tables1", (REL1 * NP, D), F32, kind="Internal").ap()

        constants(nc, c, a["x"])
        with nc.sbuf_tensor("rel4", [P, SB * P], F32) as c.rel4:
            edge_tables(nc, c, a["src"], a["dst"], a["edge_type_4"], a["edge_type_8"])
            edge_weights(nc, c)
        with nc.sbuf_tensor("wt", [P, KH, 5 * D], F32) as wt:
            weights0(nc, c, a, wt)
            norm0(nc, c, wt)
        gnn0(nc, c, a)
        with ExitStack() as l1:
            small = lambda n, s, d=F32: l1.enter_context(nc.sbuf_tensor(n, s, d))
            score, take = small("score", [P, NT]), small("take", [P, NT])
            mx, scale, total = small("mx", [P, KH, D]), small("scale", [P, D]), small("total", [P, D])
            chosen, share = small("chosen", [1, 2], I32), small("share", [P, 2])
            ffn0(nc, c, a, score)
            select(nc, c, score, take)
            with nc.sbuf_tensor("acc1", [P, 4 * P + KH], F32) as acc:
                with nc.sbuf_tensor("wt1", [P, KH, 2 * D], F32) as wt:
                    weights1(nc, c, a, ("wk", "wv"), c.agg[:, 0:4 * D].rearrange("p (b i) -> p b i", i=D), wt)
                    tables1(nc, c, a, take)
                    gnn1(nc, c, wt, acc)
                with nc.sbuf_tensor("nat1", [P, 2, D], F32) as nat, nc.sbuf_tensor("wo1", [P, KH, D], F32) as wo:
                    weights1(nc, c, a, ("wo",), nat, wo)
                    mix1_matrix(nc, c, a, acc, wo, mx)
            batch_norm(nc, c, a, scale)
            mix1_main(nc, c, a, scale, mx, total)
            router(nc, c, a, total, chosen, share)
            experts(nc, c, a, chosen, share, out)


def constants(nc, c, x):
    s_x, s_pad, s_c, s_v, s_free = (c.sem(n) for n in ("x_in", "pad_cleared", "constants_made", "ident_cleared", "real_step"))
    with nc.Block() as block:

        @block.sync
        def _(sp):
            full = c.res[:, 0:(NT - 1) * D].rearrange("p (t c) -> p t c", c=D)
            sp.dma_start(full, x[0:(NT - 1) * P, :].rearrange("(t p) c -> p t c", p=P)).then_inc(s_x, 16)
            sp.wait_ge(s_pad, 1)
            sp.dma_start(c.res[0:LAST, (NT - 1) * D:NT * D], x[(NT - 1) * P:N, :]).then_inc(s_x, 16)
            sp.wait_ge(s_x, 32)

        @block.gpsimd
        def _(pool):
            g = nc.gpsimd
            g.memset(c.res[:, (NT - 1) * D:NT * D], 0.0).then_inc(s_pad, 1)
            g.memset(c.ident[:], 0.0).then_inc(s_v, 1)
            g.memset(c.ones[:], 1.0).then_inc(s_c, 1)
            g.iota(c.iota[:], [[1, P]], base=0, channel_multiplier=0,
                   allow_small_or_imprecise_dtypes=True).then_inc(s_c, 1)
            g.iota(c.real[:], [[P, NT]], base=0, channel_multiplier=1,
                   allow_small_or_imprecise_dtypes=True).then_inc(s_free, 1)
            g.iota(c.row_no[:], [[0, 1]], base=0, channel_multiplier=1,
                   allow_small_or_imprecise_dtypes=True).then_inc(s_c, 1)
            pool.wait_ge(s_v, 1)
            g.affine_select(out=c.ident[:], in_=c.ident[:], compare_op=ALU.not_equal, fill=1.0, base=0,
                            pattern=[[-1, P]], channel_multiplier=1).then_inc(s_c, 1)

        @block.vector
        def _(dve):
            v = nc.vector
            v.memset(c.eps7[:], EPS).then_inc(s_c, 1)
            v.memset(c.pow7[:], -0.5).then_inc(s_c, 1)
            dve.wait_ge(s_free, 1)
            v.tensor_scalar(c.real[:], c.real[:], float(N), None, ALU.is_lt).then_inc(s_c, 1)
            for b in range(8):
                dve.sem_inc(c.bank_free[b], 1)


def kernel(**inputs):
    import numpy as _np
    import concourse.bacc as _bacc
    from concourse import mybir as _mybir
    from concourse.bass_utils import run_bass_kernel_spmd as _run

    nc = _bacc.Bacc("TRN2", target_bir_lowering=False, num_devices=1)
    arrays, args = {}, {}
    for name, value in inputs.items():
        a = _np.ascontiguousarray(value)
        arrays[f"in_{name}_dram"] = a
        args[name] = nc.dram_tensor(f"in_{name}_dram", a.shape, _mybir.dt.from_np(a.dtype), kind="ExternalInput").ap()
    out = nc.dram_tensor("out_0_dram", (N, D), F32, kind="ExternalOutput").ap()
    program(nc, args, out)
    r = _run(nc, [arrays], core_ids=[0])
    return r.results[0]["out_0_dram"]
```
